# Optimizing a Trainium2 kernel written in Bass

```python
import numpy as np
import jax
import jax.numpy as jnp

def _softmax(x, axis=-1):
    return jax.nn.softmax(x, axis=axis)

def _gelu(x):
    return jax.nn.gelu(x, approximate=True)

def _silu(x):
    return jax.nn.silu(x)

def _sigmoid(x):
    return jax.nn.sigmoid(x)

def _layernorm(x, axis=-1, eps=1e-05):
    m = jnp.mean(x, axis=axis, keepdims=True)
    v = jnp.var(x, axis=axis, keepdims=True)
    return (x - m) / jnp.sqrt(v + eps)

def _scatter_add(tgt, idx, src, axis=0):
    return tgt.at[idx].add(src)

def _segment_sum(src, seg, n):
    return jax.ops.segment_sum(src, seg, n)
kernel_name = 'mk_decoder_preln_d2_seqx_r4_d430b7'

def setup_inputs(seed: int=0):
    np.random.seed(seed)
    _w = jnp.asarray

    def _rec_inputs():
        import jax
        import jax.numpy as jnp
        _rk = jax.random.key(seed)
        x = -0.000125 + 0.9999 * jax.random.normal(jax.random.fold_in(_rk, 1), (32, 256, 256), jnp.float32)
        _lenS = 256 - jax.random.randint(jax.random.fold_in(_rk, 7), (32,), 0, max(1, 256 // 4) + 1, jnp.int32)
        _lenS2 = 256 - jax.random.randint(jax.random.fold_in(_rk, 8), (32,), 0, max(1, 256 // 4) + 1, jnp.int32)
        _ctx_1024P = jax.random.normal(jax.random.fold_in(_rk, 11), (32, 16, 256), jnp.float32)
        _ctx_1024c = jax.random.dirichlet(jax.random.fold_in(_rk, 511), 0.3 * jnp.ones((16,), jnp.float32), (32, 256))
        _ctx_1024t = jnp.einsum('bsk,bkd->bsd', _ctx_1024c, _ctx_1024P)
        _ctx_1024t = _ctx_1024t * jax.lax.rsqrt(jnp.mean(jnp.square(_ctx_1024t)) + 1e-12) * 0.953939
        ctx_1024 = -1.52775e-05 + 0.999936 * (_ctx_1024t + 0.3 * jax.random.normal(jax.random.fold_in(_rk, 611), (32, 256, 256), jnp.float32))
        return (x, ctx_1024)
    x, ctx_1024 = _rec_inputs()

    def _L0_attn_setup():
        import jax, jax.numpy as jnp
        import numpy as np
        EPS = 1e-05

        def _proj_ln(x, W, b, g, beta):
            y = jnp.einsum('blc,cd->bld', x, W) + b
            mu = jnp.mean(y, axis=-1, keepdims=True)
            var = jnp.var(y, axis=-1, keepdims=True)
            return (y - mu) * jax.lax.rsqrt(var + EPS) * g + beta
        key = jax.random.key(seed)
        B, L, C, H = (4, 512, 256, 256)
        ks = jax.random.split(key, 7)
        s_in = 1.0 / np.sqrt(C)
        inp = {'input_sequence': jax.random.normal(ks[0], (B, L, C), jnp.float32), 'Wk': jax.random.normal(ks[1], (C, H), jnp.float32) * s_in, 'bk': jnp.zeros((H,), jnp.float32), 'gk': jnp.ones((H,), jnp.float32), 'betak': jnp.zeros((H,), jnp.float32), 'Wq': jax.random.normal(ks[2], (C, H), jnp.float32) * s_in, 'bq': jnp.zeros((H,), jnp.float32), 'gq': jnp.ones((H,), jnp.float32), 'betaq': jnp.zeros((H,), jnp.float32), 'Wv': jax.random.normal(ks[3], (C, C), jnp.float32) * s_in, 'bv': jnp.zeros((C,), jnp.float32), 'gv': jnp.ones((C,), jnp.float32), 'betav': jnp.zeros((C,), jnp.float32)}
        return inp
    _L0_attn_all = _L0_attn_setup()
    _L0_attn_in = {k: v for k, v in _L0_attn_all.items() if k in ('Wk', 'bk', 'gk', 'betak', 'Wq', 'bq', 'gq', 'betaq', 'Wv', 'bv', 'gv', 'betav')}
    del _L0_attn_all

    def _L0_xattn_setup():
        import jax, jax.numpy as jnp
        import numpy as np
        DECAY = 0.9
        key = jax.random.key(seed)
        k1, k2, k3 = jax.random.split(key, 3)
        B, S, D = (8, 1024, 256)
        q = jax.random.normal(k1, (B, S, D), dtype=jnp.float32)
        k = jax.random.normal(k2, (B, S, D), dtype=jnp.float32)
        v = jax.random.normal(k3, (B, S, D), dtype=jnp.float32)
        return {'q': q, 'k': k, 'v': v}
    _L0_xattn_all = _L0_xattn_setup()
    _L0_xattn_in = {k: v for k, v in _L0_xattn_all.items() if k in ()}
    del _L0_xattn_all

    def _L0_ffn_setup():
        import jax, jax.numpy as jnp
        import numpy as np
        HIDDEN = 256
        FF = 1024
        N_EXPERTS = 8
        CAP_FACTOR = 1.0
        B, S = (4, 512)
        STD = 0.02

        def _gelu(x):
            return x * 0.5 * (1.0 + jax.lax.erf(x / 1.41421))
        key = jax.random.key(seed)
        ks = jax.random.split(key, 6)
        x = jax.random.normal(ks[0], (B, S, HIDDEN), dtype=jnp.float32)
        W_sw = jax.random.normal(ks[1], (HIDDEN, N_EXPERTS), dtype=jnp.float32) * STD
        b_sw = jnp.zeros((N_EXPERTS,), dtype=jnp.float32)
        W1 = jax.random.normal(ks[2], (N_EXPERTS, HIDDEN, FF), dtype=jnp.float32) * STD
        b1 = jnp.zeros((N_EXPERTS, FF), dtype=jnp.float32)
        W2 = jax.random.normal(ks[3], (N_EXPERTS, FF, HIDDEN), dtype=jnp.float32) * STD
        b2 = jnp.zeros((N_EXPERTS, HIDDEN), dtype=jnp.float32)
        return {'x': x, 'W_sw': W_sw, 'b_sw': b_sw, 'W1': W1, 'b1': b1, 'W2': W2, 'b2': b2}
    _L0_ffn_all = _L0_ffn_setup()
    _L0_ffn_in = {k: v for k, v in _L0_ffn_all.items() if k in ('W_sw', 'b_sw', 'W1', 'b1', 'W2', 'b2')}
    del _L0_ffn_all

    def _L1_attn_setup():
        import math
        import jax, jax.numpy as jnp
        import numpy as np
        D_MODEL = 256
        N_HEAD = 16
        HEAD_DIM = D_MODEL // N_HEAD
        T = 1.0
        EPS = 1e-05

        def _layernorm(t, gamma, beta):
            m = t.mean(axis=-1, keepdims=True)
            var = ((t - m) ** 2).mean(axis=-1, keepdims=True)
            return (t - m) * jax.lax.rsqrt(var + EPS) * gamma + beta
        key = jax.random.key(seed)
        k1, k2, k3 = jax.random.split(key, 3)
        B, S = (4, 512)
        scale = 1.0 / math.sqrt(D_MODEL)
        return {'x': jax.random.normal(k1, (B, S, D_MODEL), dtype=jnp.float32), 'w_qkv': jax.random.normal(k2, (D_MODEL, 3 * D_MODEL), dtype=jnp.float32) * scale, 'w_proj': jax.random.normal(k3, (D_MODEL, D_MODEL), dtype=jnp.float32) * scale, 'q_gamma': jnp.ones((HEAD_DIM,), dtype=jnp.float32), 'q_beta': jnp.zeros((HEAD_DIM,), dtype=jnp.float32), 'k_gamma': jnp.ones((HEAD_DIM,), dtype=jnp.float32), 'k_beta': jnp.zeros((HEAD_DIM,), dtype=jnp.float32)}
    _L1_attn_all = _L1_attn_setup()
    _L1_attn_in = {k: v for k, v in _L1_attn_all.items() if k in ('w_qkv', 'w_proj', 'q_gamma', 'q_beta', 'k_gamma', 'k_beta')}
    del _L1_attn_all

    def _L1_xattn_setup():
        import jax, jax.numpy as jnp
        import numpy as np
        B, S, E, H = (4, 512, 128, 256)
        key = jax.random.key(seed)
        ks = jax.random.split(key, 8)
        s = 1.0 / np.sqrt(H)
        return {'hidden_states': jax.random.normal(ks[0], (B, S, H), jnp.float32), 'external_embeddings': jax.random.normal(ks[1], (B, E, H), jnp.float32), 'Wq': jax.random.normal(ks[2], (H, H), jnp.float32) * s, 'bq': jax.random.normal(ks[3], (H,), jnp.float32) * 0.02, 'Wk': jax.random.normal(ks[4], (H, H), jnp.float32) * s, 'bk': jax.random.normal(ks[5], (H,), jnp.float32) * 0.02, 'Wv': jax.random.normal(ks[6], (H, H), jnp.float32) * s, 'bv': jax.random.normal(ks[7], (H,), jnp.float32) * 0.02}
    _L1_xattn_all = _L1_xattn_setup()
    _L1_xattn_in = {k: v for k, v in _L1_xattn_all.items() if k in ('Wq', 'bq', 'Wk', 'bk', 'Wv', 'bv')}
    del _L1_xattn_all

    def _L1_ffn_setup():
        import jax, jax.numpy as jnp
        import numpy as np
        D_MODEL = 256
        EXPERT_DIM = 256
        NUM_EXPERTS = 8
        TOP_K = 2
        B, T = (8, 1024)
        key = jax.random.key(seed)
        ks = jax.random.split(key, 5)
        scale_in = 1.0 / np.sqrt(D_MODEL)
        scale_h = 1.0 / np.sqrt(EXPERT_DIM)
        return {'x': jax.random.normal(ks[0], (B, T, D_MODEL), dtype=jnp.float32), 'gate_w': jax.random.normal(ks[1], (D_MODEL, NUM_EXPERTS), dtype=jnp.float32) * scale_in, 'gate_b': jnp.zeros((NUM_EXPERTS,), dtype=jnp.float32), 'w1': jax.random.normal(ks[2], (NUM_EXPERTS, D_MODEL, EXPERT_DIM), dtype=jnp.float32) * scale_in, 'b1': jnp.zeros((NUM_EXPERTS, EXPERT_DIM), dtype=jnp.float32), 'w2': jax.random.normal(ks[3], (NUM_EXPERTS, EXPERT_DIM, D_MODEL), dtype=jnp.float32) * scale_h, 'b2': jnp.zeros((NUM_EXPERTS, D_MODEL), dtype=jnp.float32)}
    _L1_ffn_all = _L1_ffn_setup()
    _L1_ffn_in = {k: v for k, v in _L1_ffn_all.items() if k in ('gate_w', 'gate_b', 'w1', 'b1', 'w2', 'b2')}
    del _L1_ffn_all
    return {'x': x, 'ctx_1024': ctx_1024, 'L0_attn_Wk': _L0_attn_in['Wk'], 'L0_attn_bk': _L0_attn_in['bk'], 'L0_attn_gk': _L0_attn_in['gk'], 'L0_attn_betak': _L0_attn_in['betak'], 'L0_attn_Wq': _L0_attn_in['Wq'], 'L0_attn_bq': _L0_attn_in['bq'], 'L0_attn_gq': _L0_attn_in['gq'], 'L0_attn_betaq': _L0_attn_in['betaq'], 'L0_attn_Wv': _L0_attn_in['Wv'], 'L0_attn_bv': _L0_attn_in['bv'], 'L0_attn_gv': _L0_attn_in['gv'], 'L0_attn_betav': _L0_attn_in['betav'], 'L0_ffn_W_sw': _L0_ffn_in['W_sw'], 'L0_ffn_b_sw': _L0_ffn_in['b_sw'], 'L0_ffn_W1': _L0_ffn_in['W1'], 'L0_ffn_b1': _L0_ffn_in['b1'], 'L0_ffn_W2': _L0_ffn_in['W2'], 'L0_ffn_b2': _L0_ffn_in['b2'], 'L1_attn_w_qkv': _L1_attn_in['w_qkv'], 'L1_attn_w_proj': _L1_attn_in['w_proj'], 'L1_attn_q_gamma': _L1_attn_in['q_gamma'], 'L1_attn_q_beta': _L1_attn_in['q_beta'], 'L1_attn_k_gamma': _L1_attn_in['k_gamma'], 'L1_attn_k_beta': _L1_attn_in['k_beta'], 'L1_xattn_Wq': _L1_xattn_in['Wq'], 'L1_xattn_bq': _L1_xattn_in['bq'], 'L1_xattn_Wk': _L1_xattn_in['Wk'], 'L1_xattn_bk': _L1_xattn_in['bk'], 'L1_xattn_Wv': _L1_xattn_in['Wv'], 'L1_xattn_bv': _L1_xattn_in['bv'], 'L1_ffn_gate_w': _L1_ffn_in['gate_w'], 'L1_ffn_gate_b': _L1_ffn_in['gate_b'], 'L1_ffn_w1': _L1_ffn_in['w1'], 'L1_ffn_b1': _L1_ffn_in['b1'], 'L1_ffn_w2': _L1_ffn_in['w2'], 'L1_ffn_b2': _L1_ffn_in['b2']}

def reference(x, ctx_1024, L0_attn_Wk, L0_attn_bk, L0_attn_gk, L0_attn_betak, L0_attn_Wq, L0_attn_bq, L0_attn_gq, L0_attn_betaq, L0_attn_Wv, L0_attn_bv, L0_attn_gv, L0_attn_betav, L0_ffn_W_sw, L0_ffn_b_sw, L0_ffn_W1, L0_ffn_b1, L0_ffn_W2, L0_ffn_b2, L1_attn_w_qkv, L1_attn_w_proj, L1_attn_q_gamma, L1_attn_q_beta, L1_attn_k_gamma, L1_attn_k_beta, L1_xattn_Wq, L1_xattn_bq, L1_xattn_Wk, L1_xattn_bk, L1_xattn_Wv, L1_xattn_bv, L1_ffn_gate_w, L1_ffn_gate_b, L1_ffn_w1, L1_ffn_b1, L1_ffn_w2, L1_ffn_b2):
    import jax
    import jax.numpy as jnp

    def _L0_attn_ref(input_sequence, Wk, bk, gk, betak, Wq, bq, gq, betaq, Wv, bv, gv, betav):
        import jax, jax.numpy as jnp
        import numpy as np
        EPS = 1e-05

        def _proj_ln(x, W, b, g, beta):
            y = jnp.einsum('blc,cd->bld', x, W) + b
            mu = jnp.mean(y, axis=-1, keepdims=True)
            var = jnp.var(y, axis=-1, keepdims=True)
            return (y - mu) * jax.lax.rsqrt(var + EPS) * g + beta
        values = _proj_ln(input_sequence, Wv, bv, gv, betav)
        k = _proj_ln(input_sequence, Wk, bk, gk, betak)
        q = _proj_ln(input_sequence, Wq, bq, gq, betaq)
        scores = jnp.einsum('blc,bLc->blL', k, q)
        attn = jax.nn.softmax(scores, axis=-1)
        out = jnp.einsum('blL,bLc->blc', attn, values)
        return out + input_sequence

    def _L0_xattn_ref(q, k, v):
        import jax, jax.numpy as jnp
        import numpy as np
        DECAY = 0.9
        kv = jnp.swapaxes(k * v, 0, 1)

        def step(r, kv_t):
            r = DECAY * r + kv_t
            return (r, r)
        r0 = jnp.zeros(q.shape[:1] + q.shape[2:], dtype=q.dtype)
        _, rs = jax.lax.scan(step, r0, kv)
        return q * jnp.swapaxes(rs, 0, 1)

    def _L0_ffn_ref(x, W_sw, b_sw, W1, b1, W2, b2):
        import jax, jax.numpy as jnp
        import numpy as np
        HIDDEN = 256
        FF = 1024
        N_EXPERTS = 8
        CAP_FACTOR = 1.0
        B, S = (4, 512)
        STD = 0.02

        def _gelu(x):
            return x * 0.5 * (1.0 + jax.lax.erf(x / 1.41421))
        Bb, Ss, D = x.shape
        T = Bb * Ss
        E = W1.shape[0]
        capacity = int(CAP_FACTOR * T / E)
        xf = x.reshape(T, D)
        logits = xf @ W_sw + b_sw
        probs = jax.nn.softmax(logits, axis=-1)
        pmax = jnp.max(probs, axis=-1)
        routes = jnp.argmax(probs, axis=-1)
        factor = pmax / jax.lax.stop_gradient(pmax)
        xs = xf * factor[:, None]
        onehot = jax.nn.one_hot(routes, E, dtype=jnp.int32)
        pos = jnp.cumsum(onehot, axis=0) - 1
        pos_tok = jnp.take_along_axis(pos, routes[:, None], axis=1)[:, 0]
        keep = pos_tok < capacity
        pos_safe = jnp.where(keep, pos_tok, capacity)
        buf = jnp.zeros((E, capacity + 1, D), dtype=xs.dtype)
        buf = buf.at[routes, pos_safe].set(xs)
        buf = buf[:, :capacity]
        h = _gelu(jnp.einsum('ecd,edf->ecf', buf, W1) + b1[:, None, :])
        expert_out = jnp.einsum('ecf,efd->ecd', h, W2) + b2[:, None, :]
        gathered = expert_out[routes, jnp.minimum(pos_tok, capacity - 1)]
        final = jnp.where(keep[:, None], gathered, xs)
        return final.reshape(Bb, Ss, D)

    def _L1_attn_ref(x, w_qkv, w_proj, q_gamma, q_beta, k_gamma, k_beta):
        import math
        import jax, jax.numpy as jnp
        import numpy as np
        D_MODEL = 256
        N_HEAD = 16
        HEAD_DIM = D_MODEL // N_HEAD
        T = 1.0
        EPS = 1e-05

        def _layernorm(t, gamma, beta):
            m = t.mean(axis=-1, keepdims=True)
            var = ((t - m) ** 2).mean(axis=-1, keepdims=True)
            return (t - m) * jax.lax.rsqrt(var + EPS) * gamma + beta
        B, S, C = x.shape
        H, Dh = (N_HEAD, HEAD_DIM)
        qkv = (x @ w_qkv).reshape(B, S, 3, H, Dh)
        qkv = jnp.transpose(qkv, (2, 0, 3, 1, 4))
        q, k, v = (qkv[0], qkv[1], qkv[2])
        q = _layernorm(q, q_gamma, q_beta)
        k = _layernorm(k, k_gamma, k_beta)
        logits = jnp.einsum('bhsd,bhtd->bhst', q, k) / (math.sqrt(Dh) * T)
        att = jax.nn.softmax(logits, axis=-1)
        out = jnp.einsum('bhst,bhtd->bhsd', att, v)
        out = jnp.transpose(out, (0, 2, 1, 3)).reshape(B, S, C)
        return out @ w_proj

    def _L1_xattn_ref(hidden_states, external_embeddings, Wq, bq, Wk, bk, Wv, bv):
        import jax, jax.numpy as jnp
        import numpy as np
        B, S, E, H = (4, 512, 128, 256)
        q = hidden_states @ Wq + bq
        k_tok = hidden_states @ Wk + bk
        v_tok = hidden_states @ Wv + bv
        k_ext = external_embeddings @ Wk + bk
        v_ext = external_embeddings @ Wv + bv
        s_self = jnp.einsum('bsh,bsh->bs', q, k_tok)[..., None]
        s_ext = jnp.einsum('bsh,beh->bse', q, k_ext)
        scores = jnp.concatenate([s_self, s_ext], axis=-1)
        probs = jax.nn.softmax(scores, axis=-1)
        ctx = probs[..., :1] * v_tok + jnp.einsum('bse,beh->bsh', probs[..., 1:], v_ext)
        return ctx

    def _L1_ffn_ref(x, gate_w, gate_b, w1, b1, w2, b2):
        import jax, jax.numpy as jnp
        import numpy as np
        D_MODEL = 256
        EXPERT_DIM = 256
        NUM_EXPERTS = 8
        TOP_K = 2
        B, T = (8, 1024)
        b, t, d = x.shape
        xf = x.reshape(b * t, d)
        scores = xf @ gate_w + gate_b
        topk_s, topk_i = jax.lax.top_k(scores, TOP_K)
        n = xf.shape[0]
        comb = jnp.zeros_like(scores).at[jnp.arange(n)[:, None], topk_i].add(topk_s)
        h = jnp.maximum(jnp.einsum('nd,edh->neh', xf, w1) + b1, 0.0)
        eo = jnp.einsum('neh,ehd->ned', h, w2) + b2
        out = jnp.einsum('ne,ned->nd', comb, eo)
        return out.reshape(b, t, d)
    x = x + _L0_attn_ref(_layernorm(x, axis=-1), L0_attn_Wk, L0_attn_bk, L0_attn_gk, L0_attn_betak, L0_attn_Wq, L0_attn_bq, L0_attn_gq, L0_attn_betaq, L0_attn_Wv, L0_attn_bv, L0_attn_gv, L0_attn_betav)
    x = x + _L0_xattn_ref(_layernorm(x, axis=-1), ctx_1024, ctx_1024)
    x = x + _L0_ffn_ref(_layernorm(x, axis=-1), L0_ffn_W_sw, L0_ffn_b_sw, L0_ffn_W1, L0_ffn_b1, L0_ffn_W2, L0_ffn_b2)
    x = x + _L1_attn_ref(_layernorm(x, axis=-1), L1_attn_w_qkv, L1_attn_w_proj, L1_attn_q_gamma, L1_attn_q_beta, L1_attn_k_gamma, L1_attn_k_beta)
    x = x + _L1_xattn_ref(_layernorm(x, axis=-1), ctx_1024, L1_xattn_Wq, L1_xattn_bq, L1_xattn_Wk, L1_xattn_bk, L1_xattn_Wv, L1_xattn_bv)
    x = x + _L1_ffn_ref(_layernorm(x, axis=-1), L1_ffn_gate_w, L1_ffn_gate_b, L1_ffn_w1, L1_ffn_b1, L1_ffn_w2, L1_ffn_b2)
    return x

_drawn_inputs = setup_inputs


def setup_inputs(seed=0):
    import zlib

    import numpy as np

    out = dict(_drawn_inputs(seed))
    spreads = {'L0_attn_bk': (0.0, 0.1),
     'L0_attn_gk': (1.0, 0.2),
     'L0_attn_betak': (0.0, 0.1),
     'L0_attn_bq': (0.0, 0.27),
     'L0_attn_gq': (1.0, 0.2),
     'L0_attn_betaq': (0.0, 2.0),
     'L0_attn_bv': (0.0, 0.1),
     'L0_attn_gv': (1.0, 0.2),
     'L0_attn_betav': (0.0, 0.1),
     'L0_ffn_b_sw': (0.0, 0.1),
     'L0_ffn_b1': (0.0, 0.8),
     'L0_ffn_b2': (0.0, 0.8),
     'L1_attn_q_gamma': (1.0, 0.6),
     'L1_attn_q_beta': (0.0, 0.8),
     'L1_attn_k_gamma': (1.0, 0.6),
     'L1_attn_k_beta': (0.0, 2.0),
     'L1_ffn_gate_b': (0.0, 0.427),
     'L1_ffn_b1': (0.0, 0.744),
     'L1_ffn_b2': (0.0, 0.541)}
    factors = {'L0_ffn_W1': 6.493,
     'L0_ffn_W2': 6.048,
     'L1_attn_w_qkv': 4.312,
     'L1_attn_w_proj': 4.277,
     'L1_xattn_bq': 8.0,
     'L1_xattn_bk': 64.0,
     'L1_xattn_bv': 35.978}
    for name, (base, spread) in spreads.items():
        noise = np.random.default_rng([zlib.crc32(name.encode()), seed]).standard_normal(out[name].shape)
        drawn = base * np.exp(spread * noise) if base else spread * noise
        out[name] = jnp.asarray(drawn.astype(out[name].dtype))
    for name, factor in factors.items():
        out[name] = (out[name] * factor).astype(out[name].dtype)
    return out
```

```python
from contextlib import ExitStack

import concourse.bass as bass
from concourse import mybir

F32 = mybir.dt.float32
F32R = mybir.dt.float32r
I32 = mybir.dt.int32
U32 = mybir.dt.uint32
ALU = mybir.AluOpType
ACT = mybir.ActivationFunctionType
AX = mybir.AxisListType

P = 128
EPS = 1e-5


def all_passes(eng, count, one_pass):
    one_pass(0)
    with eng.Fori(1, count) as i:
        one_pass(i)


def stand_alone(eng, passed):
    eng.sem_inc(passed, 1)


class Steps:

    def __init__(self, eng, sem):
        self.eng, self.sem, self.base, self.n = eng, sem, 0, 0

    def begin(self, base):
        self.base, self.n = base, 0

    def did(self, ins):
        self.n += 1
        ins.then_inc(self.sem, 1)
        return self.n

    def need(self, n):
        self.eng.wait_ge(self.sem, self.base + n)


def make_identity(nc, tile, ready, before):
    nc.gpsimd.memset(tile[:, :], 0.0).then_inc(ready, 1)
    nc.gpsimd.wait_ge(ready, before + 1)
    nc.gpsimd.affine_select(out=tile[:, :], in_=tile[:, :], compare_op=ALU.not_equal, fill=1.0, base=0,
                            pattern=[[-1, P]], channel_multiplier=1).then_inc(ready, 1)


def phase_a(nc, a, x2_d, x3_d, table_d):
    x_in, ctx_in = a["x"], a["ctx_1024"]
    B, S, D = x_in.shape
    C, T = D // P, S // P
    NE = a["L0_ffn_W_sw"].shape[1]
    CAP = B * S // NE
    PAIRS = B // 2
    SLOTS = NE * CAP
    with ExitStack() as ctx:
        sb = lambda name, shape, dt=F32: ctx.enter_context(nc.sbuf_tensor("a_" + name, shape, dt))
        sb2 = lambda name, shape, dt=F32: [sb(f"{name}{u}", shape, dt) for u in range(2)]
        sem = lambda name: nc.alloc_semaphore("a_" + name)
        sem2 = lambda name: [sem(f"{name}{u}") for u in range(2)]
        X = [ctx.enter_context(nc.psum_tensor(f"a_X{u}", [P, 512], F32)) for u in range(2)]
        Y = [ctx.enter_context(nc.psum_tensor(f"a_Y{u}", [P, 512], F32)) for u in range(2)]
        PJ = [ctx.enter_context(nc.psum_tensor(f"a_PJ{n}", [P, 512], F32)) for n in range(3)]
        R = [ctx.enter_context(nc.psum_tensor("a_R", [P, 512], F32)), PJ[0]]
        halves = lambda bank: bank[:, :].rearrange("p (c n) -> p c n", c=2)

        ident = sb("ident", [P, P])
        ones = sb("ones", [P, P])
        upto = sb("upto", [P, P])
        decay = sb("decay", [P, T, S])
        expo = sb("expo", [P, T * S])
        nine = sb("nine", [P, T * S])
        mhalf = sb("mhalf", [P, 6])
        iota8 = sb("iota8", [P, NE])
        empty = sb("empty", [P, SLOTS // P], I32)
        w = sb("w", [P, C, 3 * D])
        bias = sb("bias", [P, 3 * D])
        gqT, bqT = sb("gqT", [P, C]), sb("bqT", [P, C])
        gkT, bkT = sb("gkT", [P, C]), sb("bkT", [P, C])
        gv, bv = sb("gv", [P, D]), sb("bv", [P, D])
        wsw = sb("wsw", [P, C, NE])
        bsw = sb("bsw", [P, NE])
        carry = sb("carry", [P, NE])

        x = sb2("x", [P, T, D])
        cx = sb2("cx", [P, T, D])
        kv = sb2("kv", [P, T, D])
        st = sb2("st", [P, 6, 6])
        mv = sb2("mv", [P, 6, 2])
        rs = sb2("rs", [P, 6])
        xn = sb2("xn", [P, T, D])
        xnT = sb2("xnT", [P, C, S])
        qkv = sb2("qkv", [P, T, 3 * D])
        vn = sb2("vn", [P, T, D])
        qT = sb2("qT", [P, C, S])
        kT = sb2("kT", [P, C, S])
        nm = sb2("nm", [P, T])
        pr = sb2("pr", [P, T, S])
        prT = sb2("prT", [P, T, S])
        den = sb2("den", [P, T])
        rden = sb2("rden", [P, T])
        x1 = sb2("x1", [P, T, D])
        x1n = sb2("x1n", [P, T, D])
        x2 = sb2("x2", [P, T, D])
        x2n = sb2("x2n", [P, T, D])
        x2nT = sb2("x2nT", [P, C, S])
        x3 = sb2("x3", [P, T, D])
        lg = sb2("lg", [P, T, NE])
        mx = sb2("mx", [P, T, 8])
        ix = sb2("ix", [P, T, 8], U32)
        ixf = sb2("ixf", [P, T])
        oh = sb2("oh", [P, T, NE])
        rk = sb2("rk", [P, T, NE])
        pos = sb2("pos", [P, T])
        slot = sb2("slot", [P, T])
        over = sb2("over", [P, T])
        sloti = sb2("sloti", [P, T], I32)
        tok = sb2("tok", [P, T], I32)

        weights_in = sem("weights_in")
        consts = sem("consts")
        table_empty = sem("table_empty")
        x_in_s, cx_in_s = sem2("x_loaded"), sem2("ctx_loaded")
        dve_step, pool_step = sem("dve_step"), sem("pool_step")
        dve_passed, pool_passed = sem("dve_passed"), sem("pool_passed")
        var1, rstd1 = sem2("var1"), sem2("rstd1")
        xn_ready, xnT_psum, xnT_ready = sem2("xn_ready"), sem2("xnT_psum"), sem2("xnT_ready")
        qkv_psum, qkv_taken = sem2("qkv_psum"), sem2("qkv_taken")
        var2, rstd2, qkvn_ready, v_ready = sem2("var2"), sem2("rstd2"), sem2("qkvn_ready"), sem2("v_ready")
        qkT_psum, qkT_ready = sem2("qkT_psum"), sem2("qkT_ready")
        scores_psum, max_ready, probs_ready = sem2("scores_psum"), sem2("max_ready"), sem2("probs_ready")
        kv_ready, sums_psum, sums_used = sem2("kv_ready"), sem2("sums_psum"), sem2("sums_used")
        prT_psum, prT_ready, att_psum = sem2("prT_psum"), sem2("prT_ready"), sem2("att_psum")
        x1_ready, var3, rstd3 = sem2("x1_ready"), sem2("var3"), sem2("rstd3")
        x2_ready, var4, rstd4, x2n_ready = sem2("x2_ready"), sem2("var4"), sem2("rstd4"), sem2("x2n_ready")
        x3_ready = sem2("x3_ready")
        x2nT_psum, x2nT_ready, logits_psum = sem2("x2nT_psum"), sem2("x2nT_ready"), sem2("logits_psum")
        onehot_ready, ranks_psum, slot_ready = sem2("onehot_ready"), sem2("ranks_psum"), sem2("slot_ready")
        x2_stored, x3_stored, filed = sem2("x2_stored"), sem2("x3_stored"), sem2("filed")

        rows = lambda t: t.rearrange("(i u t p) d -> i u p t d", u=2, t=T, p=P)
        x_rows = rows(x_in.rearrange("b s d -> (b s) d"))
        cx_rows = rows(ctx_in.rearrange("b s d -> (b s) d"))
        x2_rows, x3_rows = rows(x2_d), rows(x3_d)
        

        block = ctx.enter_context(nc.Block())

        @block.sync
        def _(sync):
            def load(i):
                for u in range(2):
                    sync.wait_ge(x1_ready[u], i)
                    sync.dma_start(x[u][:, :, :], x_rows[i, u]).then_inc(x_in_s[u], 16)
                for u in range(2):
                    sync.wait_ge(kv_ready[u], i)
                    sync.dma_start(cx[u][:, :, :], cx_rows[i, u]).then_inc(cx_in_s[u], 16)

            def store(i):
                for u in range(2):
                    sync.wait_ge(x2_ready[u], i + 1)
                    sync.dma_start(x2_rows[i, u], x2[u][:, :, :]).then_inc(x2_stored[u], 16)
                    sync.wait_ge(x3_ready[u], i + 1)
                    sync.dma_start(x3_rows[i, u], x3[u][:, :, :]).then_inc(x3_stored[u], 16)

            load(0)
            for n, name in enumerate("qkv"):
                cols = slice(n * D, (n + 1) * D)
                sync.dma_start(w[:, :, cols], a[f"L0_attn_W{name}"].rearrange("(c p) n -> p c n", p=P))\
                    .then_inc(weights_in, 16)
                sync.dma_start(bias[:, cols], a[f"L0_attn_b{name}"].partition_broadcast(P)).then_inc(weights_in, 16)
            for tile, name in ((gqT, "gq"), (bqT, "betaq"), (gkT, "gk"), (bkT, "betak")):
                sync.dma_start(tile[:, :], a[f"L0_attn_{name}"].rearrange("(c p) -> p c", p=P),
                               allow_slow_non_contiguous=True).then_inc(weights_in, 16)
            for tile, name in ((gv, "gv"), (bv, "betav")):
                sync.dma_start(tile[:, :], a[f"L0_attn_{name}"].partition_broadcast(P)).then_inc(weights_in, 16)
            sync.dma_start(wsw[:, :, :], a["L0_ffn_W_sw"].rearrange("(c p) n -> p c n", p=P)).then_inc(weights_in, 16)
            sync.dma_start(bsw[:, :], a["L0_ffn_b_sw"].partition_broadcast(P)).then_inc(weights_in, 16)
            sync.wait_ge(consts, 12)
            sync.dma_start(table_d.rearrange("(p n) o -> p (n o)", p=P), empty[:, :]).then_inc(table_empty, 16)
            with sync.Fori(0, PAIRS - 1) as i:
                load(i + 1)
                store(i)
            store(PAIRS - 1)
            for u in range(2):
                sync.wait_ge(x2_stored[u], 16 * PAIRS)
                sync.wait_ge(x3_stored[u], 16 * PAIRS)

        @block.gpsimd
        def _(pool):
            g = nc.gpsimd
            make_identity(nc, ident, consts, 0)
            g.memset(ones[:, :], 1.0).then_inc(consts, 1)
            pool.wait_ge(consts, 3)
            g.affine_select(out=upto[:, :], in_=ones[:, :], compare_op=ALU.is_ge, fill=0.0, base=0,
                            pattern=[[1, P]], channel_multiplier=-1).then_inc(consts, 1)
            g.iota(expo[:, :], [[-P, T], [1, S]], base=0, channel_multiplier=-1,
                   allow_small_or_imprecise_dtypes=True).then_inc(consts, 1)
            g.memset(nine[:, :], 0.9).then_inc(consts, 1)
            pool.wait_ge(consts, 6)
            g.tensor_scalar(expo[:, :], expo[:, :], 0.0, None, ALU.max).then_inc(consts, 1)
            pool.wait_ge(consts, 7)
            g.tensor_tensor(expo[:, :], nine[:, :], expo[:, :], ALU.pow).then_inc(consts, 1)
            pool.wait_ge(consts, 8)
            g.affine_select(out=decay[:, :, :], in_=expo[:, :].rearrange("p (t s) -> p t s", t=T),
                            compare_op=ALU.is_ge, fill=0.0, base=0, pattern=[[-P, T], [1, S]],
                            channel_multiplier=-1).then_inc(consts, 1)
            g.memset(mhalf[:, :], -0.5).then_inc(consts, 1)
            g.iota(iota8[:, :], [[1, NE]], base=0, channel_multiplier=0,
                   allow_small_or_imprecise_dtypes=True).then_inc(consts, 1)
            g.iota(empty[:, :], [[1, SLOTS // P]], base=8 * SLOTS, channel_multiplier=SLOTS // P).then_inc(consts, 1)
            g.memset(carry[:, :], 0.0).then_inc(consts, 1)
            for u in range(2):
                g.iota(tok[u][:, :], [[P, T]], base=(u - 2) * S, channel_multiplier=1).then_inc(consts, 1)
            pool.wait_ge(consts, 15)
            pool.wait_ge(weights_in, 16 * 14)
            pool.wait_ge(table_empty, 16)
            steps = Steps(pool, pool_step)

            def rstd(u, i, n, var, out):
                pool.wait_ge(var[u], i + 1)
                stand_alone(pool, pool_passed)
                e = steps.did(g.tensor_scalar(rs[u][:, 0:n], mv[u][:, 0:n, 1], EPS, None, ALU.add))
                steps.need(e)
                g.tensor_tensor(rs[u][:, 0:n], rs[u][:, 0:n], mhalf[:, 0:n], ALU.pow).then_inc(out[u], 1)

            def one_pass(i):
                steps.begin(i * 14)
                for u in range(2):
                    rstd(u, i, T, var1, rstd1)
                for u in range(2):
                    rstd(u, i, 3 * T, var2, rstd2)
                    pool.wait_ge(qkvn_ready[u], i + 1)
                    pool.wait_ge(att_psum[u], i)
                    m = [steps.did(g.tensor_tensor(vn[u][:, t, :], qkv[u][:, t, 2 * D:3 * D], gv[:, :], ALU.mult))
                         for t in range(T)]
                    for t in range(T):
                        steps.need(m[t])
                        last = g.tensor_tensor(vn[u][:, t, :], vn[u][:, t, :], bv[:, :], ALU.add)
                        if t == T - 1:
                            last.then_inc(v_ready[u], 1)
                for u in range(2):
                    rstd(u, i, T, var3, rstd3)
                    rstd(u, i, T, var4, rstd4)
                for u in range(2):
                    pool.wait_ge(x2n_ready[u], i + 1)
                    pool.wait_ge(x3_stored[u], 16 * i)
                    g.tensor_tensor(x3[u][:, :, :], x2[u][:, :, :], x2n[u][:, :, :], ALU.add).then_inc(x3_ready[u], 1)
                    pool.wait_ge(filed[u], 32 * i)
                    stand_alone(pool, pool_passed)
                    k = steps.did(g.tensor_scalar(tok[u][:, :], tok[u][:, :], float(2 * S), None, ALU.add))
                    steps.need(k)
                    pool.wait_ge(slot_ready[u], i + 1)
                    stand_alone(pool, pool_passed)
                    for t in range(T):
                        g.indirect_dma_start(table_d, bass.IndirectOffsetOnAxis(ap=sloti[u][:, t:t + 1], axis=0),
                                             tok[u][:, t:t + 1], None, bounds_check=SLOTS - 1,
                                             oob_is_err=False).then_inc(filed[u], 16)
                assert steps.n == 14, steps.n

            all_passes(pool, PAIRS, one_pass)
            for u in range(2):
                pool.wait_ge(filed[u], 32 * PAIRS)

        @block.scalar
        def _(act):
            s = nc.scalar
            act.wait_ge(weights_in, 16 * 14)
            def one_pass(i):
                for u in range(2):
                    act.wait_ge(xnT_psum[u], i + 1)
                    s.activation(xnT[u][:, :, :], halves(X[u]), ACT.Copy).then_inc(xnT_ready[u], 1)
                for u in range(2):
                    act.wait_ge(cx_in_s[u], 16 * i + 16)
                    act.wait_ge(sums_psum[u], i)
                    s.activation(kv[u][:, :, :], cx[u][:, :, :], ACT.Square).then_inc(kv_ready[u], 1)
                for u in range(2):
                    act.wait_ge(qkT_psum[u], i + 1)
                    for c in range(C):
                        s.activation(qT[u][:, c, :], halves(X[u])[:, c, :], ACT.Identity,
                                     bias=bqT[:, c:c + 1], scale=gqT[:, c:c + 1])
                        last = s.activation(kT[u][:, c, :], halves(Y[u])[:, c, :], ACT.Identity,
                                            bias=bkT[:, c:c + 1], scale=gkT[:, c:c + 1])
                    last.then_inc(qkT_ready[u], 1)
                for u in range(2):
                    act.wait_ge(max_ready[u], i + 1)
                    for t in range(T):
                        last = s.activation(pr[u][:, t, :], halves(X[u])[:, t, :], ACT.Exp, bias=nm[u][:, t:t + 1],
                                            accum_out=den[u][:, t:t + 1])
                    last.then_inc(probs_ready[u], 1)
                for u in range(2):
                    act.wait_ge(x2nT_psum[u], i + 1)
                    s.activation(x2nT[u][:, :, :], halves(X[u]), ACT.Copy).then_inc(x2nT_ready[u], 1)

            all_passes(act, PAIRS, one_pass)

        @block.vector
        def _(dve):
            v = nc.vector
            dve.wait_ge(weights_in, 16 * 14)
            dve.wait_ge(consts, 15)
            steps = Steps(dve, dve_step)

            def stats(u, src, n, ready):
                done = [steps.did(v.bn_stats(st[u][:, k, :], src(k))) for k in range(n)]
                for k in range(n):
                    steps.need(done[k])
                    stand_alone(dve, dve_passed)
                    last = v.bn_aggr(mv[u][:, k, :], st[u][:, k, :])
                    if k == n - 1:
                        last.then_inc(ready[u], 1)

            def normalize(u, dst, src, k):
                return v.tensor_scalar(dst, src, mv[u][:, k, 0:1], rs[u][:, k:k + 1], ALU.subtract, ALU.mult)

            def one_pass(i):
                steps.begin(i * 62)
                for u in range(2):
                    dve.wait_ge(x_in_s[u], 16 * i + 16)
                    stats(u, lambda k: x[u][:, k, :], T, var1)
                for u in range(2):
                    dve.wait_ge(rstd1[u], i + 1)
                    for t in range(T):
                        last = normalize(u, xn[u][:, t, :], x[u][:, t, :], t)
                    last.then_inc(xn_ready[u], 1)
                for u in range(2):
                    dve.wait_ge(qkv_psum[u], i + 1)
                    add = [steps.did(v.tensor_tensor(qkv[u][:, t, 0:2 * D], PJ[t][:, :], bias[:, 0:2 * D], ALU.add))
                           for t in range(T)]
                    v.tensor_tensor(qkv[u][:, :, 2 * D:3 * D], halves(PJ[2]),
                                    bias[:, 2 * D:3 * D].unsqueeze(1).broadcast_to([P, T, D]), ALU.add)\
                        .then_inc(qkv_taken[u], 1)
                    dve.wait_ge(qkv_taken[u], i + 1)
                    stats(u, lambda k: qkv[u][:, k // 3, k % 3 * D:(k % 3 + 1) * D], 3 * T, var2)
                for u in range(2):
                    dve.wait_ge(rstd2[u], i + 1)
                    for k in range(3 * T):
                        part = qkv[u][:, k // 3, k % 3 * D:(k % 3 + 1) * D]
                        last = normalize(u, part, part, k)
                    last.then_inc(qkvn_ready[u], 1)
                for u in range(2):
                    dve.wait_ge(scores_psum[u], i + 1)
                    v.tensor_reduce(nm[u][:, :], halves(X[u]), AX.X, ALU.max, negate=True).then_inc(max_ready[u], 1)
                for u in range(2):
                    dve.wait_ge(prT_psum[u], i + 1)
                    v.tensor_copy(prT[u][:, :, :], halves(Y[u])).then_inc(prT_ready[u], 1)
                for u in range(2):
                    r = steps.did(v.reciprocal(rden[u][:, :], den[u][:, :]))
                    dve.wait_ge(att_psum[u], i + 1)
                    steps.need(r)
                    m = [steps.did(v.scalar_tensor_tensor(x1[u][:, t, :], halves(X[u])[:, t, :], rden[u][:, t:t + 1],
                                                          xn[u][:, t, :], ALU.mult, ALU.add)) for t in range(T)]
                    steps.need(m[T - 1])
                    v.tensor_tensor(x1[u][:, :, :], x1[u][:, :, :], x[u][:, :, :], ALU.add).then_inc(x1_ready[u], 1)
                    dve.wait_ge(x1_ready[u], i + 1)
                    stats(u, lambda k: x1[u][:, k, :], T, var3)
                for u in range(2):
                    dve.wait_ge(rstd3[u], i + 1)
                    m = [steps.did(normalize(u, x1n[u][:, t, :], x1[u][:, t, :], t)) for t in range(T)]
                    dve.wait_ge(sums_psum[u], i + 1)
                    steps.need(m[T - 1])
                    v.tensor_tensor(x1n[u][:, :, :], x1n[u][:, :, :], halves(R[u]), ALU.mult).then_inc(sums_used[u], 1)
                    dve.wait_ge(sums_used[u], i + 1)
                    dve.wait_ge(x2_stored[u], 16 * i)
                    dve.wait_ge(x3_ready[u], i)
                    v.tensor_tensor(x2[u][:, :, :], x1[u][:, :, :], x1n[u][:, :, :], ALU.add).then_inc(x2_ready[u], 1)
                    dve.wait_ge(x2_ready[u], i + 1)
                    stats(u, lambda k: x2[u][:, k, :], T, var4)
                for u in range(2):
                    dve.wait_ge(rstd4[u], i + 1)
                    for t in range(T):
                        last = normalize(u, x2n[u][:, t, :], x2[u][:, t, :], t)
                    last.then_inc(x2n_ready[u], 1)
                for u in range(2):
                    dve.wait_ge(logits_psum[u], i + 1)
                    lgp = Y[u][:, 0:T * NE].rearrange("p (t e) -> p t e", t=T)
                    k = steps.did(v.tensor_tensor(lg[u][:, :, :], lgp, bsw[:, :].unsqueeze(1).broadcast_to([P, T, NE]),
                                                  ALU.add))
                    steps.need(k)
                    stand_alone(dve, dve_passed)
                    m = [steps.did(v.max(mx[u][:, t, :], lg[u][:, t, :])) for t in range(T)]
                    for t in range(T):
                        steps.need(m[t])
                        stand_alone(dve, dve_passed)
                        k = steps.did(v.max_index(ix[u][:, t, :], mx[u][:, t, :], lg[u][:, t, :]))
                    steps.need(k)
                    k = steps.did(v.tensor_copy(ixf[u][:, :], ix[u][:, :, 0]))
                    steps.need(k)
                    for t in range(T):
                        last = v.tensor_scalar(oh[u][:, t, :], iota8[:, :], ixf[u][:, t:t + 1], None, ALU.is_equal)
                    last.then_inc(onehot_ready[u], 1)
                for u in range(2):
                    dve.wait_ge(ranks_psum[u], i + 1)
                    rkp = Y[u][:, 64:64 + T * NE].rearrange("p (t e) -> p t e", t=T)
                    k = steps.did(v.tensor_tensor(rk[u][:, :, :], rkp, carry[:, :].unsqueeze(1).broadcast_to([P, T, NE]),
                                                  ALU.add))
                    steps.need(k)
                    c = steps.did(v.tensor_tensor(carry[:, :], carry[:, :], Y[u][:, 128:128 + NE], ALU.add))
                    steps.need(c)
                    k = steps.did(v.tensor_tensor(rk[u][:, :, :], rk[u][:, :, :], oh[u][:, :, :], ALU.mult))
                    steps.need(k)
                    k = steps.did(v.tensor_reduce(pos[u][:, :], rk[u][:, :, :], AX.X, ALU.add))
                    steps.need(k)
                    k = steps.did(v.tensor_scalar(over[u][:, :], pos[u][:, :], float(CAP), float(8 * SLOTS),
                                                  ALU.is_gt, ALU.mult))
                    k = steps.did(v.scalar_tensor_tensor(slot[u][:, :], ixf[u][:, :], float(CAP), pos[u][:, :],
                                                         ALU.mult, ALU.add))
                    steps.need(k)
                    dve.wait_ge(filed[u], 32 * i)
                    v.scalar_tensor_tensor(sloti[u][:, :], slot[u][:, :], -1.0, over[u][:, :],
                                           ALU.add, ALU.add).then_inc(slot_ready[u], 1)
                assert steps.n == 62, steps.n

            all_passes(dve, PAIRS, one_pass)

        @block.tensor
        def _(pe):
            t_ = nc.tensor

            def transposes(bank, src, done):
                for c in range(C):
                    for t in range(T):
                        last = t_.transpose(halves(bank)[:, c, t * P:(t + 1) * P], src[:, t, c * P:(c + 1) * P],
                                            ident[:, :])
                if done is not None:
                    last.then_inc(done, 1)

            pe.wait_ge(consts, 15)
            pe.wait_ge(weights_in, 16 * 14)
            def one_pass(i):
                for u in range(2):
                    pe.wait_ge(xn_ready[u], i + 1)
                    pe.wait_ge(x2nT_ready[u], i)
                    transposes(X[u], xn[u], xnT_psum[u])
                for u in range(2):
                    pe.wait_ge(xnT_ready[u], i + 1)
                    pe.wait_ge(qkv_taken[1 - u], i + u)
                    if u == 0:
                        pe.wait_ge(sums_used[1], i)
                    for t in range(T):
                        for c in range(C):
                            lhs = xnT[u][:, c, t * P:(t + 1) * P]
                            t_.matmul(PJ[t][:, :], lhs, w[:, c, 0:2 * D], start=c == 0, stop=c == C - 1)
                        for c in range(C):
                            lhs = xnT[u][:, c, t * P:(t + 1) * P]
                            last = t_.matmul(halves(PJ[2])[:, t, :], lhs, w[:, c, 2 * D:3 * D], start=c == 0,
                                             stop=c == C - 1)
                    last.then_inc(qkv_psum[u], 1)
                for u in range(2):
                    pe.wait_ge(kv_ready[u], i + 1)
                    if u == 0:
                        pe.wait_ge(sums_used[0], i)
                    else:
                        pe.wait_ge(qkv_taken[1], i + 1)
                    sums = halves(R[u])
                    t_.matmul(sums[:, 0, :], decay[:, 0, 0:P], kv[u][:, 0, :], start=True, stop=True)
                    t_.matmul(sums[:, 1, :], decay[:, 0, P:2 * P], kv[u][:, 0, :], start=True, stop=False)
                    t_.matmul(sums[:, 1, :], decay[:, 1, P:2 * P], kv[u][:, 1, :], start=False, stop=True)\
                        .then_inc(sums_psum[u], 1)
                    pe.wait_ge(qkvn_ready[u], i + 1)
                    pe.wait_ge(slot_ready[u], i)
                    transposes(X[u], qkv[u][:, :, 0:D], None)
                    transposes(Y[u], qkv[u][:, :, D:2 * D], qkT_psum[u])
                for u in range(2):
                    pe.wait_ge(qkT_ready[u], i + 1)
                    for t in range(T):
                        for c in range(C):
                            last = t_.matmul(halves(X[u])[:, t, :], kT[u][:, c, t * P:(t + 1) * P], qT[u][:, c, :],
                                             start=c == 0, stop=c == C - 1)
                    last.then_inc(scores_psum[u], 1)
                for u in range(2):
                    pe.wait_ge(probs_ready[u], i + 1)
                    transposes(Y[u], pr[u], prT_psum[u])
                for u in range(2):
                    pe.wait_ge(prT_ready[u], i + 1)
                    pe.wait_ge(v_ready[u], i + 1)
                    for t in range(T):
                        for c in range(T):
                            last = t_.matmul(halves(X[u])[:, t, :], prT[u][:, c, t * P:(t + 1) * P], vn[u][:, c, :],
                                             start=c == 0, stop=c == T - 1)
                    last.then_inc(att_psum[u], 1)
                for u in range(2):
                    pe.wait_ge(x2n_ready[u], i + 1)
                    transposes(X[u], x2n[u], x2nT_psum[u])
                for u in range(2):
                    pe.wait_ge(x2nT_ready[u], i + 1)
                    for t in range(T):
                        for c in range(C):
                            last = t_.matmul(Y[u][:, t * NE:(t + 1) * NE], x2nT[u][:, c, t * P:(t + 1) * P],
                                             wsw[:, c, :], start=c == 0, stop=c == C - 1)
                    last.then_inc(logits_psum[u], 1)
                for u in range(2):
                    pe.wait_ge(onehot_ready[u], i + 1)
                    t_.matmul(Y[u][:, 64:64 + NE], upto[:, :], oh[u][:, 0, :], start=True, stop=True)
                    t_.matmul(Y[u][:, 64 + NE:64 + 2 * NE], ones[:, :], oh[u][:, 0, :], start=True, stop=False)
                    t_.matmul(Y[u][:, 64 + NE:64 + 2 * NE], upto[:, :], oh[u][:, 1, :], start=False, stop=True)
                    t_.matmul(Y[u][:, 128:128 + NE], ones[:, :], oh[u][:, 0, :], start=True, stop=False)
                    t_.matmul(Y[u][:, 128:128 + NE], ones[:, :], oh[u][:, 1, :], start=False, stop=True)\
                        .then_inc(ranks_psum[u], 1)

            all_passes(pe, PAIRS, one_pass)

def phase_b(nc, a, x2_d, x3_d, table_d):
    NE, D, F = a["L0_ffn_W1"].shape
    SLOTS = table_d.shape[0]
    N_TOK = x2_d.shape[0]
    CAP = SLOTS // NE
    NT = 4
    N = NT * P
    C, FC = D // P, F // P
    Q = 4
    PASSES = SLOTS // N // Q
    RATIO = 2.0 ** 0.5 / 1.41421
    assert CAP == 2 * N
    with ExitStack() as ctx:
        sb = lambda name, shape, dt=F32: ctx.enter_context(nc.sbuf_tensor("b_" + name, shape, dt))
        sb2 = lambda name, shape, dt=F32: [sb(f"{name}{u}", shape, dt) for u in range(2)]
        sem = lambda name: nc.alloc_semaphore("b_" + name)
        sem2 = lambda name: [sem(f"{name}{u}") for u in range(2)]
        TB = [ctx.enter_context(nc.psum_tensor(f"b_T{n}", [P, 512], F32)) for n in range(2)]
        HB = [ctx.enter_context(nc.psum_tensor(f"b_H{n}", [P, 512], F32)) for n in range(4)]
        OB = [ctx.enter_context(nc.psum_tensor(f"b_O{n}", [P, 512], F32)) for n in range(2)]

        ident = sb("ident", [P, P])
        mhalf = sb("mhalf", [P, NT])
        idx_all = sb("idx_all", [P, SLOTS // N, NT], I32)
        idx = [sb(f"idx{q}", [P, NT], I32) for q in range(Q)]
        w1 = sb2("w1_", [P, C, F])
        w2 = sb2("w2_", [P, FC, D])
        b1 = sb2("b1_", [P, FC])
        b1r = sb2("b1r_", [P, FC])
        b2 = sb2("b2_", [P, D])
        xg = sb2("xg", [P, NT, D])
        st = sb2("st", [P, NT, 6])
        mv = sb2("mv", [P, NT, 2])
        rs = sb2("rs", [P, NT])
        xn = sb2("xn", [P, NT, D])
        xT = sb2("xT", [P, C, N])
        hT = sb2("hT", [P, FC, N])
        y = sb2("y", [P, NT, D])

        consts, table_in = sem("consts"), sem("table_in")
        w_loaded = sem2("w_loaded")
        gathered, scattered = sem2("gathered"), sem2("scattered")
        dve_step, pool_step, act_step = sem("dve_step"), sem("pool_step"), sem("act_step")
        dve_passed, pool_passed = sem("dve_passed"), sem("pool_passed")
        idx_ready = sem("idx_ready")
        var, rstd, xn_ready = sem2("var"), sem2("rstd"), sem2("xn_ready")
        xT_psum, xT_ready = sem2("xT_psum"), sem2("xT_ready")
        hidden_psum, hidden_ready = sem("hidden_psum"), sem("hidden_ready")
        out_psum, out_taken, y_ready = sem2("out_psum"), sem2("out_taken"), sem2("y_ready")
        b1_scaled = sem2("b1_scaled")

        block = ctx.enter_context(nc.Block())

        w1_v = a["L0_ffn_W1"].rearrange("(j q) (c p) f -> j q p c f", q=2, p=P)
        w2_v = a["L0_ffn_W2"].rearrange("(j q) (c p) f -> j q p c f", q=2, p=P)
        b1_v = a["L0_ffn_b1"].rearrange("(j q) (c p) -> j q p c", q=2, p=P)
        b2_v = a["L0_ffn_b2"].rearrange("(j q) d -> j q d", q=2)

        def turn(j, q):
            return q % 2, q // 2, 2 * j + q // 2

        def after(j, q):
            return (j, q + 1) if q + 1 < Q else (j + 1, 0)

        @block.sync
        def _(sync):
            def weights(j, p):
                sync.dma_start(w1[p][:, :, :], w1_v[j, p]).then_inc(w_loaded[p], 16)
                sync.dma_start(w2[p][:, :, :], w2_v[j, p]).then_inc(w_loaded[p], 16)
                sync.dma_start(b1[p][:, :], b1_v[j, p], allow_slow_non_contiguous=True).then_inc(w_loaded[p], 16)
                sync.dma_start(b2[p][:, :], b2_v[j, p].partition_broadcast(P)).then_inc(w_loaded[p], 16)

            sync.dma_start(idx_all[:, :, :], table_d.rearrange("(k p t) o -> p k (t o)", p=P, t=NT)).then_inc(table_in, 16)
            weights(0, 0)
            weights(0, 1)
            with sync.Fori(1, PASSES) as j:
                for p in range(2):
                    sync.wait_ge(y_ready[1], 2 * j + (p - 1))
                    weights(j, p)

        @block.gpsimd
        def _(pool):
            g = nc.gpsimd
            make_identity(nc, ident, consts, 0)
            g.memset(mhalf[:, :], -0.5).then_inc(consts, 1)
            for u in range(2):
                g.memset(xg[u][:, :, :], 0.0).then_inc(consts, 1)
            pool.wait_ge(consts, 5)
            pool.wait_ge(table_in, 16)
            steps = Steps(pool, pool_step)

            def gather(j, q):
                ch, p, n = turn(j, q)
                g.tensor_copy(idx[q][:, :], idx_all[:, bass.ds(Q * j + q, 1), :].rearrange("p k t -> p (k t)"))\
                    .then_inc(idx_ready, 1)
                pool.wait_ge(idx_ready, Q * j + q + 1)
                pool.wait_ge(out_taken[ch], n)
                stand_alone(pool, pool_passed)
                for t in range(NT):
                    g.indirect_dma_start(xg[ch][:, t, :], None, x2_d,
                                         bass.IndirectOffsetOnAxis(ap=idx[q][:, t:t + 1], axis=0),
                                         bounds_check=N_TOK - 1, oob_is_err=False).then_inc(gathered[ch], 16)
                pool.wait_ge(var[ch], n + 1)
                stand_alone(pool, pool_passed)
                e = steps.did(g.tensor_scalar(rs[ch][:, :], mv[ch][:, :, 1], EPS, None, ALU.add))
                steps.need(e)
                g.tensor_tensor(rs[ch][:, :], rs[ch][:, :], mhalf[:, :], ALU.pow).then_inc(rstd[ch], 1)

            def scatter(j, q):
                ch, p, n = turn(j, q)
                pool.wait_ge(out_taken[ch], n + 1)
                g.tensor_tensor(y[ch][:, :, :], y[ch][:, :, :], b2[p][:, :].unsqueeze(1).broadcast_to([P, NT, D]),
                                ALU.add).then_inc(y_ready[ch], 1)
                pool.wait_ge(y_ready[ch], n + 1)
                stand_alone(pool, pool_passed)
                for t in range(NT):
                    g.indirect_dma_start(x3_d, bass.IndirectOffsetOnAxis(ap=idx[q][:, t:t + 1], axis=0),
                                         y[ch][:, t, :], None, bounds_check=N_TOK - 1,
                                         oob_is_err=False).then_inc(scattered[ch], 16)

            def one_pass(j, last):
                steps.begin(1 + Q * j)
                for q in range(Q):
                    if not (last and q == Q - 1):
                        gather(*after(j, q))
                    scatter(j, q)

            gather(0, 0)
            one_pass(0, False)
            with pool.Fori(1, PASSES - 1) as j:
                one_pass(j, False)
            one_pass(PASSES - 1, True)
            for ch in range(2):
                pool.wait_ge(scattered[ch], 16 * NT * 2 * PASSES)

        @block.scalar
        def _(act):
            s = nc.scalar

            def take_xT(j, q):
                ch, p, n = turn(j, q)
                act.wait_ge(xT_psum[ch], n + 1)
                s.activation(xT[ch][:, 0, :], TB[0][:, :], ACT.Copy)
                s.activation(xT[ch][:, 1, :], TB[1][:, :], ACT.Copy).then_inc(xT_ready[ch], 1)

            def one_pass(j, last):
                for q in range(Q):
                    ch, p, n = turn(j, q)
                    if ch == 0:
                        act.wait_ge(w_loaded[p], 64 * (j + 1))
                        s.activation(b1r[p][:, :], b1[p][:, :], ACT.Copy, scale=RATIO).then_inc(b1_scaled[p], 1)
                        act.wait_ge(b1_scaled[p], j + 1)
                    for f in range(FC):
                        act.wait_ge(hidden_psum, (Q * j + q) * FC + f + 1)
                        s.activation(hT[ch][:, f, :], HB[f % 4][:, :], ACT.Gelu, bias=b1r[p][:, f:f + 1],
                                     scale=RATIO).then_inc(hidden_ready, 1)
                    if not (last and q == Q - 1):
                        take_xT(*after(j, q))

            take_xT(0, 0)
            one_pass(0, False)
            with act.Fori(1, PASSES - 1) as j:
                one_pass(j, False)
            one_pass(PASSES - 1, True)

        @block.vector
        def _(dve):
            v = nc.vector
            steps = Steps(dve, dve_step)

            def norm(j, q):
                ch, p, n = turn(j, q)
                dve.wait_ge(gathered[ch], 16 * NT * (n + 1))
                done = [steps.did(v.bn_stats(st[ch][:, t, :], xg[ch][:, t, :])) for t in range(NT)]
                for t in range(NT):
                    steps.need(done[t])
                    stand_alone(dve, dve_passed)
                    last = v.bn_aggr(mv[ch][:, t, :], st[ch][:, t, :])
                last.then_inc(var[ch], 1)
                dve.wait_ge(rstd[ch], n + 1)
                for t in range(NT):
                    last = v.tensor_scalar(xn[ch][:, t, :], xg[ch][:, t, :], mv[ch][:, t, 0:1], rs[ch][:, t:t + 1],
                                           ALU.subtract, ALU.mult)
                last.then_inc(xn_ready[ch], 1)

            def residual(j, q):
                ch, p, n = turn(j, q)
                dve.wait_ge(out_psum[ch], n + 1)
                dve.wait_ge(scattered[ch], 16 * NT * n)
                for b in range(2):
                    last = v.scalar_tensor_tensor(y[ch][:, 2 * b:2 * b + 2, :],
                                                  OB[b][:, :].rearrange("p (t d) -> p t d", t=2), 1.0 / RATIO,
                                                  xg[ch][:, 2 * b:2 * b + 2, :], ALU.mult, ALU.add)
                last.then_inc(out_taken[ch], 1)

            def one_pass(j, last):
                steps.begin(NT + NT * Q * j)
                for q in range(Q):
                    if not (last and q == Q - 1):
                        norm(*after(j, q))
                    residual(j, q)

            norm(0, 0)
            one_pass(0, False)
            with dve.Fori(1, PASSES - 1) as j:
                one_pass(j, False)
            one_pass(PASSES - 1, True)

        @block.tensor
        def _(pe):
            t_ = nc.tensor

            def transposes(j, q):
                ch, p, n = turn(j, q)
                pe.wait_ge(xn_ready[ch], n + 1)
                for c in range(C):
                    for t in range(NT):
                        last = t_.transpose(TB[c][:, t * P:(t + 1) * P], xn[ch][:, t, c * P:(c + 1) * P], ident[:, :])
                last.then_inc(xT_psum[ch], 1)

            def up(j, q):
                ch, p, n = turn(j, q)
                pe.wait_ge(xT_ready[ch], n + 1)
                if ch == 0:
                    pe.wait_ge(w_loaded[p], 64 * (j + 1))
                for f in range(FC):
                    if f >= 4:
                        pe.wait_ge(hidden_ready, (Q * j + q) * FC + f - 3)
                    for c in range(C):
                        last = t_.matmul(HB[f % 4][:, :], w1[p][:, c, f * P:(f + 1) * P], xT[ch][:, c, :],
                                         start=c == 0, stop=c == C - 1)
                    last.then_inc(hidden_psum, 1)

            def down(j, q):
                ch, p, n = turn(j, q)
                if ch == 0:
                    pe.wait_ge(out_taken[1], n)
                else:
                    pe.wait_ge(out_taken[0], n + 1)
                for t in range(NT):
                    for f in range(FC):
                        if t == 0:
                            pe.wait_ge(hidden_ready, (Q * j + q) * FC + f + 1)
                        last = t_.matmul(OB[t // 2][:, t % 2 * D:(t % 2 + 1) * D], hT[ch][:, f, t * P:(t + 1) * P],
                                         w2[p][:, f, :], start=f == 0, stop=f == FC - 1)
                last.then_inc(out_psum[ch], 1)

            def one_pass(j, last):
                for q in range(Q):
                    up(j, q)
                    if not (last and q == Q - 1):
                        transposes(*after(j, q))
                    down(j, q)

            pe.wait_ge(consts, 5)
            transposes(0, 0)
            one_pass(0, False)
            with pe.Fori(1, PASSES - 1) as j:
                one_pass(j, False)
            one_pass(PASSES - 1, True)


def phase_c(nc, a, x3_d, out):
    ctx_in = a["ctx_1024"]
    B, S, D = ctx_in.shape
    C, T = D // P, S // P
    DH = a["L1_attn_q_gamma"].shape[0]
    H = D // DH
    NE = a["L1_ffn_gate_w"].shape[1]
    PAIRS = B // 2
    HG = 4
    NG = H // HG
    SL = 4 * DH
    NB = H * SL // P
    with ExitStack() as ctx:
        sb = lambda name, shape, dt=F32: ctx.enter_context(nc.sbuf_tensor("c_" + name, shape, dt))
        sb2 = lambda name, shape, dt=F32: [sb(f"{name}{u}", shape, dt) for u in range(2)]
        sem = lambda name: nc.alloc_semaphore("c_" + name)
        sem2 = lambda name: [sem(f"{name}{u}") for u in range(2)]
        X = [ctx.enter_context(nc.psum_tensor(f"c_X{u}", [P, 512], F32)) for u in range(2)]
        Y = [ctx.enter_context(nc.psum_tensor(f"c_Y{u}", [P, 512], F32)) for u in range(2)]
        SR = [ctx.enter_context(nc.psum_tensor(f"c_S{n}", [P, 1024], F32)) for n in range(2)]
        halves = lambda bank: bank[:, 0:512].rearrange("p (c n) -> p c n", c=2)
        heads = lambda ring: ring[:, :].rearrange("p (h n) -> p h n", h=HG)
        place = lambda h: h % 2 * 2 + h % HG // 2

        ident = sb("ident", [P, P])
        identr = sb("identr", [P, P], F32R)
        ones = sb("ones", [P, 1])
        mhalf = sb("mhalf", [P, 2 * T * H])
        iota8 = sb("iota8", [P, NE])
        selh = sb("selh", [P, H, DH])
        wqkv = sb("wqkv", [P, C, 3 * D])
        wo = sb("wo", [P, C, D])
        wvx = sb("wvx", [P, C, D])
        wqk = sb("wqk", [P, C, D])
        g0 = sb("g0", [P, C])
        wr = sb("wr", [P, C])
        r0 = sb("r0", [P, 1])
        bvx = sb("bvx", [P, D])
        gam = sb("gam", [P, 2 * H, DH])
        bet = sb("bet", [P, 2 * H, DH])
        gw = sb("gw", [P, C, NE])
        gb = sb("gb", [P, NE])
        w1 = sb("w1", [P, NE, C, D])
        w2 = sb("w2", [P, NE, C, D])
        b1 = sb("b1", [P, NE, C])
        b2 = sb("b2", [NE, D])
        bqT, bkT = sb("bqT", [P, C]), sb("bkT", [P, C])

        q4 = sb("q4", [P, T, H, SL], F32R)
        k4 = sb("k4", [P, T, H, SL], F32R)
        PT = [sb(f"PT{n}", [P, T, HG, S]) for n in range(3)]
        sq = sb("sq", [P, T, 2 * H, DH])
        hid = [sb(f"hid{n}", [P, C, S]) for n in range(2)]

        x = sb2("x", [P, T, D])
        cx = sb2("cx", [P, T, D])
        cxT = sb2("cxT", [P, C, S])
        st = sb2("st", [P, T, 6])
        mv = sb2("mv", [P, T, 2])
        rs = sb2("rs", [P, T])
        xn = sb2("xn", [P, T, D])
        xnT = sb2("xnT", [P, C, S])
        qk = sb2("qk", [P, T, 2 * H, DH])
        hm = sb2("hm", [P, T * 2 * H])
        v32 = sb2("v32", [P, T, H, 2 * DH])
        q4T = sb2("q4T", [P, NB, S], F32R)
        k4T = sb2("k4T", [P, NB, S], F32R)
        nm = sb2("nm", [P, T, P])
        nmT = sb2("nmT", [P, S])
        rden = sb2("rden", [P, T, H])
        x4 = sb2("x4", [P, T, D])
        pe2 = sb2("pe2", [P, T, S + 1])
        m2 = sb2("m2", [P, T])
        nb2 = sb2("nb2", [P, T])
        r2 = sb2("r2", [P, T])
        den2 = sb2("den2", [P, T])
        rden2 = sb2("rden2", [P, T])
        peT = sb2("peT", [P, T, S])
        mix = sb2("mix", [P, T, D])
        x5 = sb2("x5", [P, T, D])
        lg = sb2("lg", [P, T, NE])
        mx = sb2("mx", [P, T, 8])
        ix = sb2("ix", [P, T, 8], U32)
        ixf = sb2("ixf", [P, T, 2])
        top = sb2("top", [P, T, NE])
        comb = sb2("comb", [P, T, NE])
        combT = sb2("combT", [NE, S])
        y = sb2("y", [P, T, D])
        oT = [t[:, :, :, :].rearrange("p t h d -> p (t h d)").rearrange("p (g s) -> p g s", g=NG) for t in qk]
        gT = [t[:, 0, :, :].rearrange("p h d -> p (h d)").rearrange("p (c s) -> p c s", c=C) for t in qk]
        gx = [t[:, 1, :, :].rearrange("p h d -> p (h d)").rearrange("p (c s) -> p c s", c=C) for t in qk]

        consts, w_in, dve_consts = sem("consts"), sem("w_in"), sem("dve_consts")
        pro_psum, pro_sb = sem("pro_psum"), sem("pro_sb")
        dve_step, pool_step, act_step = sem("dve_step"), sem("pool_step"), sem("act_step")
        dve_passed, pool_passed = sem("dve_passed"), sem("pool_passed")
        x_loaded, cx_loaded, out_stored = sem2("x_loaded"), sem2("cx_loaded"), sem2("out_stored")
        var, rstd, xn_ready = sem2("var"), sem2("rstd"), sem2("xn_ready")
        xnT_psum, xnT_ready = sem2("xnT_psum"), sem2("xnT_ready")
        cxT_psum, cxT_ready = sem2("cxT_psum"), sem2("cxT_ready")
        qk_psum, qk_taken = sem2("qk_psum"), sem2("qk_taken")
        v_psum, v_ready = sem2("v_psum"), sem2("v_ready")
        hsum, hmean, centred, hvar, hrstd = sem2("hsum"), sem2("hmean"), sem2("centred"), sem2("hvar"), sem2("hrstd")
        scaled, qk_ready, high_ready, low_ready = sem2("scaled"), sem2("qk_ready"), sem2("high_ready"), sem2("low_ready")
        q4T_psum, k4T_psum = sem("q4T_psum"), sem("k4T_psum")
        q4T_taken, k4T_taken = sem("q4T_taken"), sem("k4T_taken")
        raw_psum, raw_taken = sem("raw_psum"), sem("raw_taken")
        nm_ready, nmT_psum, nmT_ready, shift_ready = sem2("nm_ready"), sem2("nmT_psum"), sem2("nmT_ready"), sem2("shift_ready")
        scores_psum, probs_ready, probs_used = sem("scores_psum"), sem("probs_ready"), sem("probs_used")
        oT_ready, o_psum, o_ready = sem2("oT_ready"), sem2("o_psum"), sem2("o_ready")
        o2T_psum, o2T_ready, proj_psum, x4_ready = sem2("o2T_psum"), sem2("o2T_ready"), sem2("proj_psum"), sem2("x4_ready")
        g_psum, g_ready, gx_ready = sem2("g_psum"), sem2("g_ready"), sem2("gx_ready")
        s2_psum, nb2_ready, p2_ready = sem2("s2_psum"), sem2("nb2_ready"), sem2("p2_ready")
        peT_psum, peT_ready, mix_psum, mix_ready = sem2("peT_psum"), sem2("peT_ready"), sem2("mix_psum"), sem2("mix_ready")
        mixT_psum, mixT_ready, cross_psum, x5_ready = sem2("mixT_psum"), sem2("mixT_ready"), sem2("cross_psum"), sem2("x5_ready")
        gates_psum, comb_ready, combT_psum, combT_ready = sem2("gates_psum"), sem2("comb_ready"), sem2("combT_psum"), sem2("combT_ready")
        bias_psum = sem2("bias_psum")
        hid_psum, hid_ready, eo_psum, eo_taken = sem("hid_psum"), sem("hid_ready"), sem("eo_psum"), sem("eo_taken")

        rows = lambda t: t.rearrange("(i u t p) d -> i u p t d", u=2, t=T, p=P)
        x_rows, cx_rows, out_rows = rows(x3_d), rows(ctx_in.rearrange("b s d -> (b s) d")), rows(out.rearrange("b s d -> (b s) d"))
        by_chunk = lambda t: t.rearrange("(c p) n -> p c n", p=P)
        N_W = 20

        block = ctx.enter_context(nc.Block())

        @block.sync
        def _(sync):
            def load(i):
                for u in range(2):
                    sync.wait_ge(x4_ready[u], i)
                    sync.dma_start(x[u][:, :, :], x_rows[i, u]).then_inc(x_loaded[u], 16)
                for u in range(2):
                    sync.wait_ge(mix_psum[u], i)
                    sync.dma_start(cx[u][:, :, :], cx_rows[i, u]).then_inc(cx_loaded[u], 16)

            def store(i):
                for u in range(2):
                    sync.wait_ge(eo_taken, (2 * i + u + 1) * NE)
                    sync.dma_start(out_rows[i, u], y[u][:, :, :]).then_inc(out_stored[u], 16)

            def weight(dst, src, **kw):
                sync.dma_start(dst, src, **kw).then_inc(w_in, 16)

            load(0)
            col = dict(allow_slow_non_contiguous=True)
            weight(cxT[0][:, :, :], by_chunk(a["L1_xattn_Wq"]))
            weight(cxT[1][:, :, :], by_chunk(a["L1_xattn_Wk"]))
            weight(bqT[:, :], a["L1_xattn_bq"].rearrange("(c p) -> p c", p=P), **col)
            weight(bkT[:, :], a["L1_xattn_bk"].rearrange("(c p) -> p c", p=P), **col)
            weight(wqkv[:, :, :], by_chunk(a["L1_attn_w_qkv"]))
            weight(wo[:, :, :], by_chunk(a["L1_attn_w_proj"]))
            weight(wvx[:, :, :], by_chunk(a["L1_xattn_Wv"]))
            weight(bvx[:, :], a["L1_xattn_bv"].partition_broadcast(P))
            for n, name in enumerate("qk"):
                weight(gam[:, n * H, :], a[f"L1_attn_{name}_gamma"].partition_broadcast(P))
                weight(bet[:, n * H, :], a[f"L1_attn_{name}_beta"].partition_broadcast(P))
            weight(gw[:, :, :], by_chunk(a["L1_ffn_gate_w"]))
            weight(gb[:, :], a["L1_ffn_gate_b"].partition_broadcast(P))
            weight(w1[:, :, :, :], a["L1_ffn_w1"].rearrange("e (c p) n -> p e c n", p=P))
            weight(w2[:, :, :, :], a["L1_ffn_w2"].rearrange("e (c p) n -> p e c n", p=P))
            weight(b1[:, :, :], a["L1_ffn_b1"].rearrange("e (c p) -> p e c", p=P), **col)
            weight(b2[:, :], a["L1_ffn_b2"])
            with sync.Fori(0, PAIRS - 1) as i:
                load(i + 1)
                store(i)
            store(PAIRS - 1)
            for u in range(2):
                sync.wait_ge(out_stored[u], 16 * PAIRS)

        @block.gpsimd
        def _(pool):
            g = nc.gpsimd
            make_identity(nc, ident, consts, 0)
            g.memset(ones[:, :], 1.0).then_inc(consts, 1)
            g.memset(mhalf[:, :], -0.5).then_inc(consts, 1)
            g.iota(iota8[:, :], [[1, NE]], base=0, channel_multiplier=0,
                   allow_small_or_imprecise_dtypes=True).then_inc(consts, 1)
            g.memset(selh[:, :, :], 0.0).then_inc(consts, 1)
            pool.wait_ge(consts, 6)
            by_place = selh[:, :, :].rearrange("p (g a b) d -> p g a b d", a=2, b=2).rearrange("p g a b d -> p g a (b d)")
            for b in range(2):
                part = by_place[:, :, :, b * DH:(b + 1) * DH]
                g.affine_select(out=part, in_=part, compare_op=ALU.not_equal, fill=1.0, base=2 * b,
                                pattern=[[HG, NG], [1, 2], [-1, DH]], channel_multiplier=0).then_inc(consts, 1)
            for u in range(2):
                g.memset(v32[u][:, :, :, :], 0.0).then_inc(consts, 1)
                g.memset(nm[u][:, :, :], 0.0).then_inc(consts, 1)
            pool.wait_ge(consts, 12)
            for u in range(2):
                g.memset(v32[u][:, :, :, DH:DH + 1], 1.0).then_inc(consts, 1)
            pool.wait_ge(consts, 14)
            pool.wait_ge(w_in, 16 * 18)
            pool.wait_ge(dve_consts, 7)
            steps = Steps(pool, pool_step)

            def row_rstd(u, n):
                pool.wait_ge(var[u], n)
                stand_alone(pool, pool_passed)
                e = steps.did(g.tensor_scalar(rs[u][:, :], mv[u][:, :, 1], EPS, None, ALU.add))
                steps.need(e)
                g.tensor_tensor(rs[u][:, :], rs[u][:, :], mhalf[:, 0:T], ALU.pow).then_inc(rstd[u], 1)

            flat = lambda t: t[:, :, :, :].rearrange("p t h d -> p (t h d)")
            def one_pass(i):
                steps.begin(i * 12)
                for u in range(2):
                    row_rstd(u, 3 * i + 1)
                for u in range(2):
                    pool.wait_ge(hsum[u], i + 1)
                    stand_alone(pool, pool_passed)
                    g.tensor_scalar(hm[u][:, :], hm[u][:, :], 1.0 / DH, None, ALU.mult).then_inc(hmean[u], 1)
                    pool.wait_ge(hvar[u], i + 1)
                    stand_alone(pool, pool_passed)
                    e = steps.did(g.tensor_scalar(hm[u][:, :], hm[u][:, :], 1.0 / DH, EPS, ALU.mult, ALU.add))
                    steps.need(e)
                    g.tensor_tensor(hm[u][:, :], hm[u][:, :], mhalf[:, :], ALU.pow).then_inc(hrstd[u], 1)
                    pool.wait_ge(scaled[u], i + 1)
                    m = [steps.did(g.tensor_tensor(qk[u][:, t, :, :], qk[u][:, t, :, :], gam[:, :, :], ALU.mult))
                         for t in range(T)]
                    for t in range(T):
                        steps.need(m[t])
                        last = g.tensor_tensor(qk[u][:, t, :, :], qk[u][:, t, :, :], bet[:, :, :], ALU.add)
                    last.then_inc(qk_ready[u], 1)
                for u in range(2):
                    pool.wait_ge(nmT_ready[u], i + 1)
                    stand_alone(pool, pool_passed)
                    for half in range(2):
                        at = slice(64 * half, 64 * half + H)
                        last = g.tensor_copy(q4T[u][at, :, :], nmT[u][at, :].unsqueeze(1).broadcast_to([H, NB, S]))
                    last.then_inc(shift_ready[u], 1)
                for u in range(2):
                    row_rstd(u, 3 * i + 2)
                for u in range(2):
                    pool.wait_ge(g_ready[u], i + 1)
                    g.tensor_tensor(gx[u], gT[u], xnT[u][:, :, :], ALU.mult).then_inc(gx_ready[u], 1)
                for u in range(2):
                    row_rstd(u, 3 * i + 3)
                assert steps.n == 12, steps.n

            all_passes(pool, PAIRS, one_pass)

        @block.scalar
        def _(act):
            s = nc.scalar
            steps = Steps(act, act_step)
            act.wait_ge(pro_psum, 1)
            s.activation(xnT[0][:, :, :], halves(X[0]), ACT.Copy).then_inc(pro_sb, 1)
            s.activation(xnT[1][:, :, :], halves(X[1]), ACT.Copy).then_inc(pro_sb, 1)
            act.wait_ge(pro_psum, 2)
            s.activation(wqk[:, :, :], halves(X[0]), ACT.Copy).then_inc(pro_sb, 1)
            s.activation(g0[:, :], X[1][:, 0:C], ACT.Copy).then_inc(pro_sb, 1)
            s.activation(wr[:, :], X[1][:, C:2 * C], ACT.Copy).then_inc(pro_sb, 1)
            s.activation(r0[:, :], X[1][:, 2 * C:2 * C + 1], ACT.Copy).then_inc(pro_sb, 1)
            act.wait_ge(pro_sb, 6)
            act.wait_ge(w_in, 16 * 18)
            act.wait_ge(consts, 14)

            def take_xnT(u, n):
                act.wait_ge(xnT_psum[u], n)
                s.activation(xnT[u][:, :, :], halves(X[u]), ACT.Copy).then_inc(xnT_ready[u], 1)

            def one_pass(i):
                for u in range(2):
                    take_xnT(u, 3 * i + 1)
                    act.wait_ge(cxT_psum[u], i + 1)
                    s.activation(cxT[u][:, :, :], halves(Y[u]), ACT.Copy).then_inc(cxT_ready[u], 1)
                for u in range(2):
                    act.wait_ge(qk_psum[u], i + 1)
                    for t, bank in enumerate((X[u], Y[u])):
                        last = s.activation(qk[u][:, t, :, :], bank[:, :].rearrange("p (h d) -> p h d", d=DH), ACT.Copy)
                    last.then_inc(qk_taken[u], 1)
                for u in range(2):
                    act.wait_ge(v_psum[u], i + 1)
                    s.activation(v32[u][:, :, :, 0:DH], X[u][:, :].rearrange("p (t h d) -> p t h d", t=T, d=DH),
                                 ACT.Copy).then_inc(v_ready[u], 1)
                for u in range(2):
                    act.wait_ge(centred[u], i + 1)
                    if u == 1:
                        act.wait_ge(hvar[0], i + 1)
                    s.activation(sq[:, :, :, :], qk[u][:, :, :, :], ACT.Square).then_inc(act_step, 1)
                    act.wait_ge(qk_ready[u], i + 1)
                    act.wait_ge(k4T_psum, 4 * i + 2 * u)
                    for t in range(T):
                        src = lambda n: qk[u][:, t, n * H:(n + 1) * H, :].unsqueeze(2).broadcast_to([P, H, 2, DH])
                        s.activation(q4[:, t, :, DH:3 * DH].rearrange("p h (r d) -> p h r d", r=2), src(0), ACT.Copy)
                        k = k4[:, t, :, :].rearrange("p h (r d) -> p h r d", d=DH)[:, :, 1:4:2, :]
                        last = s.activation(k, src(1), ACT.Copy)
                    last.then_inc(high_ready[u], 1)
                    for t in range(T):
                        act.wait_ge(q4T_psum, 4 * i + 2 * u + t + 1)
                        s.activation(q4T[u][:, :, t * P:(t + 1) * P], SR[0][:, :].rearrange("p (b n) -> p b n", b=NB),
                                     ACT.Copy).then_inc(q4T_taken, 1)
                for u in range(2):
                    for g in range(NG):
                        n = (2 * i + u) * NG + g
                        act.wait_ge(probs_used, n - 2 if u * NG + g >= 3 else 2 * i * NG)
                        for t in range(T):
                            act.wait_ge(scores_psum, n * T + t + 1)
                            s.activation(PT[(u * NG + g) % 3][:, t, :, :], heads(SR[t]), ACT.Exp,
                                         scale=float(DH) ** -0.5).then_inc(probs_ready, 1)
                    act.wait_ge(probs_used, (2 * i + u + 1) * NG)
                    for b, bank in enumerate((X[u], Y[u])):
                        last = s.activation(oT[u][:, 2 * b:2 * b + 2, :], halves(bank), ACT.Copy)
                    last.then_inc(oT_ready[u], 1)
                for u in range(2):
                    act.wait_ge(o2T_psum[u], i + 1)
                    s.activation(xnT[u][:, :, :], halves(X[u]), ACT.Copy).then_inc(o2T_ready[u], 1)
                for u in range(2):
                    take_xnT(u, 3 * i + 2)
                for u in range(2):
                    act.wait_ge(g_psum[u], i + 1)
                    for c in range(C):
                        last = s.activation(gT[u][:, c, :], halves(Y[u])[:, c, :], ACT.Identity, bias=g0[:, c:c + 1])
                    last.then_inc(g_ready[u], 1)
                for u in range(2):
                    act.wait_ge(nb2_ready[u], i + 1)
                    for t, bank in enumerate((X[u], Y[u])):
                        last = s.activation(pe2[u][:, t, :], bank[:, 0:S + 1], ACT.Exp, bias=nb2[u][:, t:t + 1],
                                            accum_out=den2[u][:, t:t + 1])
                    last.then_inc(p2_ready[u], 1)
                for u in range(2):
                    act.wait_ge(mixT_psum[u], i + 1)
                    s.activation(peT[u][:, :, :], halves(X[u]), ACT.Copy).then_inc(mixT_ready[u], 1)
                for u in range(2):
                    take_xnT(u, 3 * i + 3)
                for u in range(2):
                    act.wait_ge(combT_psum[u], i + 1)
                    s.activation(combT[u][:, :], Y[u][0:NE, 128:128 + S], ACT.Copy).then_inc(combT_ready[u], 1)
                    for e in range(NE):
                        n = (2 * i + u) * NE + e
                        act.wait_ge(hid_psum, n + 1)
                        for c in range(C):
                            last = s.activation(hid[e % 2][:, c, :], SR[0][:, e % 2 * 512 + c * S:e % 2 * 512 + (c + 1) * S],
                                                ACT.Relu, bias=b1[:, e, c:c + 1])
                        last.then_inc(hid_ready, 1)

            all_passes(act, PAIRS, one_pass)

        @block.vector
        def _(dve):
            v = nc.vector
            dve.wait_ge(w_in, 16 * 18)
            dve.wait_ge(consts, 14)
            v.tensor_copy(identr[:, :], ident[:, :]).then_inc(dve_consts, 1)
            for n in range(2):
                for tile in (gam, bet):
                    v.tensor_copy(tile[:, n * H + 1:(n + 1) * H, :],
                                  tile[:, n * H:n * H + 1, :].broadcast_to([P, H - 1, DH])).then_inc(dve_consts, 1)
            for t in range(T):
                v.tensor_copy(k4[:, t, :, 0:DH], selh[:, :, :])
                last = v.tensor_scalar(q4[:, t, :, 0:DH], selh[:, :, :], 0.0, None, ALU.mult)
            last.then_inc(dve_consts, 1)
            v.memset(hm[0][:, :], 0.0).then_inc(dve_consts, 1)
            steps = Steps(dve, dve_step)

            def norm(u, src, n):
                done = [steps.did(v.bn_stats(st[u][:, t, :], src[:, t, :])) for t in range(T)]
                for t in range(T):
                    steps.need(done[t])
                    stand_alone(dve, dve_passed)
                    last = v.bn_aggr(mv[u][:, t, :], st[u][:, t, :])
                last.then_inc(var[u], 1)

            def norm_end(u, src, n):
                dve.wait_ge(rstd[u], n)
                for t in range(T):
                    last = v.tensor_scalar(xn[u][:, t, :], src[:, t, :], mv[u][:, t, 0:1], rs[u][:, t:t + 1],
                                           ALU.subtract, ALU.mult)
                last.then_inc(xn_ready[u], 1)

            def one_pass(i):
                steps.begin(i * 56)
                for u in range(2):
                    dve.wait_ge(x_loaded[u], 16 * i + 16)
                    norm(u, x[u], 3 * i + 1)
                for u in range(2):
                    norm_end(u, x[u], 3 * i + 1)
                for u in range(2):
                    q32 = qk[u][:, :, :, :].rearrange("p t h d -> p (t h) d")
                    s32 = sq[:, :, :, :].rearrange("p t h d -> p (t h) d")
                    over_head = hm[u][:, :].unsqueeze(2).broadcast_to([P, T * 2 * H, DH])
                    dve.wait_ge(qk_taken[u], i + 1)
                    v.tensor_reduce(hm[u][:, :], q32, AX.X, ALU.add).then_inc(hsum[u], 1)
                    dve.wait_ge(hmean[u], i + 1)
                    v.tensor_tensor(q32, q32, over_head, ALU.subtract).then_inc(centred[u], 1)
                    dve.wait_ge(act_step, 2 * i + u + 1)
                    v.tensor_reduce(hm[u][:, :], s32, AX.X, ALU.add).then_inc(hvar[u], 1)
                    dve.wait_ge(hrstd[u], i + 1)
                    v.tensor_tensor(q32, q32, over_head, ALU.mult).then_inc(scaled[u], 1)
                    dve.wait_ge(high_ready[u], i + 1)
                    for t in range(T):
                        for n, (dst, at) in enumerate(((q4, 3 * DH), (k4, 2 * DH))):
                            last = v.tensor_tensor(dst[:, t, :, at:at + DH], qk[u][:, t, n * H:(n + 1) * H, :],
                                                   dst[:, t, :, DH:2 * DH].bitcast(F32), ALU.subtract)
                    last.then_inc(low_ready[u], 1)
                    for t in range(T):
                        dve.wait_ge(k4T_psum, 4 * i + 2 * u + t + 1)
                        v.tensor_copy(k4T[u][:, :, t * P:(t + 1) * P], SR[1][:, :].rearrange("p (b n) -> p b n", b=NB))\
                            .then_inc(k4T_taken, 1)
                for u in range(2):
                    for f in range(T * NG):
                        t, g = f // NG, f % NG
                        dve.wait_ge(raw_psum, (2 * i + u) * T * NG + f + 1)
                        v.tensor_reduce(nm[u][:, t, g * HG:(g + 1) * HG], heads(SR[f % 2]), AX.X, ALU.max, negate=True)\
                            .then_inc(raw_taken, 1)
                    dve.wait_ge(raw_taken, (2 * i + u + 1) * T * NG)
                    v.tensor_copy(nm[u][:, :, 64:64 + H], nm[u][:, :, 0:H]).then_inc(nm_ready[u], 1)
                for u in range(2):
                    dve.wait_ge(nmT_psum[u], i + 1)
                    v.tensor_copy(nmT[u][:, :], X[u][:, 0:S]).then_inc(nmT_ready[u], 1)
                for u in range(2):
                    dve.wait_ge(o_psum[u], i + 1)
                    for t, bank in enumerate((X[u], Y[u])):
                        o = bank[:, :].rearrange("p (h d) -> p h d", h=H)
                        k = steps.did(v.reciprocal(rden[u][:, t, :], o[:, :, DH]))
                        steps.need(k)
                        last = v.tensor_tensor(xn[u][:, t, :].rearrange("p (h d) -> p h d", h=H), o[:, :, 0:DH],
                                               rden[u][:, t, :].unsqueeze(2).broadcast_to([P, H, DH]), ALU.mult)
                    last.then_inc(o_ready[u], 1)
                for u in range(2):
                    dve.wait_ge(proj_psum[u], i + 1)
                    v.tensor_tensor(x4[u][:, :, :], x[u][:, :, :], halves(Y[u]), ALU.add).then_inc(x4_ready[u], 1)
                    dve.wait_ge(x4_ready[u], i + 1)
                    norm(u, x4[u], 3 * i + 2)
                for u in range(2):
                    norm_end(u, x4[u], 3 * i + 2)
                    dve.wait_ge(xn_ready[u], 3 * i + 2)
                    k = steps.did(v.tensor_tensor(x4[u][:, :, :], x4[u][:, :, :],
                                                  bvx[:, :].unsqueeze(1).broadcast_to([P, T, D]), ALU.add))
                for u in range(2):
                    dve.wait_ge(s2_psum[u], i + 1)
                    for t, bank in enumerate((X[u], Y[u])):
                        steps.did(v.tensor_reduce(m2[u][:, t:t + 1], bank[:, 0:S + 1], AX.X, ALU.max))
                        k = steps.did(v.tensor_scalar(r2[u][:, t:t + 1], bank[:, S + 2:S + 3], r0[:, 0:1], None, ALU.add))
                    steps.need(k)
                    k = steps.did(v.tensor_tensor(m2[u][:, :], m2[u][:, :], r2[u][:, :], ALU.add))
                    steps.need(k)
                    v.tensor_tensor(nb2[u][:, :], r2[u][:, :], m2[u][:, :], ALU.subtract).then_inc(nb2_ready[u], 1)
                for u in range(2):
                    dve.wait_ge(peT_psum[u], i + 1)
                    v.tensor_copy(peT[u][:, :, :], halves(X[u])).then_inc(peT_ready[u], 1)
                    for t in range(T):
                        k = steps.did(v.tensor_scalar(mix[u][:, t, :], xn[u][:, t, :], pe2[u][:, t, S:S + 1], None,
                                                      ALU.mult))
                    steps.did(v.reciprocal(rden2[u][:, :], den2[u][:, :]))
                    dve.wait_ge(mix_psum[u], i + 1)
                    steps.need(k)
                    v.tensor_tensor(mix[u][:, :, :], mix[u][:, :, :], halves(Y[u]), ALU.add).then_inc(mix_ready[u], 1)
                for u in range(2):
                    dve.wait_ge(cross_psum[u], i + 1)
                    for t in range(T):
                        last = v.scalar_tensor_tensor(x5[u][:, t, :], halves(Y[u])[:, t, :], rden2[u][:, t:t + 1],
                                                      x4[u][:, t, :], ALU.mult, ALU.add)
                    last.then_inc(x5_ready[u], 1)
                    dve.wait_ge(x5_ready[u], i + 1)
                    norm(u, x5[u], 3 * i + 3)
                for u in range(2):
                    norm_end(u, x5[u], 3 * i + 3)
                for u in range(2):
                    dve.wait_ge(gates_psum[u], i + 1)
                    k = steps.did(v.tensor_tensor(lg[u][:, :, :], Y[u][:, 0:T * NE].rearrange("p (t e) -> p t e", t=T),
                                                  gb[:, :].unsqueeze(1).broadcast_to([P, T, NE]), ALU.add))
                    steps.need(k)
                    stand_alone(dve, dve_passed)
                    for t in range(T):
                        k = steps.did(v.max(mx[u][:, t, :], lg[u][:, t, :]))
                    steps.need(k)
                    stand_alone(dve, dve_passed)
                    for t in range(T):
                        k = steps.did(v.max_index(ix[u][:, t, :], mx[u][:, t, :], lg[u][:, t, :]))
                    steps.need(k)
                    k = steps.did(v.tensor_copy(ixf[u][:, :, :], ix[u][:, :, 0:2]))
                    steps.need(k)
                    for t in range(T):
                        steps.did(v.scalar_tensor_tensor(comb[u][:, t, :], iota8[:, :], ixf[u][:, t, 0:1],
                                                         lg[u][:, t, :], ALU.is_equal, ALU.mult))
                        k = steps.did(v.scalar_tensor_tensor(top[u][:, t, :], iota8[:, :], ixf[u][:, t, 1:2],
                                                             lg[u][:, t, :], ALU.is_equal, ALU.mult))
                    steps.need(k)
                    v.tensor_tensor(comb[u][:, :, :], comb[u][:, :, :], top[u][:, :, :], ALU.add).then_inc(comb_ready[u], 1)
                for u in range(2):
                    dve.wait_ge(bias_psum[u], i + 1)
                    dve.wait_ge(out_stored[u], 16 * i)
                    k = steps.did(v.tensor_tensor(y[u][:, :, :], x5[u][:, :, :], halves(X[u]), ALU.add))
                    steps.need(k)
                    for e in range(NE):
                        n = (2 * i + u) * NE + e
                        dve.wait_ge(eo_psum, n + 1)
                        if e:
                            dve.wait_ge(eo_taken, n)
                        for t in range(T):
                            at = e % 2 * 512 + t * D
                            last = v.scalar_tensor_tensor(y[u][:, t, :], SR[1][:, at:at + D], comb[u][:, t, e:e + 1],
                                                          y[u][:, t, :], ALU.mult, ALU.add)
                        last.then_inc(eo_taken, 1)
                assert steps.n == 56, steps.n

            all_passes(dve, PAIRS, one_pass)

        @block.tensor
        def _(pe):
            t_ = nc.tensor

            def transposes(bank, src):
                for c in range(C):
                    for t in range(T):
                        last = t_.transpose(halves(bank)[:, c, t * P:(t + 1) * P], src[:, t, c * P:(c + 1) * P],
                                            ident[:, :])
                return last

            def project(bank, srcT, weight):
                for t in range(T):
                    for c in range(C):
                        last = t_.matmul(halves(bank)[:, t, :], srcT[:, c, t * P:(t + 1) * P], weight[:, c, :],
                                         start=c == 0, stop=c == C - 1)
                return last

            pe.wait_ge(consts, 14)
            pe.wait_ge(w_in, 16 * 18)
            pe.wait_ge(dve_consts, 7)
            transposes(X[0], cxT[0])
            transposes(X[1], cxT[1]).then_inc(pro_psum, 1)
            pe.wait_ge(pro_sb, 2)
            wqT, wkT = xnT
            for m in range(C):
                cols = slice(m * P, (m + 1) * P)
                for c in range(C):
                    t_.matmul(halves(X[0])[:, m, :], wqT[:, c, cols], wkT[:, c, :], start=c == 0, stop=c == C - 1)
                for c in range(C):
                    t_.matmul(X[1][:, m:m + 1], wkT[:, c, cols], bqT[:, c:c + 1], start=c == 0, stop=c == C - 1)
                for c in range(C):
                    t_.matmul(X[1][:, C + m:C + m + 1], wqT[:, c, cols], bkT[:, c:c + 1], start=c == 0, stop=c == C - 1)
            for c in range(C):
                last = t_.matmul(X[1][:, 2 * C:2 * C + 1], bqT[:, c:c + 1].broadcast_to([P, P]), bkT[:, c:c + 1],
                                 start=c == 0, stop=c == C - 1)
            last.then_inc(pro_psum, 1)
            pe.wait_ge(pro_sb, 6)

            def one_pass(i):
                for u in range(2):
                    pe.wait_ge(xn_ready[u], 3 * i + 1)
                    pe.wait_ge(eo_taken, 2 * i * NE)
                    transposes(X[u], xn[u]).then_inc(xnT_psum[u], 1)
                    pe.wait_ge(cx_loaded[u], 16 * i + 16)
                    transposes(Y[u], cx[u]).then_inc(cxT_psum[u], 1)
                for u in range(2):
                    pe.wait_ge(xnT_ready[u], 3 * i + 1)
                    pe.wait_ge(cxT_ready[u], i + 1)
                    for t, bank in enumerate((X[u], Y[u])):
                        for c in range(C):
                            last = t_.matmul(bank[:, :], xnT[u][:, c, t * P:(t + 1) * P], wqkv[:, c, 0:2 * D],
                                             start=c == 0, stop=c == C - 1)
                    last.then_inc(qk_psum[u], 1)
                for u in range(2):
                    pe.wait_ge(qk_taken[u], i + 1)
                    project(X[u], xnT[u], wqkv[:, :, 2 * D:3 * D]).then_inc(v_psum[u], 1)
                for u in range(2):
                    pe.wait_ge(low_ready[u], i + 1)
                    for t in range(T):
                        for src, ring, full, taken in ((q4, SR[0], q4T_psum, q4T_taken), (k4, SR[1], k4T_psum, k4T_taken)):
                            pe.wait_ge(taken, 4 * i + 2 * u + t)
                            for b in range(NB):
                                last = t_.transpose(ring[:, b * P:(b + 1) * P].bitcast(F32R),
                                                    src[:, t, 2 * b:2 * b + 2, :].rearrange("p h n -> p (h n)"),
                                                    identr[:, :])
                            last.then_inc(full, 1)
                for u in range(2):
                    pe.wait_ge(q4T_taken, 4 * i + 4)
                    pe.wait_ge(k4T_taken, 4 * i + 4)
                    for f in range(T * NG):
                        t, g = f // NG, f % NG
                        n = (2 * i + u) * T * NG + f
                        if u or f >= 2:
                            pe.wait_ge(raw_taken, n - 1)
                        for h in range(g * HG, (g + 1) * HG):
                            at = slice(h % 2 * SL, h % 2 * SL + SL)
                            last = t_.matmul(heads(SR[f % 2])[:, place(h), :], q4T[u][at, h // 2, t * P:(t + 1) * P],
                                             k4T[u][at, h // 2, :], start=True, stop=True)
                        last.then_inc(raw_psum, 1)
                for u in range(2):
                    pe.wait_ge(nm_ready[u], i + 1)
                    pe.wait_ge(v_ready[u], i + 1)
                    for t in range(T):
                        last = t_.transpose(X[u][:, t * P:(t + 1) * P], nm[u][:, t, :], ident[:, :])
                    last.then_inc(nmT_psum[u], 1)
                for u in range(2):
                    def scores(g):
                        n = (2 * i + u) * NG + g
                        for t in range(T):
                            if u or g:
                                pe.wait_ge(probs_ready, (n - 1) * T + t + 1)
                            for h in range(g * HG, (g + 1) * HG):
                                at = slice(h % 2 * SL, h % 2 * SL + SL)
                                last = t_.matmul(heads(SR[t])[:, place(h), :], k4T[u][at, h // 2, t * P:(t + 1) * P],
                                                 q4T[u][at, h // 2, :], start=True, stop=True)
                            last.then_inc(scores_psum, 1)

                    def weighted(g):
                        n = (2 * i + u) * NG + g
                        pe.wait_ge(probs_ready, (n + 1) * T)
                        bank = halves((X[u], Y[u])[g // 2])[:, g % 2, :]
                        for t in range(T):
                            for h in range(HG):
                                last = t_.matmul(bank[h * 2 * DH:(h + 1) * 2 * DH, :], v32[u][:, t, g * HG + h, :],
                                                 PT[(u * NG + g) % 3][:, t, place(h), :], start=t == 0, stop=t == T - 1)
                        last.then_inc(probs_used, 1)

                    pe.wait_ge(shift_ready[u], i + 1)
                    pe.wait_ge(raw_taken, (2 * i + 2) * T * NG)
                    scores(0)
                    for g in range(1, NG):
                        scores(g)
                        weighted(g - 1)
                    weighted(NG - 1)
                for u in range(2):
                    pe.wait_ge(oT_ready[u], i + 1)
                    for t, bank in enumerate((X[u], Y[u])):
                        for g in range(NG):
                            last = t_.transpose(bank[:, g * P:(g + 1) * P], oT[u][:, g, t * P:(t + 1) * P], ident[:, :])
                    last.then_inc(o_psum[u], 1)
                for u in range(2):
                    pe.wait_ge(o_ready[u], i + 1)
                    transposes(X[u], xn[u]).then_inc(o2T_psum[u], 1)
                for u in range(2):
                    pe.wait_ge(o2T_ready[u], i + 1)
                    project(Y[u], xnT[u], wo).then_inc(proj_psum[u], 1)
                for u in range(2):
                    pe.wait_ge(xn_ready[u], 3 * i + 2)
                    transposes(X[u], xn[u]).then_inc(xnT_psum[u], 1)
                for u in range(2):
                    pe.wait_ge(xnT_ready[u], 3 * i + 2)
                    for m in range(C):
                        for c in range(C):
                            last = t_.matmul(halves(Y[u])[:, m, :], wqk[:, c, m * P:(m + 1) * P], xnT[u][:, c, :],
                                             start=c == 0, stop=c == C - 1)
                    last.then_inc(g_psum[u], 1)
                for u in range(2):
                    pe.wait_ge(g_ready[u], i + 1)
                    pe.wait_ge(gx_ready[u], i + 1)
                    for t, bank in enumerate((X[u], Y[u])):
                        cols = slice(t * P, (t + 1) * P)
                        for lhs, rhs, at in ((gT[u], lambda c: cxT[u][:, c, :], slice(0, S)),
                                             (gx[u], lambda c: ones[:, :], slice(S, S + 1)),
                                             (xnT[u], lambda c: wr[:, c:c + 1], slice(S + 2, S + 3))):
                            for c in range(C):
                                last = t_.matmul(bank[:, at], lhs[:, c, cols], rhs(c), start=c == 0, stop=c == C - 1)
                    last.then_inc(s2_psum[u], 1)
                for u in range(2):
                    pe.wait_ge(p2_ready[u], i + 1)
                    transposes(X[u], pe2[u]).then_inc(peT_psum[u], 1)
                for u in range(2):
                    pe.wait_ge(peT_ready[u], i + 1)
                    project(Y[u], peT[u], cx[u]).then_inc(mix_psum[u], 1)
                for u in range(2):
                    pe.wait_ge(mix_ready[u], i + 1)
                    transposes(X[u], mix[u]).then_inc(mixT_psum[u], 1)
                for u in range(2):
                    pe.wait_ge(mixT_ready[u], i + 1)
                    project(Y[u], peT[u], wvx).then_inc(cross_psum[u], 1)
                for u in range(2):
                    pe.wait_ge(xn_ready[u], 3 * i + 3)
                    transposes(X[u], xn[u]).then_inc(xnT_psum[u], 1)
                for u in range(2):
                    pe.wait_ge(xnT_ready[u], 3 * i + 3)
                    for t in range(T):
                        for c in range(C):
                            last = t_.matmul(Y[u][:, t * NE:(t + 1) * NE], xnT[u][:, c, t * P:(t + 1) * P], gw[:, c, :],
                                             start=c == 0, stop=c == C - 1)
                    last.then_inc(gates_psum[u], 1)
                for u in range(2):
                    pe.wait_ge(comb_ready[u], i + 1)
                    for t in range(T):
                        last = t_.transpose(Y[u][0:NE, P + t * P:P + (t + 1) * P], comb[u][:, t, :], ident[:, :])
                    last.then_inc(combT_psum[u], 1)
                for u in range(2):
                    pe.wait_ge(combT_ready[u], i + 1)
                    for t in range(T):
                        last = t_.matmul(halves(X[u])[:, t, :], combT[u][:, t * P:(t + 1) * P], b2[:, :], start=True, stop=True)
                    last.then_inc(bias_psum[u], 1)

                    def up(e):
                        n = (2 * i + u) * NE + e
                        if u or e >= 2:
                            pe.wait_ge(hid_ready, n - 1)
                        for m in range(C):
                            for c in range(C):
                                at = e % 2 * 512 + m * S
                                last = t_.matmul(SR[0][:, at:at + S], w1[:, e, c, m * P:(m + 1) * P], xnT[u][:, c, :],
                                                 start=c == 0, stop=c == C - 1)
                        last.then_inc(hid_psum, 1)

                    def down(e):
                        n = (2 * i + u) * NE + e
                        pe.wait_ge(hid_ready, n + 1)
                        if u or e >= 2:
                            pe.wait_ge(eo_taken, n - 1)
                        for t in range(T):
                            for m in range(C):
                                at = e % 2 * 512 + t * D
                                last = t_.matmul(SR[1][:, at:at + D], hid[e % 2][:, m, t * P:(t + 1) * P], w2[:, e, m, :],
                                                 start=m == 0, stop=m == C - 1)
                        last.then_inc(eo_psum, 1)

                    up(0)
                    for e in range(1, NE):
                        up(e)
                        down(e - 1)
                    down(NE - 1)

            all_passes(pe, PAIRS, one_pass)

_INS = [
    "x", "ctx_1024",
    *[f"L0_attn_{n}" for n in ("Wk", "bk", "gk", "betak", "Wq", "bq", "gq", "betaq", "Wv", "bv", "gv", "betav")],
    *[f"L0_ffn_{n}" for n in ("W_sw", "b_sw", "W1", "b1", "W2", "b2")],
    *[f"L1_attn_{n}" for n in ("w_qkv", "w_proj", "q_gamma", "q_beta", "k_gamma", "k_beta")],
    *[f"L1_xattn_{n}" for n in ("Wq", "bq", "Wk", "bk", "Wv", "bv")],
    *[f"L1_ffn_{n}" for n in ("gate_w", "gate_b", "w1", "b1", "w2", "b2")],
]


def decoder(nc, a, out):
    B, S, D = a["x"].shape
    x2_d = nc.dram_tensor("x2_scratch", (B * S, D), F32).ap()
    x3_d = nc.dram_tensor("x3_scratch", (B * S, D), F32).ap()
    table_d = nc.dram_tensor("slot_table", (B * S, 1), I32).ap()
    with nc.cleanup_on_exit():
        phase_a(nc, a, x2_d, x3_d, table_d)
    nc.all_engine_barrier()
    with nc.cleanup_on_exit():
        phase_b(nc, a, x2_d, x3_d, table_d)
    nc.all_engine_barrier()
    phase_c(nc, a, x3_d, out)


def kernel(**inputs):
    import numpy as _np
    import concourse.bacc as _bacc
    from concourse import mybir as _mybir
    from concourse.bass_utils import run_bass_kernel_spmd as _run

    nc = _bacc.Bacc("TRN2", target_bir_lowering=False, num_devices=1)
    arrays, args = {}, {}
    for name in _INS:
        arrays[f"in_{name}_dram"] = _np.ascontiguousarray(inputs[name])
        args[name] = nc.dram_tensor(f"in_{name}_dram", arrays[f"in_{name}_dram"].shape, _mybir.dt.float32,
                                    kind="ExternalInput").ap()
    out = nc.dram_tensor("out_0_dram", inputs["x"].shape, _mybir.dt.float32, kind="ExternalOutput").ap()
    decoder(nc, args, out)
    r = _run(nc, [arrays], core_ids=[0])
    return r.results[0]["out_0_dram"]
```

```python
from contextlib import ExitStack
from functools import partial

import concourse.bass as bass
from concourse import mybir

F32 = mybir.dt.float32
F32R = mybir.dt.float32r
I32 = mybir.dt.int32
U32 = mybir.dt.uint32
ALU = mybir.AluOpType
ACT = mybir.ActivationFunctionType
AX = mybir.AxisListType

P = 128
EPS = 1e-5


def skewed(eng, pairs, order, parts, *steps):
    def beside(front, back):
        for n, here in enumerate((front, back)):
            if here and steps:
                u, i = here
                steps[n].begin(2 * i + u)
        for part in order:
            here = front if part[0] == "f" else back
            if here and part in parts:
                parts[part](*here)

    def one_pair(i):
        beside((0, i), (1, i - 1) if not isinstance(i, int) or i > 0 else None)
        beside((1, i), (0, i))

    one_pair(0)
    one_pair(1)
    with eng.Fori(2, pairs) as i:
        one_pair(i)
    beside(None, (1, pairs - 1))


def all_passes(eng, count, one_pass):
    one_pass(0)
    with eng.Fori(1, count) as i:
        one_pass(i)


def stand_alone(eng, passed):
    eng.sem_inc(passed, 1)


class Steps:

    def __init__(self, eng, sem, each, before=0):
        self.eng, self.sem, self.each, self.before, self.base, self.n = eng, sem, each, before, 0, 0

    def begin(self, passes):
        assert self.n in (0, self.before, self.each), self.n
        self.base, self.n = self.before + self.each * passes, 0

    def did(self, ins):
        self.n += 1
        ins.then_inc(self.sem, 1)
        return self.n

    def need(self, n):
        self.eng.wait_ge(self.sem, self.base + n)


def make_identity(nc, tile, ready, before):
    nc.gpsimd.memset(tile[:, :], 0.0).then_inc(ready, 1)
    nc.gpsimd.wait_ge(ready, before + 1)
    nc.gpsimd.affine_select(out=tile[:, :], in_=tile[:, :], compare_op=ALU.not_equal, fill=1.0, base=0,
                            pattern=[[-1, P]], channel_multiplier=1).then_inc(ready, 1)


def phase_a(nc, a, x2_d, x3_d, table_d):
    x_in, ctx_in = a["x"], a["ctx_1024"]
    B, S, D = x_in.shape
    C, T = D // P, S // P
    NE = a["L0_ffn_W_sw"].shape[1]
    CAP = B * S // NE
    PAIRS = B // 2
    SLOTS = NE * CAP
    with ExitStack() as ctx:
        sb = lambda name, shape, dt=F32: ctx.enter_context(nc.sbuf_tensor("a_" + name, shape, dt))
        sb2 = lambda name, shape, dt=F32: [sb(f"{name}{u}", shape, dt) for u in range(2)]
        sem = lambda name: nc.alloc_semaphore("a_" + name)
        sem2 = lambda name: [sem(f"{name}{u}") for u in range(2)]
        X = [ctx.enter_context(nc.psum_tensor(f"a_X{u}", [P, 512], F32)) for u in range(2)]
        Y = [ctx.enter_context(nc.psum_tensor(f"a_Y{u}", [P, 512], F32)) for u in range(2)]
        PJ = [ctx.enter_context(nc.psum_tensor(f"a_PJ{n}", [P, 512], F32)) for n in range(3)]
        R = [ctx.enter_context(nc.psum_tensor("a_R", [P, 512], F32)), PJ[0]]
        halves = lambda bank: bank[:, :].rearrange("p (c n) -> p c n", c=2)

        ident = sb("ident", [P, P])
        ones = sb("ones", [P, P])
        upto = sb("upto", [P, P])
        decay = sb("decay", [P, T, S])
        expo = sb("expo", [P, T * S])
        nine = sb("nine", [P, T * S])
        mhalf = sb("mhalf", [P, 6])
        iota8 = sb("iota8", [P, NE])
        empty = sb("empty", [P, SLOTS // P], I32)
        w = sb("w", [P, C, 3 * D])
        bias = sb("bias", [P, 3 * D])
        gqT, bqT = sb("gqT", [P, C]), sb("bqT", [P, C])
        gkT, bkT = sb("gkT", [P, C]), sb("bkT", [P, C])
        gv, bv = sb("gv", [P, D]), sb("bv", [P, D])
        wsw = sb("wsw", [P, C, NE])
        bsw = sb("bsw", [P, NE])
        carry = sb("carry", [P, NE])

        x = sb2("x", [P, T, D])
        cx = sb2("cx", [P, T, D])
        kv = sb2("kv", [P, T, D])
        st = sb2("st", [P, 6, 6])
        mv = sb2("mv", [P, 6, 2])
        rs = sb2("rs", [P, 6])
        xn = sb2("xn", [P, T, D])
        xnT = sb2("xnT", [P, C, S])
        qkv = sb2("qkv", [P, T, 3 * D])
        vn = sb2("vn", [P, T, D])
        qT = sb2("qT", [P, C, S])
        kT = sb2("kT", [P, C, S])
        nm = sb2("nm", [P, T])
        pr = sb2("pr", [P, T, S])
        prT = sb2("prT", [P, T, S])
        den = sb2("den", [P, T])
        rden = sb2("rden", [P, T])
        x1 = sb2("x1", [P, T, D])
        x1n = sb2("x1n", [P, T, D])
        x2 = sb2("x2", [P, T, D])
        x2n = sb2("x2n", [P, T, D])
        x2nT = sb2("x2nT", [P, C, S])
        x3 = sb2("x3", [P, T, D])
        lg = sb2("lg", [P, T, NE])
        mx = sb2("mx", [P, T, 8])
        ix = sb2("ix", [P, T, 8], U32)
        ixf = sb2("ixf", [P, T])
        oh = sb2("oh", [P, T, NE])
        rk = sb2("rk", [P, T, NE])
        pos = sb2("pos", [P, T])
        slot = sb2("slot", [P, T])
        over = sb2("over", [P, T])
        sloti = sb2("sloti", [P, T], I32)
        tok = sb2("tok", [P, T], I32)

        weights_in = sem("weights_in")
        consts = sem("consts")
        table_empty = sem("table_empty")
        x_in_s, cx_in_s = sem2("x_loaded"), sem2("ctx_loaded")
        dve_step, pool_step = sem("dve_step"), sem("pool_step")
        dve_passed, pool_passed = sem("dve_passed"), sem("pool_passed")
        var1, rstd1 = sem2("var1"), sem2("rstd1")
        xn_ready, xnT_psum, xnT_ready = sem2("xn_ready"), sem2("xnT_psum"), sem2("xnT_ready")
        qkv_psum, qkv_taken = sem2("qkv_psum"), sem2("qkv_taken")
        var2, rstd2, qkvn_ready, v_ready = sem2("var2"), sem2("rstd2"), sem2("qkvn_ready"), sem2("v_ready")
        qkT_psum, qkT_ready = sem2("qkT_psum"), sem2("qkT_ready")
        scores_psum, max_ready, probs_ready = sem2("scores_psum"), sem2("max_ready"), sem2("probs_ready")
        kv_ready, sums_psum, sums_used = sem2("kv_ready"), sem2("sums_psum"), sem2("sums_used")
        prT_psum, prT_ready, att_psum = sem2("prT_psum"), sem2("prT_ready"), sem2("att_psum")
        x1_ready, var3, rstd3 = sem2("x1_ready"), sem2("var3"), sem2("rstd3")
        x2_ready, var4, rstd4, x2n_ready = sem2("x2_ready"), sem2("var4"), sem2("rstd4"), sem2("x2n_ready")
        x3_ready = sem2("x3_ready")
        x2nT_psum, x2nT_ready, logits_psum = sem2("x2nT_psum"), sem2("x2nT_ready"), sem2("logits_psum")
        onehot_ready, ranks_psum, slot_ready = sem2("onehot_ready"), sem2("ranks_psum"), sem2("slot_ready")
        x2_stored, x3_stored, filed = sem2("x2_stored"), sem2("x3_stored"), sem2("filed")

        rows = lambda t: t.rearrange("(i u t p) d -> i u p t d", u=2, t=T, p=P)
        x_rows = rows(x_in.rearrange("b s d -> (b s) d"))
        cx_rows = rows(ctx_in.rearrange("b s d -> (b s) d"))
        x2_rows, x3_rows = rows(x2_d), rows(x3_d)
        

        block = ctx.enter_context(nc.Block())

        @block.sync
        def _(sync):
            def load(i):
                for u in range(2):
                    sync.wait_ge(x1_ready[u], i)
                    sync.dma_start(x[u][:, :, :], x_rows[i, u]).then_inc(x_in_s[u], 16)
                for u in range(2):
                    sync.wait_ge(kv_ready[u], i)
                    sync.dma_start(cx[u][:, :, :], cx_rows[i, u]).then_inc(cx_in_s[u], 16)

            def store(i):
                for u in range(2):
                    sync.wait_ge(x2_ready[u], i + 1)
                    sync.dma_start(x2_rows[i, u], x2[u][:, :, :]).then_inc(x2_stored[u], 16)
                    sync.wait_ge(x3_ready[u], i + 1)
                    sync.dma_start(x3_rows[i, u], x3[u][:, :, :]).then_inc(x3_stored[u], 16)

            load(0)
            for n, name in enumerate("qkv"):
                cols = slice(n * D, (n + 1) * D)
                sync.dma_start(w[:, :, cols], a[f"L0_attn_W{name}"].rearrange("(c p) n -> p c n", p=P))\
                    .then_inc(weights_in, 16)
                sync.dma_start(bias[:, cols], a[f"L0_attn_b{name}"].partition_broadcast(P)).then_inc(weights_in, 16)
            for tile, name in ((gqT, "gq"), (bqT, "betaq"), (gkT, "gk"), (bkT, "betak")):
                sync.dma_start(tile[:, :], a[f"L0_attn_{name}"].rearrange("(c p) -> p c", p=P),
                               allow_slow_non_contiguous=True).then_inc(weights_in, 16)
            for tile, name in ((gv, "gv"), (bv, "betav")):
                sync.dma_start(tile[:, :], a[f"L0_attn_{name}"].partition_broadcast(P)).then_inc(weights_in, 16)
            sync.dma_start(wsw[:, :, :], a["L0_ffn_W_sw"].rearrange("(c p) n -> p c n", p=P)).then_inc(weights_in, 16)
            sync.dma_start(bsw[:, :], a["L0_ffn_b_sw"].partition_broadcast(P)).then_inc(weights_in, 16)
            sync.wait_ge(consts, 12)
            sync.dma_start(table_d.rearrange("(p n) o -> p (n o)", p=P), empty[:, :]).then_inc(table_empty, 16)
            with sync.Fori(0, PAIRS - 1) as i:
                load(i + 1)
                store(i)
            store(PAIRS - 1)
            for u in range(2):
                sync.wait_ge(x2_stored[u], 16 * PAIRS)
                sync.wait_ge(x3_stored[u], 16 * PAIRS)

        @block.gpsimd
        def _(pool):
            g = nc.gpsimd
            make_identity(nc, ident, consts, 0)
            g.memset(ones[:, :], 1.0).then_inc(consts, 1)
            pool.wait_ge(consts, 3)
            g.affine_select(out=upto[:, :], in_=ones[:, :], compare_op=ALU.is_ge, fill=0.0, base=0,
                            pattern=[[1, P]], channel_multiplier=-1).then_inc(consts, 1)
            g.iota(expo[:, :], [[-P, T], [1, S]], base=0, channel_multiplier=-1,
                   allow_small_or_imprecise_dtypes=True).then_inc(consts, 1)
            g.memset(nine[:, :], 0.9).then_inc(consts, 1)
            pool.wait_ge(consts, 6)
            g.tensor_scalar(expo[:, :], expo[:, :], 0.0, None, ALU.max).then_inc(consts, 1)
            pool.wait_ge(consts, 7)
            g.tensor_tensor(expo[:, :], nine[:, :], expo[:, :], ALU.pow).then_inc(consts, 1)
            pool.wait_ge(consts, 8)
            g.affine_select(out=decay[:, :, :], in_=expo[:, :].rearrange("p (t s) -> p t s", t=T),
                            compare_op=ALU.is_ge, fill=0.0, base=0, pattern=[[-P, T], [1, S]],
                            channel_multiplier=-1).then_inc(consts, 1)
            g.memset(mhalf[:, :], -0.5).then_inc(consts, 1)
            g.iota(iota8[:, :], [[1, NE]], base=0, channel_multiplier=0,
                   allow_small_or_imprecise_dtypes=True).then_inc(consts, 1)
            g.iota(empty[:, :], [[1, SLOTS // P]], base=8 * SLOTS, channel_multiplier=SLOTS // P).then_inc(consts, 1)
            g.memset(carry[:, :], 0.0).then_inc(consts, 1)
            for u in range(2):
                g.iota(tok[u][:, :], [[P, T]], base=(u - 2) * S, channel_multiplier=1).then_inc(consts, 1)
            pool.wait_ge(consts, 15)
            pool.wait_ge(weights_in, 16 * 14)
            pool.wait_ge(table_empty, 16)
            steps = Steps(pool, pool_step, 14)

            def rstd(u, i, n, var, out):
                pool.wait_ge(var[u], i + 1)
                stand_alone(pool, pool_passed)
                e = steps.did(g.tensor_scalar(rs[u][:, 0:n], mv[u][:, 0:n, 1], EPS, None, ALU.add))
                steps.need(e)
                g.tensor_tensor(rs[u][:, 0:n], rs[u][:, 0:n], mhalf[:, 0:n], ALU.pow).then_inc(out[u], 1)

            def one_pass(i):
                steps.begin(i)
                for u in range(2):
                    rstd(u, i, T, var1, rstd1)
                for u in range(2):
                    rstd(u, i, 3 * T, var2, rstd2)
                    pool.wait_ge(qkvn_ready[u], i + 1)
                    pool.wait_ge(att_psum[u], i)
                    m = [steps.did(g.tensor_tensor(vn[u][:, t, :], qkv[u][:, t, 2 * D:3 * D], gv[:, :], ALU.mult))
                         for t in range(T)]
                    for t in range(T):
                        steps.need(m[t])
                        last = g.tensor_tensor(vn[u][:, t, :], vn[u][:, t, :], bv[:, :], ALU.add)
                        if t == T - 1:
                            last.then_inc(v_ready[u], 1)
                for u in range(2):
                    rstd(u, i, T, var3, rstd3)
                    rstd(u, i, T, var4, rstd4)
                for u in range(2):
                    pool.wait_ge(x2n_ready[u], i + 1)
                    pool.wait_ge(x3_stored[u], 16 * i)
                    g.tensor_tensor(x3[u][:, :, :], x2[u][:, :, :], x2n[u][:, :, :], ALU.add).then_inc(x3_ready[u], 1)
                    pool.wait_ge(filed[u], 32 * i)
                    stand_alone(pool, pool_passed)
                    k = steps.did(g.tensor_scalar(tok[u][:, :], tok[u][:, :], float(2 * S), None, ALU.add))
                    steps.need(k)
                    pool.wait_ge(slot_ready[u], i + 1)
                    stand_alone(pool, pool_passed)
                    for t in range(T):
                        g.indirect_dma_start(table_d, bass.IndirectOffsetOnAxis(ap=sloti[u][:, t:t + 1], axis=0),
                                             tok[u][:, t:t + 1], None, bounds_check=SLOTS - 1,
                                             oob_is_err=False).then_inc(filed[u], 16)

            all_passes(pool, PAIRS, one_pass)
            for u in range(2):
                pool.wait_ge(filed[u], 32 * PAIRS)

        @block.scalar
        def _(act):
            s = nc.scalar
            act.wait_ge(weights_in, 16 * 14)
            def one_pass(i):
                for u in range(2):
                    act.wait_ge(xnT_psum[u], i + 1)
                    s.activation(xnT[u][:, :, :], halves(X[u]), ACT.Copy).then_inc(xnT_ready[u], 1)
                for u in range(2):
                    act.wait_ge(cx_in_s[u], 16 * i + 16)
                    act.wait_ge(sums_psum[u], i)
                    s.activation(kv[u][:, :, :], cx[u][:, :, :], ACT.Square).then_inc(kv_ready[u], 1)
                for u in range(2):
                    act.wait_ge(qkT_psum[u], i + 1)
                    for c in range(C):
                        s.activation(qT[u][:, c, :], halves(X[u])[:, c, :], ACT.Identity,
                                     bias=bqT[:, c:c + 1], scale=gqT[:, c:c + 1])
                        last = s.activation(kT[u][:, c, :], halves(Y[u])[:, c, :], ACT.Identity,
                                            bias=bkT[:, c:c + 1], scale=gkT[:, c:c + 1])
                    last.then_inc(qkT_ready[u], 1)
                for u in range(2):
                    act.wait_ge(max_ready[u], i + 1)
                    for t in range(T):
                        last = s.activation(pr[u][:, t, :], halves(X[u])[:, t, :], ACT.Exp, bias=nm[u][:, t:t + 1],
                                            accum_out=den[u][:, t:t + 1])
                    last.then_inc(probs_ready[u], 1)
                for u in range(2):
                    act.wait_ge(x2nT_psum[u], i + 1)
                    s.activation(x2nT[u][:, :, :], halves(X[u]), ACT.Copy).then_inc(x2nT_ready[u], 1)

            all_passes(act, PAIRS, one_pass)

        @block.vector
        def _(dve):
            v = nc.vector
            dve.wait_ge(weights_in, 16 * 14)
            dve.wait_ge(consts, 15)
            steps = Steps(dve, dve_step, 62)

            def stats(u, src, n, ready):
                done = [steps.did(v.bn_stats(st[u][:, k, :], src(k))) for k in range(n)]
                for k in range(n):
                    steps.need(done[k])
                    stand_alone(dve, dve_passed)
                    last = v.bn_aggr(mv[u][:, k, :], st[u][:, k, :])
                    if k == n - 1:
                        last.then_inc(ready[u], 1)

            def normalize(u, dst, src, k):
                return v.tensor_scalar(dst, src, mv[u][:, k, 0:1], rs[u][:, k:k + 1], ALU.subtract, ALU.mult)

            def one_pass(i):
                steps.begin(i)
                for u in range(2):
                    dve.wait_ge(x_in_s[u], 16 * i + 16)
                    stats(u, lambda k: x[u][:, k, :], T, var1)
                for u in range(2):
                    dve.wait_ge(rstd1[u], i + 1)
                    for t in range(T):
                        last = normalize(u, xn[u][:, t, :], x[u][:, t, :], t)
                    last.then_inc(xn_ready[u], 1)
                for u in range(2):
                    dve.wait_ge(qkv_psum[u], i + 1)
                    add = [steps.did(v.tensor_tensor(qkv[u][:, t, 0:2 * D], PJ[t][:, :], bias[:, 0:2 * D], ALU.add))
                           for t in range(T)]
                    v.tensor_tensor(qkv[u][:, :, 2 * D:3 * D], halves(PJ[2]),
                                    bias[:, 2 * D:3 * D].unsqueeze(1).broadcast_to([P, T, D]), ALU.add)\
                        .then_inc(qkv_taken[u], 1)
                    dve.wait_ge(qkv_taken[u], i + 1)
                    stats(u, lambda k: qkv[u][:, k // 3, k % 3 * D:(k % 3 + 1) * D], 3 * T, var2)
                for u in range(2):
                    dve.wait_ge(rstd2[u], i + 1)
                    for k in range(3 * T):
                        part = qkv[u][:, k // 3, k % 3 * D:(k % 3 + 1) * D]
                        last = normalize(u, part, part, k)
                    last.then_inc(qkvn_ready[u], 1)
                for u in range(2):
                    dve.wait_ge(scores_psum[u], i + 1)
                    v.tensor_reduce(nm[u][:, :], halves(X[u]), AX.X, ALU.max, negate=True).then_inc(max_ready[u], 1)
                for u in range(2):
                    dve.wait_ge(prT_psum[u], i + 1)
                    v.tensor_copy(prT[u][:, :, :], halves(Y[u])).then_inc(prT_ready[u], 1)
                for u in range(2):
                    r = steps.did(v.reciprocal(rden[u][:, :], den[u][:, :]))
                    dve.wait_ge(att_psum[u], i + 1)
                    steps.need(r)
                    m = [steps.did(v.scalar_tensor_tensor(x1[u][:, t, :], halves(X[u])[:, t, :], rden[u][:, t:t + 1],
                                                          xn[u][:, t, :], ALU.mult, ALU.add)) for t in range(T)]
                    steps.need(m[T - 1])
                    v.tensor_tensor(x1[u][:, :, :], x1[u][:, :, :], x[u][:, :, :], ALU.add).then_inc(x1_ready[u], 1)
                    dve.wait_ge(x1_ready[u], i + 1)
                    stats(u, lambda k: x1[u][:, k, :], T, var3)
                for u in range(2):
                    dve.wait_ge(rstd3[u], i + 1)
                    m = [steps.did(normalize(u, x1n[u][:, t, :], x1[u][:, t, :], t)) for t in range(T)]
                    dve.wait_ge(sums_psum[u], i + 1)
                    steps.need(m[T - 1])
                    v.tensor_tensor(x1n[u][:, :, :], x1n[u][:, :, :], halves(R[u]), ALU.mult).then_inc(sums_used[u], 1)
                    dve.wait_ge(sums_used[u], i + 1)
                    dve.wait_ge(x2_stored[u], 16 * i)
                    dve.wait_ge(x3_ready[u], i)
                    v.tensor_tensor(x2[u][:, :, :], x1[u][:, :, :], x1n[u][:, :, :], ALU.add).then_inc(x2_ready[u], 1)
                    dve.wait_ge(x2_ready[u], i + 1)
                    stats(u, lambda k: x2[u][:, k, :], T, var4)
                for u in range(2):
                    dve.wait_ge(rstd4[u], i + 1)
                    for t in range(T):
                        last = normalize(u, x2n[u][:, t, :], x2[u][:, t, :], t)
                    last.then_inc(x2n_ready[u], 1)
                for u in range(2):
                    dve.wait_ge(logits_psum[u], i + 1)
                    lgp = Y[u][:, 0:T * NE].rearrange("p (t e) -> p t e", t=T)
                    k = steps.did(v.tensor_tensor(lg[u][:, :, :], lgp, bsw[:, :].unsqueeze(1).broadcast_to([P, T, NE]),
                                                  ALU.add))
                    steps.need(k)
                    stand_alone(dve, dve_passed)
                    m = [steps.did(v.max(mx[u][:, t, :], lg[u][:, t, :])) for t in range(T)]
                    for t in range(T):
                        steps.need(m[t])
                        stand_alone(dve, dve_passed)
                        k = steps.did(v.max_index(ix[u][:, t, :], mx[u][:, t, :], lg[u][:, t, :]))
                    steps.need(k)
                    k = steps.did(v.tensor_copy(ixf[u][:, :], ix[u][:, :, 0]))
                    steps.need(k)
                    for t in range(T):
                        last = v.tensor_scalar(oh[u][:, t, :], iota8[:, :], ixf[u][:, t:t + 1], None, ALU.is_equal)
                    last.then_inc(onehot_ready[u], 1)
                for u in range(2):
                    dve.wait_ge(ranks_psum[u], i + 1)
                    rkp = Y[u][:, 64:64 + T * NE].rearrange("p (t e) -> p t e", t=T)
                    k = steps.did(v.tensor_tensor(rk[u][:, :, :], rkp, carry[:, :].unsqueeze(1).broadcast_to([P, T, NE]),
                                                  ALU.add))
                    steps.need(k)
                    c = steps.did(v.tensor_tensor(carry[:, :], carry[:, :], Y[u][:, 128:128 + NE], ALU.add))
                    steps.need(c)
                    k = steps.did(v.tensor_tensor(rk[u][:, :, :], rk[u][:, :, :], oh[u][:, :, :], ALU.mult))
                    steps.need(k)
                    k = steps.did(v.tensor_reduce(pos[u][:, :], rk[u][:, :, :], AX.X, ALU.add))
                    steps.need(k)
                    k = steps.did(v.tensor_scalar(over[u][:, :], pos[u][:, :], float(CAP), float(8 * SLOTS),
                                                  ALU.is_gt, ALU.mult))
                    k = steps.did(v.scalar_tensor_tensor(slot[u][:, :], ixf[u][:, :], float(CAP), pos[u][:, :],
                                                         ALU.mult, ALU.add))
                    steps.need(k)
                    dve.wait_ge(filed[u], 32 * i)
                    v.scalar_tensor_tensor(sloti[u][:, :], slot[u][:, :], -1.0, over[u][:, :],
                                           ALU.add, ALU.add).then_inc(slot_ready[u], 1)

            all_passes(dve, PAIRS, one_pass)

        @block.tensor
        def _(pe):
            t_ = nc.tensor

            def transposes(bank, src, done):
                for c in range(C):
                    for t in range(T):
                        last = t_.transpose(halves(bank)[:, c, t * P:(t + 1) * P], src[:, t, c * P:(c + 1) * P],
                                            ident[:, :])
                if done is not None:
                    last.then_inc(done, 1)

            pe.wait_ge(consts, 15)
            pe.wait_ge(weights_in, 16 * 14)
            def one_pass(i):
                for u in range(2):
                    pe.wait_ge(xn_ready[u], i + 1)
                    pe.wait_ge(x2nT_ready[u], i)
                    transposes(X[u], xn[u], xnT_psum[u])
                for u in range(2):
                    pe.wait_ge(xnT_ready[u], i + 1)
                    pe.wait_ge(qkv_taken[1 - u], i + u)
                    if u == 0:
                        pe.wait_ge(sums_used[1], i)
                    for t in range(T):
                        for c in range(C):
                            lhs = xnT[u][:, c, t * P:(t + 1) * P]
                            t_.matmul(PJ[t][:, :], lhs, w[:, c, 0:2 * D], start=c == 0, stop=c == C - 1)
                        for c in range(C):
                            lhs = xnT[u][:, c, t * P:(t + 1) * P]
                            last = t_.matmul(halves(PJ[2])[:, t, :], lhs, w[:, c, 2 * D:3 * D], start=c == 0,
                                             stop=c == C - 1)
                    last.then_inc(qkv_psum[u], 1)
                for u in range(2):
                    pe.wait_ge(kv_ready[u], i + 1)
                    if u == 0:
                        pe.wait_ge(sums_used[0], i)
                    else:
                        pe.wait_ge(qkv_taken[1], i + 1)
                    sums = halves(R[u])
                    t_.matmul(sums[:, 0, :], decay[:, 0, 0:P], kv[u][:, 0, :], start=True, stop=True)
                    t_.matmul(sums[:, 1, :], decay[:, 0, P:2 * P], kv[u][:, 0, :], start=True, stop=False)
                    t_.matmul(sums[:, 1, :], decay[:, 1, P:2 * P], kv[u][:, 1, :], start=False, stop=True)\
                        .then_inc(sums_psum[u], 1)
                    pe.wait_ge(qkvn_ready[u], i + 1)
                    pe.wait_ge(slot_ready[u], i)
                    transposes(X[u], qkv[u][:, :, 0:D], None)
                    transposes(Y[u], qkv[u][:, :, D:2 * D], qkT_psum[u])
                for u in range(2):
                    pe.wait_ge(qkT_ready[u], i + 1)
                    for t in range(T):
                        for c in range(C):
                            last = t_.matmul(halves(X[u])[:, t, :], kT[u][:, c, t * P:(t + 1) * P], qT[u][:, c, :],
                                             start=c == 0, stop=c == C - 1)
                    last.then_inc(scores_psum[u], 1)
                for u in range(2):
                    pe.wait_ge(probs_ready[u], i + 1)
                    transposes(Y[u], pr[u], prT_psum[u])
                for u in range(2):
                    pe.wait_ge(prT_ready[u], i + 1)
                    pe.wait_ge(v_ready[u], i + 1)
                    for t in range(T):
                        for c in range(T):
                            last = t_.matmul(halves(X[u])[:, t, :], prT[u][:, c, t * P:(t + 1) * P], vn[u][:, c, :],
                                             start=c == 0, stop=c == T - 1)
                    last.then_inc(att_psum[u], 1)
                for u in range(2):
                    pe.wait_ge(x2n_ready[u], i + 1)
                    transposes(X[u], x2n[u], x2nT_psum[u])
                for u in range(2):
                    pe.wait_ge(x2nT_ready[u], i + 1)
                    for t in range(T):
                        for c in range(C):
                            last = t_.matmul(Y[u][:, t * NE:(t + 1) * NE], x2nT[u][:, c, t * P:(t + 1) * P],
                                             wsw[:, c, :], start=c == 0, stop=c == C - 1)
                    last.then_inc(logits_psum[u], 1)
                for u in range(2):
                    pe.wait_ge(onehot_ready[u], i + 1)
                    t_.matmul(Y[u][:, 64:64 + NE], upto[:, :], oh[u][:, 0, :], start=True, stop=True)
                    t_.matmul(Y[u][:, 64 + NE:64 + 2 * NE], ones[:, :], oh[u][:, 0, :], start=True, stop=False)
                    t_.matmul(Y[u][:, 64 + NE:64 + 2 * NE], upto[:, :], oh[u][:, 1, :], start=False, stop=True)
                    t_.matmul(Y[u][:, 128:128 + NE], ones[:, :], oh[u][:, 0, :], start=True, stop=False)
                    t_.matmul(Y[u][:, 128:128 + NE], ones[:, :], oh[u][:, 1, :], start=False, stop=True)\
                        .then_inc(ranks_psum[u], 1)

            all_passes(pe, PAIRS, one_pass)

def phase_b(nc, a, x2_d, x3_d, table_d):
    NE, D, F = a["L0_ffn_W1"].shape
    SLOTS = table_d.shape[0]
    N_TOK = x2_d.shape[0]
    CAP = SLOTS // NE
    NT = 4
    N = NT * P
    C, FC = D // P, F // P
    Q = 4
    PASSES = SLOTS // N // Q
    RATIO = 2.0 ** 0.5 / 1.41421
    assert CAP == 2 * N
    with ExitStack() as ctx:
        sb = lambda name, shape, dt=F32: ctx.enter_context(nc.sbuf_tensor("b_" + name, shape, dt))
        sb2 = lambda name, shape, dt=F32: [sb(f"{name}{u}", shape, dt) for u in range(2)]
        sem = lambda name: nc.alloc_semaphore("b_" + name)
        sem2 = lambda name: [sem(f"{name}{u}") for u in range(2)]
        TB = [ctx.enter_context(nc.psum_tensor(f"b_T{n}", [P, 512], F32)) for n in range(2)]
        HB = [ctx.enter_context(nc.psum_tensor(f"b_H{n}", [P, 512], F32)) for n in range(4)]
        OB = [ctx.enter_context(nc.psum_tensor(f"b_O{n}", [P, 512], F32)) for n in range(2)]

        ident = sb("ident", [P, P])
        mhalf = sb("mhalf", [P, NT])
        idx_all = sb("idx_all", [P, SLOTS // N, NT], I32)
        idx = [sb(f"idx{q}", [P, NT], I32) for q in range(Q)]
        w1 = sb2("w1_", [P, C, F])
        w2 = sb2("w2_", [P, FC, D])
        b1 = sb2("b1_", [P, FC])
        b1r = sb2("b1r_", [P, FC])
        b2 = sb2("b2_", [P, D])
        xg = sb2("xg", [P, NT, D])
        st = sb2("st", [P, NT, 6])
        mv = sb2("mv", [P, NT, 2])
        rs = sb2("rs", [P, NT])
        xn = sb2("xn", [P, NT, D])
        xT = sb2("xT", [P, C, N])
        hT = sb2("hT", [P, FC, N])
        y = sb2("y", [P, NT, D])

        consts, table_in = sem("consts"), sem("table_in")
        w_loaded = sem2("w_loaded")
        gathered, scattered = sem2("gathered"), sem2("scattered")
        dve_step, pool_step, act_step = sem("dve_step"), sem("pool_step"), sem("act_step")
        dve_passed, pool_passed = sem("dve_passed"), sem("pool_passed")
        idx_ready = sem("idx_ready")
        var, rstd, xn_ready = sem2("var"), sem2("rstd"), sem2("xn_ready")
        xT_psum, xT_ready = sem2("xT_psum"), sem2("xT_ready")
        hidden_psum, hidden_ready = sem("hidden_psum"), sem("hidden_ready")
        out_psum, out_taken, y_ready = sem2("out_psum"), sem2("out_taken"), sem2("y_ready")
        b1_scaled = sem2("b1_scaled")

        block = ctx.enter_context(nc.Block())

        w1_v = a["L0_ffn_W1"].rearrange("(j q) (c p) f -> j q p c f", q=2, p=P)
        w2_v = a["L0_ffn_W2"].rearrange("(j q) (c p) f -> j q p c f", q=2, p=P)
        b1_v = a["L0_ffn_b1"].rearrange("(j q) (c p) -> j q p c", q=2, p=P)
        b2_v = a["L0_ffn_b2"].rearrange("(j q) d -> j q d", q=2)

        def turn(j, q):
            return q % 2, q // 2, 2 * j + q // 2

        def after(j, q):
            return (j, q + 1) if q + 1 < Q else (j + 1, 0)

        @block.sync
        def _(sync):
            def weights(j, p):
                sync.dma_start(w1[p][:, :, :], w1_v[j, p]).then_inc(w_loaded[p], 16)
                sync.dma_start(w2[p][:, :, :], w2_v[j, p]).then_inc(w_loaded[p], 16)
                sync.dma_start(b1[p][:, :], b1_v[j, p], allow_slow_non_contiguous=True).then_inc(w_loaded[p], 16)
                sync.dma_start(b2[p][:, :], b2_v[j, p].partition_broadcast(P)).then_inc(w_loaded[p], 16)

            sync.dma_start(idx_all[:, :, :], table_d.rearrange("(k p t) o -> p k (t o)", p=P, t=NT)).then_inc(table_in, 16)
            weights(0, 0)
            weights(0, 1)
            with sync.Fori(1, PASSES) as j:
                for p in range(2):
                    sync.wait_ge(y_ready[1], 2 * j + (p - 1))
                    weights(j, p)

        @block.gpsimd
        def _(pool):
            g = nc.gpsimd
            make_identity(nc, ident, consts, 0)
            g.memset(mhalf[:, :], -0.5).then_inc(consts, 1)
            for u in range(2):
                g.memset(xg[u][:, :, :], 0.0).then_inc(consts, 1)
            pool.wait_ge(consts, 5)
            pool.wait_ge(table_in, 16)
            steps = Steps(pool, pool_step, Q, 1)

            def gather(j, q):
                ch, p, n = turn(j, q)
                g.tensor_copy(idx[q][:, :], idx_all[:, bass.ds(Q * j + q, 1), :].rearrange("p k t -> p (k t)"))\
                    .then_inc(idx_ready, 1)
                pool.wait_ge(idx_ready, Q * j + q + 1)
                pool.wait_ge(out_taken[ch], n)
                stand_alone(pool, pool_passed)
                for t in range(NT):
                    g.indirect_dma_start(xg[ch][:, t, :], None, x2_d,
                                         bass.IndirectOffsetOnAxis(ap=idx[q][:, t:t + 1], axis=0),
                                         bounds_check=N_TOK - 1, oob_is_err=False).then_inc(gathered[ch], 16)
                pool.wait_ge(var[ch], n + 1)
                stand_alone(pool, pool_passed)
                e = steps.did(g.tensor_scalar(rs[ch][:, :], mv[ch][:, :, 1], EPS, None, ALU.add))
                steps.need(e)
                g.tensor_tensor(rs[ch][:, :], rs[ch][:, :], mhalf[:, :], ALU.pow).then_inc(rstd[ch], 1)

            def scatter(j, q):
                ch, p, n = turn(j, q)
                pool.wait_ge(out_taken[ch], n + 1)
                g.tensor_tensor(y[ch][:, :, :], y[ch][:, :, :], b2[p][:, :].unsqueeze(1).broadcast_to([P, NT, D]),
                                ALU.add).then_inc(y_ready[ch], 1)
                pool.wait_ge(y_ready[ch], n + 1)
                stand_alone(pool, pool_passed)
                for t in range(NT):
                    g.indirect_dma_start(x3_d, bass.IndirectOffsetOnAxis(ap=idx[q][:, t:t + 1], axis=0),
                                         y[ch][:, t, :], None, bounds_check=N_TOK - 1,
                                         oob_is_err=False).then_inc(scattered[ch], 16)

            def one_pass(j, last):
                steps.begin(j)
                for q in range(Q):
                    if not (last and q == Q - 1):
                        gather(*after(j, q))
                    scatter(j, q)

            gather(0, 0)
            one_pass(0, False)
            with pool.Fori(1, PASSES - 1) as j:
                one_pass(j, False)
            one_pass(PASSES - 1, True)
            for ch in range(2):
                pool.wait_ge(scattered[ch], 16 * NT * 2 * PASSES)

        @block.scalar
        def _(act):
            s = nc.scalar

            def take_xT(j, q):
                ch, p, n = turn(j, q)
                act.wait_ge(xT_psum[ch], n + 1)
                s.activation(xT[ch][:, 0, :], TB[0][:, :], ACT.Copy)
                s.activation(xT[ch][:, 1, :], TB[1][:, :], ACT.Copy).then_inc(xT_ready[ch], 1)

            def one_pass(j, last):
                for q in range(Q):
                    ch, p, n = turn(j, q)
                    if ch == 0:
                        act.wait_ge(w_loaded[p], 64 * (j + 1))
                        s.activation(b1r[p][:, :], b1[p][:, :], ACT.Copy, scale=RATIO).then_inc(b1_scaled[p], 1)
                        act.wait_ge(b1_scaled[p], j + 1)
                    for f in range(FC):
                        act.wait_ge(hidden_psum, (Q * j + q) * FC + f + 1)
                        s.activation(hT[ch][:, f, :], HB[f % 4][:, :], ACT.Gelu, bias=b1r[p][:, f:f + 1],
                                     scale=RATIO).then_inc(hidden_ready, 1)
                    if not (last and q == Q - 1):
                        take_xT(*after(j, q))

            take_xT(0, 0)
            one_pass(0, False)
            with act.Fori(1, PASSES - 1) as j:
                one_pass(j, False)
            one_pass(PASSES - 1, True)

        @block.vector
        def _(dve):
            v = nc.vector
            steps = Steps(dve, dve_step, NT * Q, NT)

            def norm(j, q):
                ch, p, n = turn(j, q)
                dve.wait_ge(gathered[ch], 16 * NT * (n + 1))
                done = [steps.did(v.bn_stats(st[ch][:, t, :], xg[ch][:, t, :])) for t in range(NT)]
                for t in range(NT):
                    steps.need(done[t])
                    stand_alone(dve, dve_passed)
                    last = v.bn_aggr(mv[ch][:, t, :], st[ch][:, t, :])
                last.then_inc(var[ch], 1)
                dve.wait_ge(rstd[ch], n + 1)
                for t in range(NT):
                    last = v.tensor_scalar(xn[ch][:, t, :], xg[ch][:, t, :], mv[ch][:, t, 0:1], rs[ch][:, t:t + 1],
                                           ALU.subtract, ALU.mult)
                last.then_inc(xn_ready[ch], 1)

            def residual(j, q):
                ch, p, n = turn(j, q)
                dve.wait_ge(out_psum[ch], n + 1)
                dve.wait_ge(scattered[ch], 16 * NT * n)
                for b in range(2):
                    last = v.scalar_tensor_tensor(y[ch][:, 2 * b:2 * b + 2, :],
                                                  OB[b][:, :].rearrange("p (t d) -> p t d", t=2), 1.0 / RATIO,
                                                  xg[ch][:, 2 * b:2 * b + 2, :], ALU.mult, ALU.add)
                last.then_inc(out_taken[ch], 1)

            def one_pass(j, last):
                steps.begin(j)
                for q in range(Q):
                    if not (last and q == Q - 1):
                        norm(*after(j, q))
                    residual(j, q)

            norm(0, 0)
            one_pass(0, False)
            with dve.Fori(1, PASSES - 1) as j:
                one_pass(j, False)
            one_pass(PASSES - 1, True)

        @block.tensor
        def _(pe):
            t_ = nc.tensor

            def transposes(j, q):
                ch, p, n = turn(j, q)
                pe.wait_ge(xn_ready[ch], n + 1)
                for c in range(C):
                    for t in range(NT):
                        last = t_.transpose(TB[c][:, t * P:(t + 1) * P], xn[ch][:, t, c * P:(c + 1) * P], ident[:, :])
                last.then_inc(xT_psum[ch], 1)

            def up(j, q):
                ch, p, n = turn(j, q)
                pe.wait_ge(xT_ready[ch], n + 1)
                if ch == 0:
                    pe.wait_ge(w_loaded[p], 64 * (j + 1))
                for f in range(FC):
                    if f >= 4:
                        pe.wait_ge(hidden_ready, (Q * j + q) * FC + f - 3)
                    for c in range(C):
                        last = t_.matmul(HB[f % 4][:, :], w1[p][:, c, f * P:(f + 1) * P], xT[ch][:, c, :],
                                         start=c == 0, stop=c == C - 1)
                    last.then_inc(hidden_psum, 1)

            def down(j, q):
                ch, p, n = turn(j, q)
                if ch == 0:
                    pe.wait_ge(out_taken[1], n)
                else:
                    pe.wait_ge(out_taken[0], n + 1)
                for t in range(NT):
                    for f in range(FC):
                        if t == 0:
                            pe.wait_ge(hidden_ready, (Q * j + q) * FC + f + 1)
                        last = t_.matmul(OB[t // 2][:, t % 2 * D:(t % 2 + 1) * D], hT[ch][:, f, t * P:(t + 1) * P],
                                         w2[p][:, f, :], start=f == 0, stop=f == FC - 1)
                last.then_inc(out_psum[ch], 1)

            def one_pass(j, last):
                for q in range(Q):
                    up(j, q)
                    if not (last and q == Q - 1):
                        transposes(*after(j, q))
                    down(j, q)

            pe.wait_ge(consts, 5)
            transposes(0, 0)
            one_pass(0, False)
            with pe.Fori(1, PASSES - 1) as j:
                one_pass(j, False)
            one_pass(PASSES - 1, True)


def phase_c(nc, a, x3_d, out):
    ctx_in = a["ctx_1024"]
    B, S, D = ctx_in.shape
    C, T = D // P, S // P
    DH = a["L1_attn_q_gamma"].shape[0]
    H = D // DH
    NE = a["L1_ffn_gate_w"].shape[1]
    PAIRS = B // 2
    HG = 4
    NG = H // HG
    SL = 4 * DH
    NB = H * SL // P
    with ExitStack() as ctx:
        sb = lambda name, shape, dt=F32: ctx.enter_context(nc.sbuf_tensor("c_" + name, shape, dt))
        sb2 = lambda name, shape, dt=F32: [sb(f"{name}{u}", shape, dt) for u in range(2)]
        sem = lambda name: nc.alloc_semaphore("c_" + name)
        sem2 = lambda name: [sem(f"{name}{u}") for u in range(2)]
        X = [ctx.enter_context(nc.psum_tensor(f"c_X{u}", [P, 512], F32)) for u in range(2)]
        Y = [ctx.enter_context(nc.psum_tensor(f"c_Y{u}", [P, 512], F32)) for u in range(2)]
        SR = [ctx.enter_context(nc.psum_tensor(f"c_S{n}", [P, 1024], F32)) for n in range(2)]
        halves = lambda bank: bank[:, 0:512].rearrange("p (c n) -> p c n", c=2)
        heads = lambda ring: ring[:, :].rearrange("p (h n) -> p h n", h=HG)
        place = lambda h: h % 2 * 2 + h % HG // 2

        ident = sb("ident", [P, P])
        identr = sb("identr", [P, P], F32R)
        ones = sb("ones", [P, 1])
        mhalf = sb("mhalf", [P, 2 * T * H])
        iota8 = sb("iota8", [P, NE])
        selh = sb("selh", [P, H, DH])
        wqkv = sb("wqkv", [P, C, 3 * D])
        wo = sb("wo", [P, C, D])
        wvx = sb("wvx", [P, C, D])
        wqk = sb("wqk", [P, C, D])
        g0 = sb("g0", [P, C])
        wr = sb("wr", [P, C])
        r0 = sb("r0", [P, 1])
        bvx = sb("bvx", [P, D])
        gam = sb("gam", [P, 2 * H, DH])
        bet = sb("bet", [P, 2 * H, DH])
        gw = sb("gw", [P, C, NE])
        gb = sb("gb", [P, NE])
        w1 = sb("w1", [P, NE, C, D])
        w2 = sb("w2", [P, NE, C, D])
        b1 = sb("b1", [P, NE, C])
        b2 = sb("b2", [NE, D])
        bqT, bkT = sb("bqT", [P, C]), sb("bkT", [P, C])

        q4 = sb("q4", [P, T, H, SL], F32R)
        k4 = sb("k4", [P, T, H, SL], F32R)
        PT = [sb(f"PT{n}", [P, T, HG, S]) for n in range(3)]
        sq = sb("sq", [P, T, 2 * H, DH])
        hid = [sb(f"hid{n}", [P, C, S]) for n in range(2)]

        x = sb2("x", [P, T, D])
        cx = sb2("cx", [P, T, D])
        cxT = sb2("cxT", [P, C, S])
        st = sb2("st", [P, T, 6])
        mv = sb2("mv", [P, T, 2])
        rs = sb2("rs", [P, T])
        xn = sb2("xn", [P, T, D])
        xnT = sb2("xnT", [P, C, S])
        qk = sb2("qk", [P, T, 2 * H, DH])
        hm = sb2("hm", [P, T * 2 * H])
        v32 = sb2("v32", [P, T, H, 2 * DH])
        q4T = sb2("q4T", [P, NB, S], F32R)
        k4T = sb2("k4T", [P, NB, S], F32R)
        nm = sb2("nm", [P, T, P])
        nmT = sb2("nmT", [P, S])
        rden = sb2("rden", [P, T, H])
        x4 = sb2("x4", [P, T, D])
        pe2 = sb2("pe2", [P, T, S + 1])
        m2 = sb2("m2", [P, T])
        nb2 = sb2("nb2", [P, T])
        r2 = sb2("r2", [P, T])
        den2 = sb2("den2", [P, T])
        rden2 = sb2("rden2", [P, T])
        peT = sb2("peT", [P, T, S])
        mix = sb2("mix", [P, T, D])
        x5 = sb2("x5", [P, T, D])
        lg = sb2("lg", [P, T, NE])
        mx = sb2("mx", [P, T, 8])
        ix = sb2("ix", [P, T, 8], U32)
        ixf = sb2("ixf", [P, T, 2])
        top = sb2("top", [P, T, NE])
        comb = sb2("comb", [P, T, NE])
        combT = sb2("combT", [NE, S])
        y = sb2("y", [P, T, D])
        oT = [t[:, :, :, :].rearrange("p t h d -> p (t h d)").rearrange("p (g s) -> p g s", g=NG) for t in qk]
        gT = [t[:, 0, :, :].rearrange("p h d -> p (h d)").rearrange("p (c s) -> p c s", c=C) for t in qk]
        gx = [t[:, 1, :, :].rearrange("p h d -> p (h d)").rearrange("p (c s) -> p c s", c=C) for t in qk]

        consts, w_in, dve_consts = sem("consts"), sem("w_in"), sem("dve_consts")
        pro_psum, pro_sb = sem("pro_psum"), sem("pro_sb")
        dve_front, dve_back = sem("dve_front"), sem("dve_back")
        pool_front, pool_back, squared = sem("pool_front"), sem("pool_back"), sem("squared")
        dve_passed, pool_passed = sem("dve_passed"), sem("pool_passed")
        x_loaded, cx_loaded, out_stored = sem2("x_loaded"), sem2("cx_loaded"), sem2("out_stored")
        var, rstd, xn_ready = sem2("var"), sem2("rstd"), sem2("xn_ready")
        xnT_psum, xnT_ready = sem2("xnT_psum"), sem2("xnT_ready")
        cxT_psum, cxT_ready = sem2("cxT_psum"), sem2("cxT_ready")
        qk_psum, qk_taken = sem2("qk_psum"), sem2("qk_taken")
        v_psum, v_ready = sem2("v_psum"), sem2("v_ready")
        hsum, hmean, centred, hvar, hrstd = sem2("hsum"), sem2("hmean"), sem2("centred"), sem2("hvar"), sem2("hrstd")
        scaled, qk_ready, high_ready, low_ready = sem2("scaled"), sem2("qk_ready"), sem2("high_ready"), sem2("low_ready")
        q4T_psum, k4T_psum = sem("q4T_psum"), sem("k4T_psum")
        q4T_taken, k4T_taken = sem("q4T_taken"), sem("k4T_taken")
        raw_psum, raw_taken = sem("raw_psum"), sem("raw_taken")
        nm_ready, nmT_psum, nmT_ready, shift_ready = sem2("nm_ready"), sem2("nmT_psum"), sem2("nmT_ready"), sem2("shift_ready")
        scores_psum, probs_ready, probs_used = sem("scores_psum"), sem("probs_ready"), sem("probs_used")
        oT_ready, o_psum, o_ready = sem2("oT_ready"), sem2("o_psum"), sem2("o_ready")
        o2T_psum, o2T_ready, proj_psum, x4_ready = sem2("o2T_psum"), sem2("o2T_ready"), sem2("proj_psum"), sem2("x4_ready")
        g_psum, g_ready, gx_ready = sem2("g_psum"), sem2("g_ready"), sem2("gx_ready")
        s2_psum, nb2_ready, p2_ready = sem2("s2_psum"), sem2("nb2_ready"), sem2("p2_ready")
        peT_psum, peT_ready, mix_psum, mix_ready = sem2("peT_psum"), sem2("peT_ready"), sem2("mix_psum"), sem2("mix_ready")
        mixT_psum, mixT_ready, cross_psum, x5_ready = sem2("mixT_psum"), sem2("mixT_ready"), sem2("cross_psum"), sem2("x5_ready")
        gates_psum, comb_ready, combT_psum, combT_ready = sem2("gates_psum"), sem2("comb_ready"), sem2("combT_psum"), sem2("combT_ready")
        bias_psum, y_ready = sem2("bias_psum"), sem2("y_ready")
        hid_psum, hid_ready, eo_psum, eo_taken = sem2("hid_psum"), sem2("hid_ready"), sem2("eo_psum"), sem2("eo_taken")

        rows = lambda t: t.rearrange("(i u t p) d -> i u p t d", u=2, t=T, p=P)
        x_rows, cx_rows, out_rows = rows(x3_d), rows(ctx_in.rearrange("b s d -> (b s) d")), rows(out.rearrange("b s d -> (b s) d"))
        by_chunk = lambda t: t.rearrange("(c p) n -> p c n", p=P)

        ORDER = (
            "f stats", "b o", "f norm", "b o2T", "f normT", "b proj", "f qk", "b norm2", "f v", "b norm2T",
            "f head sum", "f head mean", "b g", "f head var", "b scores", "f head scale", "b exp", "b expT",
            "b mix", "f split", "b mixT", "b cross", "f splitT", "b norm3", "f raw0", "f raw1", "b norm3T",
            "f raw2", "b gates", "f raw3", "f raw4", "b bias", "f raw5", "b expert0", "f raw6", "b expert1",
            "f raw7", "f shift", "b expert2", "b expert3", "f attend0", "b expert4", "f attend1", "b expert5",
            "f attend2", "b expert6", "f attend3", "b expert7", "f attend4", "b expert8")

        block = ctx.enter_context(nc.Block())

        @block.sync
        def _(sync):
            def load(u, i):
                sync.wait_ge(x4_ready[u], i)
                sync.dma_start(x[u][:, :, :], x_rows[i, u]).then_inc(x_loaded[u], 16)
                sync.wait_ge(mix_psum[u], i)
                sync.dma_start(cx[u][:, :, :], cx_rows[i, u]).then_inc(cx_loaded[u], 16)

            def store(u, i):
                sync.wait_ge(eo_taken[u], (i + 1) * NE)
                sync.dma_start(out_rows[i, u], y[u][:, :, :]).then_inc(out_stored[u], 16)

            def weight(dst, src, **kw):
                sync.dma_start(dst, src, **kw).then_inc(w_in, 16)

            load(0, 0)
            load(1, 0)
            col = dict(allow_slow_non_contiguous=True)
            weight(cxT[0][:, :, :], by_chunk(a["L1_xattn_Wq"]))
            weight(cxT[1][:, :, :], by_chunk(a["L1_xattn_Wk"]))
            weight(bqT[:, :], a["L1_xattn_bq"].rearrange("(c p) -> p c", p=P), **col)
            weight(bkT[:, :], a["L1_xattn_bk"].rearrange("(c p) -> p c", p=P), **col)
            weight(wqkv[:, :, :], by_chunk(a["L1_attn_w_qkv"]))
            weight(wo[:, :, :], by_chunk(a["L1_attn_w_proj"]))
            weight(wvx[:, :, :], by_chunk(a["L1_xattn_Wv"]))
            weight(bvx[:, :], a["L1_xattn_bv"].partition_broadcast(P))
            for n, name in enumerate("qk"):
                weight(gam[:, n * H, :], a[f"L1_attn_{name}_gamma"].partition_broadcast(P))
                weight(bet[:, n * H, :], a[f"L1_attn_{name}_beta"].partition_broadcast(P))
            weight(gw[:, :, :], by_chunk(a["L1_ffn_gate_w"]))
            weight(gb[:, :], a["L1_ffn_gate_b"].partition_broadcast(P))
            weight(w1[:, :, :, :], a["L1_ffn_w1"].rearrange("e (c p) n -> p e c n", p=P))
            weight(w2[:, :, :, :], a["L1_ffn_w2"].rearrange("e (c p) n -> p e c n", p=P))
            weight(b1[:, :, :], a["L1_ffn_b1"].rearrange("e (c p) -> p e c", p=P), **col)
            weight(b2[:, :], a["L1_ffn_b2"])
            with sync.Fori(0, PAIRS - 1) as i:
                for u in range(2):
                    load(u, i + 1)
                    store(u, i)
            store(0, PAIRS - 1)
            store(1, PAIRS - 1)
            for u in range(2):
                sync.wait_ge(out_stored[u], 16 * PAIRS)

        @block.gpsimd
        def _(pool):
            g = nc.gpsimd
            make_identity(nc, ident, consts, 0)
            g.memset(ones[:, :], 1.0).then_inc(consts, 1)
            g.memset(mhalf[:, :], -0.5).then_inc(consts, 1)
            g.iota(iota8[:, :], [[1, NE]], base=0, channel_multiplier=0,
                   allow_small_or_imprecise_dtypes=True).then_inc(consts, 1)
            g.memset(selh[:, :, :], 0.0).then_inc(consts, 1)
            pool.wait_ge(consts, 6)
            by_place = selh[:, :, :].rearrange("p (g a b) d -> p g a b d", a=2, b=2).rearrange("p g a b d -> p g a (b d)")
            for b in range(2):
                part = by_place[:, :, :, b * DH:(b + 1) * DH]
                g.affine_select(out=part, in_=part, compare_op=ALU.not_equal, fill=1.0, base=2 * b,
                                pattern=[[HG, NG], [1, 2], [-1, DH]], channel_multiplier=0).then_inc(consts, 1)
            for u in range(2):
                g.memset(v32[u][:, :, :, :], 0.0).then_inc(consts, 1)
                g.memset(nm[u][:, :, :], 0.0).then_inc(consts, 1)
            pool.wait_ge(consts, 12)
            for u in range(2):
                g.memset(v32[u][:, :, :, DH:DH + 1], 1.0).then_inc(consts, 1)
            pool.wait_ge(consts, 14)
            pool.wait_ge(w_in, 16 * 18)
            pool.wait_ge(dve_consts, 7)
            front, back = Steps(pool, pool_front, 4), Steps(pool, pool_back, 2)

            def row_rstd(steps, u, n):
                pool.wait_ge(var[u], n)
                stand_alone(pool, pool_passed)
                e = steps.did(g.tensor_scalar(rs[u][:, :], mv[u][:, :, 1], EPS, None, ALU.add))
                steps.need(e)
                g.tensor_tensor(rs[u][:, :], rs[u][:, :], mhalf[:, 0:T], ALU.pow).then_inc(rstd[u], 1)

            def head_mean(u, i):
                pool.wait_ge(hsum[u], i + 1)
                stand_alone(pool, pool_passed)
                g.tensor_scalar(hm[u][:, :], hm[u][:, :], 1.0 / DH, None, ALU.mult).then_inc(hmean[u], 1)

            def head_scale(u, i):
                pool.wait_ge(hvar[u], i + 1)
                stand_alone(pool, pool_passed)
                e = front.did(g.tensor_scalar(hm[u][:, :], hm[u][:, :], 1.0 / DH, EPS, ALU.mult, ALU.add))
                front.need(e)
                g.tensor_tensor(hm[u][:, :], hm[u][:, :], mhalf[:, :], ALU.pow).then_inc(hrstd[u], 1)
                pool.wait_ge(scaled[u], i + 1)
                m = [front.did(g.tensor_tensor(qk[u][:, t, :, :], qk[u][:, t, :, :], gam[:, :, :], ALU.mult))
                     for t in range(T)]
                for t in range(T):
                    front.need(m[t])
                    last = g.tensor_tensor(qk[u][:, t, :, :], qk[u][:, t, :, :], bet[:, :, :], ALU.add)
                last.then_inc(qk_ready[u], 1)

            def own_scores(u, i):
                pool.wait_ge(g_ready[u], i + 1)
                g.tensor_tensor(gx[u], gT[u], xnT[u][:, :, :], ALU.mult).then_inc(gx_ready[u], 1)

            skewed(pool, PAIRS, ORDER, {
                "f stats": lambda u, i: row_rstd(front, u, 3 * i + 1), "f head mean": head_mean,
                "f head scale": head_scale, "b norm2": lambda u, i: row_rstd(back, u, 3 * i + 2),
                "b g": own_scores, "b norm3": lambda u, i: row_rstd(back, u, 3 * i + 3),
            }, front, back)

        @block.scalar
        def _(act):
            s = nc.scalar
            act.wait_ge(pro_psum, 1)
            s.activation(xnT[0][:, :, :], halves(X[0]), ACT.Copy).then_inc(pro_sb, 1)
            s.activation(xnT[1][:, :, :], halves(X[1]), ACT.Copy).then_inc(pro_sb, 1)
            act.wait_ge(pro_psum, 2)
            s.activation(wqk[:, :, :], halves(X[0]), ACT.Copy).then_inc(pro_sb, 1)
            s.activation(g0[:, :], X[1][:, 0:C], ACT.Copy).then_inc(pro_sb, 1)
            s.activation(wr[:, :], X[1][:, C:2 * C], ACT.Copy).then_inc(pro_sb, 1)
            s.activation(r0[:, :], X[1][:, 2 * C:2 * C + 1], ACT.Copy).then_inc(pro_sb, 1)
            act.wait_ge(pro_sb, 6)
            act.wait_ge(w_in, 16 * 18)
            act.wait_ge(consts, 14)

            def take_xnT(u, n):
                act.wait_ge(xnT_psum[u], n)
                s.activation(xnT[u][:, :, :], halves(X[u]), ACT.Copy).then_inc(xnT_ready[u], 1)

            def normT(u, i):
                take_xnT(u, 3 * i + 1)
                act.wait_ge(cxT_psum[u], i + 1)
                s.activation(cxT[u][:, :, :], halves(Y[u]), ACT.Copy).then_inc(cxT_ready[u], 1)

            def take_qk(u, i):
                act.wait_ge(qk_psum[u], i + 1)
                for t, bank in enumerate((X[u], Y[u])):
                    last = s.activation(qk[u][:, t, :, :], bank[:, :].rearrange("p (h d) -> p h d", d=DH), ACT.Copy)
                last.then_inc(qk_taken[u], 1)

            def take_v(u, i):
                act.wait_ge(v_psum[u], i + 1)
                s.activation(v32[u][:, :, :, 0:DH], X[u][:, :].rearrange("p (t h d) -> p t h d", t=T, d=DH),
                             ACT.Copy).then_inc(v_ready[u], 1)

            def head_squares(u, i):
                act.wait_ge(centred[u], i + 1)
                act.wait_ge(hvar[1 - u], i + u)
                s.activation(sq[:, :, :, :], qk[u][:, :, :, :], ACT.Square).then_inc(squared, 1)

            def split(u, i):
                act.wait_ge(qk_ready[u], i + 1)
                act.wait_ge(k4T_psum, 4 * i + 2 * u)
                for t in range(T):
                    src = lambda n: qk[u][:, t, n * H:(n + 1) * H, :].unsqueeze(2).broadcast_to([P, H, 2, DH])
                    s.activation(q4[:, t, :, DH:3 * DH].rearrange("p h (r d) -> p h r d", r=2), src(0), ACT.Copy)
                    k = k4[:, t, :, :].rearrange("p h (r d) -> p h r d", d=DH)[:, :, 1:4:2, :]
                    last = s.activation(k, src(1), ACT.Copy)
                last.then_inc(high_ready[u], 1)

            def take_q4T(u, i):
                for t in range(T):
                    act.wait_ge(q4T_psum, 4 * i + 2 * u + t + 1)
                    s.activation(q4T[u][:, :, t * P:(t + 1) * P], SR[0][:, :].rearrange("p (b n) -> p b n", b=NB),
                                 ACT.Copy).then_inc(q4T_taken, 1)

            def shift(u, i):
                act.wait_ge(nmT_ready[u], i + 1)
                at = slice(SL, SL + H)
                s.activation(q4T[u][at, :, :], nmT[u][at, :].unsqueeze(1).broadcast_to([H, NB, S]), ACT.Copy)\
                    .then_inc(shift_ready[u], 1)

            def attend(g, u, i):
                if g < NG:
                    n = (2 * i + u) * NG + g
                    act.wait_ge(probs_used, n - 2 if u * NG + g >= 3 else 2 * i * NG)
                    for t in range(T):
                        act.wait_ge(scores_psum, n * T + t + 1)
                        s.activation(PT[(u * NG + g) % 3][:, t, :, :], heads(SR[t]), ACT.Exp,
                                     scale=float(DH) ** -0.5).then_inc(probs_ready, 1)
                else:
                    act.wait_ge(probs_used, (2 * i + u + 1) * NG)
                    for b, bank in enumerate((X[u], Y[u])):
                        last = s.activation(oT[u][:, 2 * b:2 * b + 2, :], halves(bank), ACT.Copy)
                    last.then_inc(oT_ready[u], 1)

            def take_o2T(u, i):
                act.wait_ge(o2T_psum[u], i + 1)
                s.activation(xnT[u][:, :, :], halves(X[u]), ACT.Copy).then_inc(o2T_ready[u], 1)

            def take_g(u, i):
                act.wait_ge(g_psum[u], i + 1)
                for c in range(C):
                    last = s.activation(gT[u][:, c, :], halves(Y[u])[:, c, :], ACT.Identity, bias=g0[:, c:c + 1])
                last.then_inc(g_ready[u], 1)

            def exps(u, i):
                act.wait_ge(nb2_ready[u], i + 1)
                for t, bank in enumerate((X[u], Y[u])):
                    last = s.activation(pe2[u][:, t, :], bank[:, 0:S + 1], ACT.Exp, bias=nb2[u][:, t:t + 1],
                                        accum_out=den2[u][:, t:t + 1])
                last.then_inc(p2_ready[u], 1)

            def take_mixT(u, i):
                act.wait_ge(mixT_psum[u], i + 1)
                s.activation(peT[u][:, :, :], halves(X[u]), ACT.Copy).then_inc(mixT_ready[u], 1)

            def take_combT(u, i):
                act.wait_ge(combT_psum[u], i + 1)
                s.activation(combT[u][:, :], Y[u][0:NE, P:P + S], ACT.Copy).then_inc(combT_ready[u], 1)

            def hidden(e, u, i):
                act.wait_ge(hid_psum[u], i * NE + e + 1)
                for c in range(C):
                    last = s.activation(hid[e % 2][:, c, :], halves(X[u])[:, c, :], ACT.Relu, bias=b1[:, e, c:c + 1])
                last.then_inc(hid_ready[u], 1)

            skewed(act, PAIRS, ORDER, {
                "f normT": normT, "f qk": take_qk, "f v": take_v, "f head mean": head_squares, "f split": split,
                "f splitT": take_q4T, "f shift": shift, "b o2T": take_o2T,
                "b norm2T": lambda u, i: take_xnT(u, 3 * i + 2), "b g": take_g, "b exp": exps, "b mixT": take_mixT,
                "b norm3T": lambda u, i: take_xnT(u, 3 * i + 3), "b bias": take_combT,
                **{f"f attend{g}": partial(attend, g) for g in range(NG + 1)},
                **{f"b expert{e}": partial(hidden, e) for e in range(NE)},
            })

        @block.vector
        def _(dve):
            v = nc.vector
            dve.wait_ge(w_in, 16 * 18)
            dve.wait_ge(consts, 14)
            v.tensor_copy(identr[:, :], ident[:, :]).then_inc(dve_consts, 1)
            for n in range(2):
                for tile in (gam, bet):
                    v.tensor_copy(tile[:, n * H + 1:(n + 1) * H, :],
                                  tile[:, n * H:n * H + 1, :].broadcast_to([P, H - 1, DH])).then_inc(dve_consts, 1)
            for t in range(T):
                v.tensor_copy(k4[:, t, :, 0:DH], selh[:, :, :])
                last = v.tensor_scalar(q4[:, t, :, 0:DH], selh[:, :, :], 0.0, None, ALU.mult)
            last.then_inc(dve_consts, 1)
            v.memset(hm[0][:, :], 0.0).then_inc(dve_consts, 1)
            front, back = Steps(dve, dve_front, 2), Steps(dve, dve_back, 25)

            def stats(steps, u, src):
                done = [steps.did(v.bn_stats(st[u][:, t, :], src[:, t, :])) for t in range(T)]
                for t in range(T):
                    steps.need(done[t])
                    stand_alone(dve, dve_passed)
                    last = v.bn_aggr(mv[u][:, t, :], st[u][:, t, :])
                last.then_inc(var[u], 1)

            def norm(u, src, n):
                dve.wait_ge(rstd[u], n)
                for t in range(T):
                    last = v.tensor_scalar(xn[u][:, t, :], src[:, t, :], mv[u][:, t, 0:1], rs[u][:, t:t + 1],
                                           ALU.subtract, ALU.mult)
                last.then_inc(xn_ready[u], 1)

            def first_stats(u, i):
                dve.wait_ge(x_loaded[u], 16 * i + 16)
                stats(front, u, x[u])

            q32 = [t[:, :, :, :].rearrange("p t h d -> p (t h) d") for t in qk]
            over_head = [t[:, :].unsqueeze(2).broadcast_to([P, T * 2 * H, DH]) for t in hm]

            def head_sum(u, i):
                dve.wait_ge(qk_taken[u], i + 1)
                v.tensor_reduce(hm[u][:, :], q32[u], AX.X, ALU.add).then_inc(hsum[u], 1)

            def head_mean(u, i):
                dve.wait_ge(hmean[u], i + 1)
                v.tensor_tensor(q32[u], q32[u], over_head[u], ALU.subtract).then_inc(centred[u], 1)

            def head_var(u, i):
                dve.wait_ge(squared, 2 * i + u + 1)
                v.tensor_reduce(hm[u][:, :], sq[:, :, :, :].rearrange("p t h d -> p (t h) d"), AX.X, ALU.add)\
                    .then_inc(hvar[u], 1)

            def head_scale(u, i):
                dve.wait_ge(hrstd[u], i + 1)
                v.tensor_tensor(q32[u], q32[u], over_head[u], ALU.mult).then_inc(scaled[u], 1)

            def split(u, i):
                dve.wait_ge(high_ready[u], i + 1)
                for t in range(T):
                    for n, (dst, at) in enumerate(((q4, 3 * DH), (k4, 2 * DH))):
                        last = v.tensor_tensor(dst[:, t, :, at:at + DH], qk[u][:, t, n * H:(n + 1) * H, :],
                                               dst[:, t, :, DH:2 * DH].bitcast(F32), ALU.subtract)
                last.then_inc(low_ready[u], 1)

            def take_k4T(u, i):
                for t in range(T):
                    dve.wait_ge(k4T_psum, 4 * i + 2 * u + t + 1)
                    v.tensor_copy(k4T[u][:, :, t * P:(t + 1) * P], SR[1][:, :].rearrange("p (b n) -> p b n", b=NB))\
                        .then_inc(k4T_taken, 1)

            def raw_max(f, u, i):
                t, g = f // NG, f % NG
                dve.wait_ge(raw_psum, (2 * i + u) * T * NG + f + 1)
                v.tensor_reduce(nm[u][:, t, g * HG:(g + 1) * HG], heads(SR[f % 2]), AX.X, ALU.max, negate=True)\
                    .then_inc(raw_taken, 1)

            def shift(u, i):
                dve.wait_ge(raw_taken, (2 * i + u + 1) * T * NG)
                v.tensor_copy(nm[u][:, :, SL:SL + H], nm[u][:, :, 0:H]).then_inc(nm_ready[u], 1)
                dve.wait_ge(nmT_psum[u], i + 1)
                v.tensor_copy(nmT[u][:, :], X[u][:, 0:S]).then_inc(nmT_ready[u], 1)
                dve.wait_ge(nmT_ready[u], i + 1)
                v.tensor_copy(q4T[u][0:H, :, :], nmT[u][0:H, :].unsqueeze(1).broadcast_to([H, NB, S]))\
                    .then_inc(shift_ready[u], 1)

            def take_o(u, i):
                dve.wait_ge(o_psum[u], i + 1)
                for t, bank in enumerate((X[u], Y[u])):
                    k = back.did(v.reciprocal(rden[u][:, t, :], bank[:, :].rearrange("p (h d) -> p h d", h=H)[:, :, DH]))
                back.need(k)
                for t, bank in enumerate((X[u], Y[u])):
                    o = bank[:, :].rearrange("p (h d) -> p h d", h=H)
                    last = v.tensor_tensor(xn[u][:, t, :].rearrange("p (h d) -> p h d", h=H), o[:, :, 0:DH],
                                           rden[u][:, t, :].unsqueeze(2).broadcast_to([P, H, DH]), ALU.mult)
                last.then_inc(o_ready[u], 1)

            def add_proj(u, i):
                dve.wait_ge(proj_psum[u], i + 1)
                v.tensor_tensor(x4[u][:, :, :], x[u][:, :, :], halves(Y[u]), ALU.add).then_inc(x4_ready[u], 1)
                dve.wait_ge(x4_ready[u], i + 1)
                stats(back, u, x4[u])

            def norm2(u, i):
                norm(u, x4[u], 3 * i + 2)
                dve.wait_ge(xn_ready[u], 3 * i + 2)
                back.did(v.tensor_tensor(x4[u][:, :, :], x4[u][:, :, :],
                                         bvx[:, :].unsqueeze(1).broadcast_to([P, T, D]), ALU.add))

            def score_max(u, i):
                dve.wait_ge(s2_psum[u], i + 1)
                for t, bank in enumerate((X[u], Y[u])):
                    back.did(v.tensor_reduce(m2[u][:, t:t + 1], bank[:, 0:S + 1], AX.X, ALU.max))
                    k = back.did(v.tensor_scalar(r2[u][:, t:t + 1], bank[:, S + 2:S + 3], r0[:, 0:1], None, ALU.add))
                back.need(k)
                k = back.did(v.tensor_tensor(m2[u][:, :], m2[u][:, :], r2[u][:, :], ALU.add))
                back.need(k)
                v.tensor_tensor(nb2[u][:, :], r2[u][:, :], m2[u][:, :], ALU.subtract).then_inc(nb2_ready[u], 1)

            def take_expT(u, i):
                dve.wait_ge(p2_ready[u], i + 1)
                for t in range(T):
                    back.did(v.tensor_scalar(mix[u][:, t, :], xn[u][:, t, :], pe2[u][:, t, S:S + 1], None, ALU.mult))
                back.did(v.reciprocal(rden2[u][:, :], den2[u][:, :]))
                dve.wait_ge(peT_psum[u], i + 1)
                v.tensor_copy(peT[u][:, :, :], halves(X[u])).then_inc(peT_ready[u], 1)

            def add_mix(u, i):
                dve.wait_ge(mix_psum[u], i + 1)
                back.need(back.n)
                v.tensor_tensor(mix[u][:, :, :], mix[u][:, :, :], halves(Y[u]), ALU.add).then_inc(mix_ready[u], 1)

            def add_cross(u, i):
                dve.wait_ge(cross_psum[u], i + 1)
                for t in range(T):
                    last = v.scalar_tensor_tensor(x5[u][:, t, :], halves(Y[u])[:, t, :], rden2[u][:, t:t + 1],
                                                  x4[u][:, t, :], ALU.mult, ALU.add)
                last.then_inc(x5_ready[u], 1)
                dve.wait_ge(x5_ready[u], i + 1)
                stats(back, u, x5[u])

            def gates(u, i):
                dve.wait_ge(gates_psum[u], i + 1)
                k = back.did(v.tensor_tensor(lg[u][:, :, :], Y[u][:, 0:T * NE].rearrange("p (t e) -> p t e", t=T),
                                             gb[:, :].unsqueeze(1).broadcast_to([P, T, NE]), ALU.add))
                back.need(k)
                stand_alone(dve, dve_passed)
                for t in range(T):
                    k = back.did(v.max(mx[u][:, t, :], lg[u][:, t, :]))
                back.need(k)
                stand_alone(dve, dve_passed)
                for t in range(T):
                    k = back.did(v.max_index(ix[u][:, t, :], mx[u][:, t, :], lg[u][:, t, :]))
                back.need(k)
                k = back.did(v.tensor_copy(ixf[u][:, :, :], ix[u][:, :, 0:2]))
                back.need(k)
                for t in range(T):
                    back.did(v.scalar_tensor_tensor(comb[u][:, t, :], iota8[:, :], ixf[u][:, t, 0:1],
                                                    lg[u][:, t, :], ALU.is_equal, ALU.mult))
                    k = back.did(v.scalar_tensor_tensor(top[u][:, t, :], iota8[:, :], ixf[u][:, t, 1:2],
                                                        lg[u][:, t, :], ALU.is_equal, ALU.mult))
                back.need(k)
                v.tensor_tensor(comb[u][:, :, :], comb[u][:, :, :], top[u][:, :, :], ALU.add).then_inc(comb_ready[u], 1)

            def add_bias(u, i):
                dve.wait_ge(bias_psum[u], i + 1)
                dve.wait_ge(out_stored[u], 16 * i)
                v.tensor_tensor(y[u][:, :, :], x5[u][:, :, :], halves(Y[u]), ALU.add).then_inc(y_ready[u], 1)

            def expert(e, u, i):
                if e == 0:
                    dve.wait_ge(y_ready[u], i + 1)
                else:
                    dve.wait_ge(eo_taken[u], i * NE + e)
                dve.wait_ge(eo_psum[u], i * NE + e + 1)
                for t in range(T):
                    last = v.scalar_tensor_tensor(y[u][:, t, :], halves(Y[u])[:, t, :], comb[u][:, t, e:e + 1],
                                                  y[u][:, t, :], ALU.mult, ALU.add)
                last.then_inc(eo_taken[u], 1)

            skewed(dve, PAIRS, ORDER, {
                "f stats": first_stats, "f norm": lambda u, i: norm(u, x[u], 3 * i + 1), "f head sum": head_sum,
                "f head mean": head_mean, "f head var": head_var, "f head scale": head_scale, "f split": split,
                "f splitT": take_k4T, "f shift": shift, "b o": take_o, "b proj": add_proj, "b norm2": norm2,
                "b scores": score_max, "b expT": take_expT, "b mix": add_mix, "b cross": add_cross,
                "b norm3": lambda u, i: norm(u, x5[u], 3 * i + 3), "b gates": gates, "b bias": add_bias,
                **{f"f raw{f}": partial(raw_max, f) for f in range(T * NG)},
                **{f"b expert{e + 1}": partial(expert, e) for e in range(NE)},
            }, front, back)

        @block.tensor
        def _(pe):
            t_ = nc.tensor

            def transposes(bank, src):
                for c in range(C):
                    for t in range(T):
                        last = t_.transpose(halves(bank)[:, c, t * P:(t + 1) * P], src[:, t, c * P:(c + 1) * P],
                                            ident[:, :])
                return last

            def project(bank, srcT, weight):
                for t in range(T):
                    for c in range(C):
                        last = t_.matmul(halves(bank)[:, t, :], srcT[:, c, t * P:(t + 1) * P], weight[:, c, :],
                                         start=c == 0, stop=c == C - 1)
                return last

            pe.wait_ge(consts, 14)
            pe.wait_ge(w_in, 16 * 18)
            pe.wait_ge(dve_consts, 7)
            transposes(X[0], cxT[0])
            transposes(X[1], cxT[1]).then_inc(pro_psum, 1)
            pe.wait_ge(pro_sb, 2)
            wqT, wkT = xnT
            for m in range(C):
                cols = slice(m * P, (m + 1) * P)
                for c in range(C):
                    t_.matmul(halves(X[0])[:, m, :], wqT[:, c, cols], wkT[:, c, :], start=c == 0, stop=c == C - 1)
                for c in range(C):
                    t_.matmul(X[1][:, m:m + 1], wkT[:, c, cols], bqT[:, c:c + 1], start=c == 0, stop=c == C - 1)
                for c in range(C):
                    t_.matmul(X[1][:, C + m:C + m + 1], wqT[:, c, cols], bkT[:, c:c + 1], start=c == 0, stop=c == C - 1)
            for c in range(C):
                last = t_.matmul(X[1][:, 2 * C:2 * C + 1], bqT[:, c:c + 1].broadcast_to([P, P]), bkT[:, c:c + 1],
                                 start=c == 0, stop=c == C - 1)
            last.then_inc(pro_psum, 1)
            pe.wait_ge(pro_sb, 6)

            def rowT(n, u, i):
                pe.wait_ge(xn_ready[u], 3 * i + n)
                transposes(X[u], xn[u]).then_inc(xnT_psum[u], 1)

            def normT(u, i):
                pe.wait_ge(eo_taken[u], i * NE)
                rowT(1, u, i)
                pe.wait_ge(cx_loaded[u], 16 * i + 16)
                transposes(Y[u], cx[u]).then_inc(cxT_psum[u], 1)

            def project_qk(u, i):
                pe.wait_ge(xnT_ready[u], 3 * i + 1)
                pe.wait_ge(cxT_ready[u], i + 1)
                for t, bank in enumerate((X[u], Y[u])):
                    for c in range(C):
                        last = t_.matmul(bank[:, :], xnT[u][:, c, t * P:(t + 1) * P], wqkv[:, c, 0:2 * D],
                                         start=c == 0, stop=c == C - 1)
                last.then_inc(qk_psum[u], 1)

            def project_v(u, i):
                pe.wait_ge(qk_taken[u], i + 1)
                project(X[u], xnT[u], wqkv[:, :, 2 * D:3 * D]).then_inc(v_psum[u], 1)

            def splitT(u, i):
                pe.wait_ge(low_ready[u], i + 1)
                for t in range(T):
                    for src, ring, full, taken in ((q4, SR[0], q4T_psum, q4T_taken), (k4, SR[1], k4T_psum, k4T_taken)):
                        pe.wait_ge(taken, 4 * i + 2 * u + t)
                        for b in range(NB):
                            last = t_.transpose(ring[:, b * P:(b + 1) * P].bitcast(F32R),
                                                src[:, t, 2 * b:2 * b + 2, :].rearrange("p h n -> p (h n)"),
                                                identr[:, :])
                        last.then_inc(full, 1)

            def raw(f, u, i):
                if f < 2:
                    pe.wait_ge(q4T_taken, 4 * i + 2 * u + 2)
                    pe.wait_ge(k4T_taken, 4 * i + 2 * u + 2)
                else:
                    pe.wait_ge(raw_taken, (2 * i + u) * T * NG + f - 1)
                t, g = f // NG, f % NG
                for h in range(g * HG, (g + 1) * HG):
                    at = slice(h % 2 * SL, h % 2 * SL + SL)
                    last = t_.matmul(heads(SR[f % 2])[:, place(h), :], q4T[u][at, h // 2, t * P:(t + 1) * P],
                                     k4T[u][at, h // 2, :], start=True, stop=True)
                last.then_inc(raw_psum, 1)

            def shiftT(u, i):
                pe.wait_ge(nm_ready[u], i + 1)
                pe.wait_ge(v_ready[u], i + 1)
                for t in range(T):
                    last = t_.transpose(X[u][:, t * P:(t + 1) * P], nm[u][:, t, :], ident[:, :])
                last.then_inc(nmT_psum[u], 1)

            def attend(g, u, i):
                n = (2 * i + u) * NG + g
                if g == 0:
                    pe.wait_ge(shift_ready[u], 2 * i + 2)
                    pe.wait_ge(raw_taken, (2 * i + u + 1) * T * NG)
                if g < NG:
                    for t in range(T):
                        if g:
                            pe.wait_ge(probs_ready, (n - 1) * T + t + 1)
                        for h in range(g * HG, (g + 1) * HG):
                            at = slice(h % 2 * SL, h % 2 * SL + SL)
                            last = t_.matmul(heads(SR[t])[:, place(h), :], k4T[u][at, h // 2, t * P:(t + 1) * P],
                                             q4T[u][at, h // 2, :], start=True, stop=True)
                        last.then_inc(scores_psum, 1)
                if g:
                    b = g - 1
                    pe.wait_ge(probs_ready, n * T)
                    bank = halves((X[u], Y[u])[b // 2])[:, b % 2, :]
                    for t in range(T):
                        for h in range(HG):
                            last = t_.matmul(bank[h * 2 * DH:(h + 1) * 2 * DH, :], v32[u][:, t, b * HG + h, :],
                                             PT[(u * NG + b) % 3][:, t, place(h), :], start=t == 0, stop=t == T - 1)
                    last.then_inc(probs_used, 1)

            def o(u, i):
                pe.wait_ge(oT_ready[u], i + 1)
                for t, bank in enumerate((X[u], Y[u])):
                    for g in range(NG):
                        last = t_.transpose(bank[:, g * P:(g + 1) * P], oT[u][:, g, t * P:(t + 1) * P], ident[:, :])
                last.then_inc(o_psum[u], 1)

            def o2T(u, i):
                pe.wait_ge(o_ready[u], i + 1)
                transposes(X[u], xn[u]).then_inc(o2T_psum[u], 1)

            def project_o(u, i):
                pe.wait_ge(o2T_ready[u], i + 1)
                project(Y[u], xnT[u], wo).then_inc(proj_psum[u], 1)

            def project_g(u, i):
                pe.wait_ge(xnT_ready[u], 3 * i + 2)
                for m in range(C):
                    for c in range(C):
                        last = t_.matmul(halves(Y[u])[:, m, :], wqk[:, c, m * P:(m + 1) * P], xnT[u][:, c, :],
                                         start=c == 0, stop=c == C - 1)
                last.then_inc(g_psum[u], 1)

            def cross_scores(u, i):
                pe.wait_ge(g_ready[u], i + 1)
                for part in range(3):
                    if part == 2:
                        pe.wait_ge(gx_ready[u], i + 1)
                    for t, bank in enumerate((X[u], Y[u])):
                        cols = slice(t * P, (t + 1) * P)
                        lhs, rhs, at = ((gT[u], lambda c: cxT[u][:, c, :], slice(0, S)),
                                        (xnT[u], lambda c: wr[:, c:c + 1], slice(S + 2, S + 3)),
                                        (gx[u], lambda c: ones[:, :], slice(S, S + 1)))[part]
                        for c in range(C):
                            last = t_.matmul(bank[:, at], lhs[:, c, cols], rhs(c), start=c == 0, stop=c == C - 1)
                last.then_inc(s2_psum[u], 1)

            def expT(u, i):
                pe.wait_ge(p2_ready[u], i + 1)
                transposes(X[u], pe2[u]).then_inc(peT_psum[u], 1)

            def mixed(u, i):
                pe.wait_ge(peT_ready[u], i + 1)
                project(Y[u], peT[u], cx[u]).then_inc(mix_psum[u], 1)

            def mixT(u, i):
                pe.wait_ge(mix_ready[u], i + 1)
                transposes(X[u], mix[u]).then_inc(mixT_psum[u], 1)

            def cross(u, i):
                pe.wait_ge(mixT_ready[u], i + 1)
                project(Y[u], peT[u], wvx).then_inc(cross_psum[u], 1)

            def gates(u, i):
                pe.wait_ge(xnT_ready[u], 3 * i + 3)
                for t in range(T):
                    for c in range(C):
                        last = t_.matmul(Y[u][:, t * NE:(t + 1) * NE], xnT[u][:, c, t * P:(t + 1) * P], gw[:, c, :],
                                         start=c == 0, stop=c == C - 1)
                last.then_inc(gates_psum[u], 1)

            def bias(u, i):
                pe.wait_ge(comb_ready[u], i + 1)
                for t in range(T):
                    last = t_.transpose(Y[u][0:NE, P + t * P:P + (t + 1) * P], comb[u][:, t, :], ident[:, :])
                last.then_inc(combT_psum[u], 1)
                pe.wait_ge(combT_ready[u], i + 1)
                for t in range(T):
                    last = t_.matmul(halves(Y[u])[:, t, :], combT[u][:, t * P:(t + 1) * P], b2[:, :], start=True, stop=True)
                last.then_inc(bias_psum[u], 1)

            def expert(e, u, i):
                if e:
                    pe.wait_ge(hid_ready[u], i * NE + e)
                if e < NE:
                    for m in range(C):
                        for c in range(C):
                            last = t_.matmul(halves(X[u])[:, m, :], w1[:, e, c, m * P:(m + 1) * P], xnT[u][:, c, :],
                                             start=c == 0, stop=c == C - 1)
                    last.then_inc(hid_psum[u], 1)
                if e:
                    if e == 1:
                        pe.wait_ge(y_ready[u], i + 1)
                    else:
                        pe.wait_ge(eo_taken[u], i * NE + e - 1)
                    for t in range(T):
                        for m in range(C):
                            last = t_.matmul(halves(Y[u])[:, t, :], hid[(e - 1) % 2][:, m, t * P:(t + 1) * P],
                                             w2[:, e - 1, m, :], start=m == 0, stop=m == C - 1)
                    last.then_inc(eo_psum[u], 1)

            skewed(pe, PAIRS, ORDER, {
                "f normT": normT, "f qk": project_qk, "f v": project_v, "f splitT": splitT, "f shift": shiftT,
                "b o": o, "b o2T": o2T, "b proj": project_o, "b norm2T": partial(rowT, 2), "b g": project_g,
                "b scores": cross_scores, "b expT": expT, "b mix": mixed, "b mixT": mixT, "b cross": cross,
                "b norm3T": partial(rowT, 3), "b gates": gates, "b bias": bias,
                **{f"f raw{f}": partial(raw, f) for f in range(T * NG)},
                **{f"f attend{g}": partial(attend, g) for g in range(NG + 1)},
                **{f"b expert{e}": partial(expert, e) for e in range(NE + 1)},
            })


_INS = [
    "x", "ctx_1024",
    *[f"L0_attn_{n}" for n in ("Wk", "bk", "gk", "betak", "Wq", "bq", "gq", "betaq", "Wv", "bv", "gv", "betav")],
    *[f"L0_ffn_{n}" for n in ("W_sw", "b_sw", "W1", "b1", "W2", "b2")],
    *[f"L1_attn_{n}" for n in ("w_qkv", "w_proj", "q_gamma", "q_beta", "k_gamma", "k_beta")],
    *[f"L1_xattn_{n}" for n in ("Wq", "bq", "Wk", "bk", "Wv", "bv")],
    *[f"L1_ffn_{n}" for n in ("gate_w", "gate_b", "w1", "b1", "w2", "b2")],
]


def decoder(nc, a, out):
    B, S, D = a["x"].shape
    x2_d = nc.dram_tensor("x2_scratch", (B * S, D), F32).ap()
    x3_d = nc.dram_tensor("x3_scratch", (B * S, D), F32).ap()
    table_d = nc.dram_tensor("slot_table", (B * S, 1), I32).ap()
    with nc.cleanup_on_exit():
        phase_a(nc, a, x2_d, x3_d, table_d)
    nc.all_engine_barrier()
    with nc.cleanup_on_exit():
        phase_b(nc, a, x2_d, x3_d, table_d)
    nc.all_engine_barrier()
    phase_c(nc, a, x3_d, out)


def kernel(**inputs):
    import numpy as _np
    import concourse.bacc as _bacc
    from concourse import mybir as _mybir
    from concourse.bass_utils import run_bass_kernel_spmd as _run

    nc = _bacc.Bacc("TRN2", target_bir_lowering=False, num_devices=1)
    arrays, args = {}, {}
    for name in _INS:
        arrays[f"in_{name}_dram"] = _np.ascontiguousarray(inputs[name])
        args[name] = nc.dram_tensor(f"in_{name}_dram", arrays[f"in_{name}_dram"].shape, _mybir.dt.float32,
                                    kind="ExternalInput").ap()
    out = nc.dram_tensor("out_0_dram", inputs["x"].shape, _mybir.dt.float32, kind="ExternalOutput").ap()
    decoder(nc, args, out)
    r = _run(nc, [arrays], core_ids=[0])
    return r.results[0]["out_0_dram"]
```

```python
from contextlib import ExitStack
from functools import partial

import concourse.bass as bass
from concourse import mybir

F32 = mybir.dt.float32
F32R = mybir.dt.float32r
I32 = mybir.dt.int32
U32 = mybir.dt.uint32
ALU = mybir.AluOpType
ACT = mybir.ActivationFunctionType
AX = mybir.AxisListType

P = 128
EPS = 1e-5


def skewed(eng, rounds, groups, order, parts, *steps):
    def beside(front, back, late):
        here = [None if where and isinstance(where[1], int) and where[1] < 0 else where
                for where in (front, back, late)]
        for n, where in enumerate(here):
            if where and n < len(steps):
                g, i = where
                steps[n].begin(2 * i + g)
        for part in order:
            where = here["fbm".index(part[0])]
            if where and part in parts:
                g, i = where
                for l in groups[g]:
                    parts[part](l, i)

    def one_round(i):
        beside((0, i), (1, i - 1), (0, i - 1))
        beside((1, i), (0, i), (1, i - 1))

    one_round(0)
    one_round(1)
    with eng.Fori(2, rounds) as i:
        one_round(i)
    beside(None, (1, rounds - 1), (0, rounds - 1))
    beside(None, None, (1, rounds - 1))


def stand_alone(eng, passed):
    eng.sem_inc(passed, 1)


class Steps:

    def __init__(self, eng, sem, each, before=0):
        self.eng, self.sem, self.each, self.before, self.base, self.n = eng, sem, each, before, 0, 0

    def begin(self, passes):
        assert self.n in (0, self.before, self.each), self.n
        self.base, self.n = self.before + self.each * passes, 0

    def did(self, ins):
        self.n += 1
        ins.then_inc(self.sem, 1)
        return self.n

    def need(self, n):
        self.eng.wait_ge(self.sem, self.base + n)


def make_identity(nc, tile, ready, before):
    nc.gpsimd.memset(tile[:, :], 0.0).then_inc(ready, 1)
    nc.gpsimd.wait_ge(ready, before + 1)
    nc.gpsimd.affine_select(out=tile[:, :], in_=tile[:, :], compare_op=ALU.not_equal, fill=1.0, base=0,
                            pattern=[[-1, P]], channel_multiplier=1).then_inc(ready, 1)


def phase_a(nc, a, x2_d, x3_d, table_d):
    x_in, ctx_in = a["x"], a["ctx_1024"]
    B, S, D = x_in.shape
    C, T = D // P, S // P
    NE = a["L0_ffn_W_sw"].shape[1]
    CAP = B * S // NE
    LANES = 4
    ROUNDS = B // LANES
    SLOTS = NE * CAP
    with ExitStack() as ctx:
        sb = lambda name, shape, dt=F32: ctx.enter_context(nc.sbuf_tensor("a_" + name, shape, dt))
        sb4 = lambda name, shape, dt=F32: [sb(f"{name}{l}", shape, dt) for l in range(LANES)]
        sem = lambda name: nc.alloc_semaphore("a_" + name)
        sem2 = lambda name: [sem(f"{name}{u}") for u in range(2)]
        sem4 = lambda name: [sem(f"{name}{l}") for l in range(LANES)]
        X, Y, V, Z = [[ctx.enter_context(nc.psum_tensor(f"a_{name}{u}", [P, 512], F32)) for u in range(2)]
                      for name in "XYVZ"]
        halves = lambda bank: bank[:, :].rearrange("p (c n) -> p c n", c=2)

        ident = sb("ident", [P, P])
        ones = sb("ones", [P, P])
        upto = sb("upto", [P, P])
        decay = sb("decay", [P, T, S])
        STEP = 16
        expo = sb("expo", [P, STEP + S // STEP + T])
        nine = sb("nine", [P, STEP + S // STEP + T])
        power = sb("power", [P, S // STEP, STEP])
        mhalf = sb("mhalf", [P, 6])
        iota8 = sb("iota8", [P, NE])
        empty = sb("empty", [P, SLOTS // P], I32)
        w = sb("w", [P, C, 3 * D])
        bias = sb("bias", [P, 3 * D])
        gqT, bqT = sb("gqT", [P, C]), sb("bqT", [P, C])
        gkT, bkT = sb("gkT", [P, C]), sb("bkT", [P, C])
        gv, bv = sb("gv", [P, D]), sb("bv", [P, D])
        wsw = sb("wsw", [P, C, NE])
        bsw = sb("bsw", [P, NE])
        carry = sb("carry", [P, NE])

        x = sb4("x", [P, T, D])
        cx = sb4("cx", [P, T, D])
        kv = sb4("kv", [P, T, D])
        st = sb4("st", [P, 6, 6])
        mv = sb4("mv", [P, 6, 2])
        rs = sb4("rs", [P, 6])
        xn = sb4("xn", [P, T, D])
        xnT = sb4("xnT", [P, C, S])
        qkv = sb4("qkv", [P, T, 3 * D])
        vn = sb4("vn", [P, T, D])
        qT = sb4("qT", [P, C, S])
        kT = sb4("kT", [P, C, S])
        nm = sb4("nm", [P, T])
        pr = sb4("pr", [P, T, S])
        prT = sb4("prT", [P, T, S])
        den = sb4("den", [P, T])
        rden = sb4("rden", [P, T])
        x1 = sb4("x1", [P, T, D])
        x1n = sb4("x1n", [P, T, D])
        x2 = sb4("x2", [P, T, D])
        x2n = sb4("x2n", [P, T, D])
        x2nT = sb4("x2nT", [P, C, S])
        x3 = sb4("x3", [P, T, D])
        lg = sb4("lg", [P, T, NE])
        mx = sb4("mx", [P, T, 8])
        ix = sb4("ix", [P, T, 8], U32)
        ixf = sb4("ixf", [P, T])
        oh = sb4("oh", [P, T, NE])
        rk = sb4("rk", [P, T, NE])
        pos = sb4("pos", [P, T])
        slot = sb4("slot", [P, T])
        over = sb4("over", [P, T])
        sloti = sb4("sloti", [P, T], I32)
        tok = sb4("tok", [P, T], I32)

        weights_in, rows_in, columns_in = sem("weights_in"), sem("rows_in"), sem("columns_in")
        consts = sem("consts")
        table_empty = sem("table_empty")
        x_in_s, cx_in_s = sem4("x_loaded"), sem4("ctx_loaded")
        dve_step, pool_step = sem("dve_step"), sem("pool_step")
        dve_step2, pool_step2 = sem("dve_step2"), sem("pool_step2")
        dve_passed, pool_passed = sem("dve_passed"), sem("pool_passed")
        var1, rstd1 = sem2("var1"), sem2("rstd1")
        xn_ready, xnT_psum, xnT_ready = sem2("xn_ready"), sem2("xnT_psum"), sem2("xnT_ready")
        qk_psum, qk_taken = sem2("qk_psum"), sem2("qk_taken")
        v_psum, qkv_taken = sem2("v_psum"), sem2("qkv_taken")
        var2, rstd2, qkvn_ready, v_ready = sem2("var2"), sem2("rstd2"), sem2("qkvn_ready"), sem2("v_ready")
        qkT_psum, qkT_ready = sem2("qkT_psum"), sem2("qkT_ready")
        scores_psum, max_ready, probs_ready = sem2("scores_psum"), sem2("max_ready"), sem2("probs_ready")
        kv_ready, sums_psum, sums_used = sem2("kv_ready"), sem2("sums_psum"), sem2("sums_used")
        prT_psum, prT_ready, att_psum = sem2("prT_psum"), sem2("prT_ready"), sem2("att_psum")
        residual_ready = sem2("residual_ready")
        x1_ready, var3, rstd3 = sem2("x1_ready"), sem2("var3"), sem2("rstd3")
        x2_ready, var4, rstd4, x2n_ready = sem2("x2_ready"), sem2("var4"), sem2("rstd4"), sem2("x2n_ready")
        x3_ready = sem2("x3_ready")
        x2nT_psum, x2nT_ready, logits_psum = sem2("x2nT_psum"), sem2("x2nT_ready"), sem2("logits_psum")
        onehot_ready, ranks_psum, slot_ready = sem2("onehot_ready"), sem2("ranks_psum"), sem2("slot_ready")
        x2_stored, x3_stored, filed = sem4("x2_stored"), sem4("x3_stored"), sem4("filed")

        rows = lambda t: t.rearrange("(i l t p) d -> i l p t d", l=LANES, t=T, p=P)
        x_rows = rows(x_in.rearrange("b s d -> (b s) d"))
        cx_rows = rows(ctx_in.rearrange("b s d -> (b s) d"))
        x2_rows, x3_rows = rows(x2_d), rows(x3_d)

        def place(l, i):
            return l % 2, 2 * i + l // 2

        def first(i):
            return isinstance(i, int) and i == 0

        def of_pair(j, back):
            return max(j + 1 - back, 0) if isinstance(j, int) else j + 1 - back

        ORDER = (
            "f norm", "b probsT", "b attend", "f normT", "f project", "f project v", "f project norm",
            "f scale v", "b sums", "f qkT", "b norm2", "f scores", "b normT", "f exp", "b logits", "b ranks")

        block = ctx.enter_context(nc.Block())

        @block.sync
        def _(sync):
            def load(l, i):
                u, j = place(l, i)
                sync.wait_ge(residual_ready[u], of_pair(j, 2))
                sync.dma_start(x[l][:, :, :], x_rows[i, l]).then_inc(x_in_s[l], 16)
                sync.wait_ge(kv_ready[u], of_pair(j, 2))
                sync.dma_start(cx[l][:, :, :], cx_rows[i, l]).then_inc(cx_in_s[l], 16)

            def store(l, i):
                u, j = place(l, i)
                sync.wait_ge(x2_ready[u], j + 1)
                sync.dma_start(x2_rows[i, l], x2[l][:, :, :]).then_inc(x2_stored[l], 16)
                sync.wait_ge(x3_ready[u], j + 1)
                sync.dma_start(x3_rows[i, l], x3[l][:, :, :]).then_inc(x3_stored[l], 16)

            load(0, 0)
            load(1, 0)
            for n, name in enumerate("qkv"):
                cols = slice(n * D, (n + 1) * D)
                sync.dma_start(w[:, :, cols], a[f"L0_attn_W{name}"].rearrange("(c p) n -> p c n", p=P))\
                    .then_inc(weights_in, 16)
                sync.dma_start(bias[:, cols], a[f"L0_attn_b{name}"].partition_broadcast(P)).then_inc(weights_in, 16)
            for tile, name in ((gv, "gv"), (bv, "betav")):
                sync.dma_start(tile[:, :], a[f"L0_attn_{name}"].partition_broadcast(P)).then_inc(rows_in, 16)
            sync.dma_start(wsw[:, :, :], a["L0_ffn_W_sw"].rearrange("(c p) n -> p c n", p=P)).then_inc(rows_in, 16)
            sync.dma_start(bsw[:, :], a["L0_ffn_b_sw"].partition_broadcast(P)).then_inc(rows_in, 16)
            sync.wait_ge(consts, 16)
            sync.dma_start(table_d.rearrange("(p n) o -> p (n o)", p=P), empty[:, :]).then_inc(table_empty, 16)
            load(2, 0)
            load(3, 0)
            with sync.Fori(0, ROUNDS - 1) as i:
                for pair in ((0, 1), (2, 3)):
                    for l in pair:
                        load(l, i + 1)
                    for l in pair:
                        store(l, i)
            for l in range(LANES):
                store(l, ROUNDS - 1)
            for l in range(LANES):
                sync.wait_ge(x2_stored[l], 16 * ROUNDS)
                sync.wait_ge(x3_stored[l], 16 * ROUNDS)

        @block.gpsimd
        def _(pool):
            g = nc.gpsimd
            make_identity(nc, ident, consts, 0)
            g.memset(ones[:, :], 1.0).then_inc(consts, 1)
            pool.wait_ge(consts, 3)
            g.affine_select(out=upto[:, :], in_=ones[:, :], compare_op=ALU.is_ge, fill=0.0, base=0,
                            pattern=[[1, P]], channel_multiplier=-1).then_inc(consts, 1)
            few = dict(allow_small_or_imprecise_dtypes=True)
            rest, multiple, minus = slice(0, STEP), slice(STEP, STEP + S // STEP), slice(STEP + S // STEP, None)
            g.iota(expo[:, rest], [[1, STEP]], base=0, channel_multiplier=0, **few).then_inc(consts, 1)
            g.iota(expo[:, multiple], [[STEP, S // STEP]], base=0, channel_multiplier=0, **few).then_inc(consts, 1)
            g.iota(expo[:, minus], [[-P, T]], base=0, channel_multiplier=-1, **few).then_inc(consts, 1)
            g.memset(nine[:, :], 0.9).then_inc(consts, 1)
            pool.wait_ge(consts, 8)
            g.tensor_tensor(expo[:, :], nine[:, :], expo[:, :], ALU.pow).then_inc(consts, 1)
            pool.wait_ge(consts, 9)
            g.tensor_tensor(power[:, :, :], expo[:, multiple].unsqueeze(2).broadcast_to([P, S // STEP, STEP]),
                            expo[:, rest].unsqueeze(1).broadcast_to([P, S // STEP, STEP]), ALU.mult)\
                .then_inc(consts, 1)
            pool.wait_ge(consts, 10)
            for c in range(T):
                g.tensor_scalar(decay[:, c, :], power[:, :, :].rearrange("p m r -> p (m r)"),
                                expo[:, STEP + S // STEP + c:STEP + S // STEP + c + 1], None, ALU.mult)\
                    .then_inc(consts, 1)
            pool.wait_ge(consts, 10 + T)
            g.affine_select(out=decay[:, :, :], in_=decay[:, :, :], compare_op=ALU.is_ge, fill=0.0, base=0,
                            pattern=[[-P, T], [1, S]], channel_multiplier=-1).then_inc(consts, 1)
            g.memset(mhalf[:, :], -0.5).then_inc(consts, 1)
            g.iota(iota8[:, :], [[1, NE]], base=0, channel_multiplier=0,
                   allow_small_or_imprecise_dtypes=True).then_inc(consts, 1)
            g.iota(empty[:, :], [[1, SLOTS // P]], base=8 * SLOTS, channel_multiplier=SLOTS // P).then_inc(consts, 1)
            g.memset(carry[:, :], 0.0).then_inc(consts, 1)
            for l in range(LANES):
                g.iota(tok[l][:, :], [[P, T]], base=(l - LANES) * S, channel_multiplier=1).then_inc(consts, 1)
            pool.wait_ge(consts, 17 + LANES)
            front, back = Steps(pool, pool_step, 2 * 4), Steps(pool, pool_step2, 2 * 3)

            def rstd(steps, l, i, n, var, out):
                u, j = place(l, i)
                pool.wait_ge(var[u], j + 1)
                stand_alone(pool, pool_passed)
                e = steps.did(g.tensor_scalar(rs[l][:, 0:n], mv[l][:, 0:n, 1], EPS, None, ALU.add))
                steps.need(e)
                g.tensor_tensor(rs[l][:, 0:n], rs[l][:, 0:n], mhalf[:, 0:n], ALU.pow).then_inc(out[u], 1)

            def scale_v(l, i):
                u, j = place(l, i)
                if first(i):
                    pool.wait_ge(rows_in, 16 * 4)
                pool.wait_ge(qkvn_ready[u], j + 1)
                pool.wait_ge(att_psum[u], of_pair(j, 2))
                m = [front.did(g.tensor_tensor(vn[l][:, t, :], qkv[l][:, t, 2 * D:3 * D], gv[:, :], ALU.mult))
                     for t in range(T)]
                for t in range(T):
                    front.need(m[t])
                    last = g.tensor_tensor(vn[l][:, t, :], vn[l][:, t, :], bv[:, :], ALU.add)
                last.then_inc(v_ready[u], 1)

            def residual(l, i):
                u, j = place(l, i)
                pool.wait_ge(xnT_psum[u], j + 1)
                g.tensor_tensor(xn[l][:, :, :], xn[l][:, :, :], x[l][:, :, :], ALU.add).then_inc(residual_ready[u], 1)

            def passed_by(l, i):
                u, j = place(l, i)
                pool.wait_ge(x2n_ready[u], j + 1)
                pool.wait_ge(x3_stored[l], 16 * i)
                g.tensor_tensor(x3[l][:, :, :], x2[l][:, :, :], x2n[l][:, :, :], ALU.add).then_inc(x3_ready[u], 1)

            def file_tokens(l, i):
                u, j = place(l, i)
                if first(i):
                    pool.wait_ge(table_empty, 16)
                pool.wait_ge(filed[l], 32 * i)
                stand_alone(pool, pool_passed)
                k = back.did(g.tensor_scalar(tok[l][:, :], tok[l][:, :], float(LANES * S), None, ALU.add))
                back.need(k)
                pool.wait_ge(slot_ready[u], j + 1)
                stand_alone(pool, pool_passed)
                for t in range(T):
                    g.indirect_dma_start(table_d, bass.IndirectOffsetOnAxis(ap=sloti[l][:, t:t + 1], axis=0),
                                         tok[l][:, t:t + 1], None, bounds_check=SLOTS - 1,
                                         oob_is_err=False).then_inc(filed[l], 16)

            skewed(pool, ROUNDS, ((0, 1), (2, 3)), ORDER, {
                "f norm": lambda l, i: rstd(front, l, i, T, var1, rstd1),
                "f project norm": lambda l, i: rstd(front, l, i, 3 * T, var2, rstd2), "f scale v": scale_v,
                "f qkT": residual,
                "b attend": lambda l, i: rstd(back, l, i, T, var3, rstd3),
                "b sums": lambda l, i: rstd(back, l, i, T, var4, rstd4), "b normT": passed_by,
                "b ranks": file_tokens,
            }, front, back)
            for l in range(LANES):
                pool.wait_ge(filed[l], 32 * ROUNDS)

        @block.scalar
        def _(act):
            s = nc.scalar
            for tile, name in ((gqT, "gq"), (bqT, "betaq"), (gkT, "gk"), (bkT, "betak")):
                act.dma_start(tile[:, :], a[f"L0_attn_{name}"].rearrange("(c p) -> p c", p=P),
                              allow_slow_non_contiguous=True).then_inc(columns_in, 16)

            def take_xnT(l, i):
                u, j = place(l, i)
                act.wait_ge(xnT_psum[u], j + 1)
                s.activation(xnT[l][:, :, :], halves(X[u]), ACT.Copy).then_inc(xnT_ready[u], 1)
                act.wait_ge(cx_in_s[l], 16 * i + 16)
                act.wait_ge(sums_psum[u], of_pair(j, 2))
                s.activation(kv[l][:, :, :], cx[l][:, :, :], ACT.Square).then_inc(kv_ready[u], 1)

            def take_qkT(l, i):
                u, j = place(l, i)
                if first(i):
                    act.wait_ge(columns_in, 16 * 4)
                act.wait_ge(qkT_psum[u], j + 1)
                for c in range(C):
                    s.activation(qT[l][:, c, :], halves(X[u])[:, c, :], ACT.Identity,
                                 bias=bqT[:, c:c + 1], scale=gqT[:, c:c + 1])
                    last = s.activation(kT[l][:, c, :], halves(Y[u])[:, c, :], ACT.Identity,
                                        bias=bkT[:, c:c + 1], scale=gkT[:, c:c + 1])
                last.then_inc(qkT_ready[u], 1)

            def exps(l, i):
                u, j = place(l, i)
                act.wait_ge(max_ready[u], j + 1)
                for t in range(T):
                    last = s.activation(pr[l][:, t, :], halves(X[u])[:, t, :], ACT.Exp, bias=nm[l][:, t:t + 1],
                                        accum_out=den[l][:, t:t + 1])
                last.then_inc(probs_ready[u], 1)

            def take_probsT(l, i):
                u, j = place(l, i)
                act.wait_ge(prT_psum[u], j + 1)
                s.activation(prT[l][:, :, :], halves(V[u]), ACT.Copy).then_inc(prT_ready[u], 1)

            def take_x2nT(l, i):
                u, j = place(l, i)
                act.wait_ge(x2nT_psum[u], j + 1)
                s.activation(x2nT[l][:, :, :], halves(Z[u]), ACT.Copy).then_inc(x2nT_ready[u], 1)

            skewed(act, ROUNDS, ((0, 1), (2, 3)), ORDER, {
                "f normT": take_xnT, "f qkT": take_qkT, "f exp": exps, "b probsT": take_probsT, "b normT": take_x2nT,
            })

        @block.vector
        def _(dve):
            v = nc.vector
            front, back = Steps(dve, dve_step, 2 * 8), Steps(dve, dve_step2, 2 * 18)

            def stats(steps, l, src, n, ready):
                done = [steps.did(v.bn_stats(st[l][:, k, :], src(k))) for k in range(n)]
                steps.need(done[n - 1])
                stand_alone(dve, dve_passed)
                for k in range(n):
                    last = v.bn_aggr(mv[l][:, k, :], st[l][:, k, :])
                last.then_inc(ready[l % 2], 1)

            def normalize(l, dst, src, k):
                return v.tensor_scalar(dst, src, mv[l][:, k, 0:1], rs[l][:, k:k + 1], ALU.subtract, ALU.mult)

            def norm(l, i):
                u, j = place(l, i)
                dve.wait_ge(x_in_s[l], 16 * i + 16)
                stats(front, l, lambda k: x[l][:, k, :], T, var1)
                dve.wait_ge(rstd1[u], j + 1)
                for t in range(T):
                    last = normalize(l, xn[l][:, t, :], x[l][:, t, :], t)
                last.then_inc(xn_ready[u], 1)

            def project(l, i):
                u, j = place(l, i)
                if first(i):
                    dve.wait_ge(weights_in, 16 * 6)
                dve.wait_ge(qk_psum[u], j + 1)
                for t, bank in enumerate((X[u], Y[u])):
                    last = v.tensor_tensor(qkv[l][:, t, 0:2 * D], bank[:, :], bias[:, 0:2 * D], ALU.add)
                last.then_inc(qk_taken[u], 1)

            def project_v(l, i):
                u, j = place(l, i)
                dve.wait_ge(v_psum[u], j + 1)
                v.tensor_tensor(qkv[l][:, :, 2 * D:3 * D], halves(X[u]),
                                bias[:, 2 * D:3 * D].unsqueeze(1).broadcast_to([P, T, D]), ALU.add)\
                    .then_inc(qkv_taken[u], 1)
                dve.wait_ge(qkv_taken[u], j + 1)
                stats(front, l, lambda k: qkv[l][:, k // 3, k % 3 * D:(k % 3 + 1) * D], 3 * T, var2)

            def project_norm(l, i):
                u, j = place(l, i)
                dve.wait_ge(rstd2[u], j + 1)
                for k in range(3 * T):
                    part = qkv[l][:, k // 3, k % 3 * D:(k % 3 + 1) * D]
                    last = normalize(l, part, part, k)
                last.then_inc(qkvn_ready[u], 1)

            def score_max(l, i):
                u, j = place(l, i)
                dve.wait_ge(scores_psum[u], j + 1)
                v.tensor_reduce(nm[l][:, :], halves(X[u]), AX.X, ALU.max, negate=True).then_inc(max_ready[u], 1)

            inverted = {}

            def invert(l, i):
                u, j = place(l, i)
                dve.wait_ge(probs_ready[u], j + 1)
                inverted[u] = back.did(v.reciprocal(rden[l][:, :], den[l][:, :]))

            def attend(l, i):
                u, j = place(l, i)
                dve.wait_ge(att_psum[u], j + 1)
                dve.wait_ge(residual_ready[u], j + 1)
                back.need(inverted[u])
                for t in range(T):
                    last = v.scalar_tensor_tensor(x1[l][:, t, :], halves(Z[u])[:, t, :], rden[l][:, t:t + 1],
                                                  xn[l][:, t, :], ALU.mult, ALU.add)
                last.then_inc(x1_ready[u], 1)
                dve.wait_ge(x1_ready[u], j + 1)
                stats(back, l, lambda k: x1[l][:, k, :], T, var3)

            def sums(l, i):
                u, j = place(l, i)
                dve.wait_ge(rstd3[u], j + 1)
                for t in range(T):
                    k = back.did(normalize(l, x1n[l][:, t, :], x1[l][:, t, :], t))
                dve.wait_ge(sums_psum[u], j + 1)
                back.need(k)
                v.tensor_tensor(x1n[l][:, :, :], x1n[l][:, :, :], halves(V[u]), ALU.mult).then_inc(sums_used[u], 1)
                dve.wait_ge(sums_used[u], j + 1)
                dve.wait_ge(x2_stored[l], 16 * i)
                dve.wait_ge(x3_ready[u], of_pair(j, 2))
                v.tensor_tensor(x2[l][:, :, :], x1[l][:, :, :], x1n[l][:, :, :], ALU.add).then_inc(x2_ready[u], 1)
                dve.wait_ge(x2_ready[u], j + 1)
                stats(back, l, lambda k: x2[l][:, k, :], T, var4)

            def norm2(l, i):
                u, j = place(l, i)
                dve.wait_ge(rstd4[u], j + 1)
                for t in range(T):
                    last = normalize(l, x2n[l][:, t, :], x2[l][:, t, :], t)
                last.then_inc(x2n_ready[u], 1)

            def route(l, i):
                u, j = place(l, i)
                if first(i):
                    dve.wait_ge(rows_in, 16 * 4)
                    dve.wait_ge(consts, 17 + LANES)
                dve.wait_ge(logits_psum[u], j + 1)
                lgp = V[u][:, 0:T * NE].rearrange("p (t e) -> p t e", t=T)
                k = back.did(v.tensor_tensor(lg[l][:, :, :], lgp, bsw[:, :].unsqueeze(1).broadcast_to([P, T, NE]),
                                             ALU.add))
                back.need(k)
                stand_alone(dve, dve_passed)
                for t in range(T):
                    k = back.did(v.max(mx[l][:, t, :], lg[l][:, t, :]))
                back.need(k)
                stand_alone(dve, dve_passed)
                for t in range(T):
                    k = back.did(v.max_index(ix[l][:, t, :], mx[l][:, t, :], lg[l][:, t, :]))
                back.need(k)
                k = back.did(v.tensor_copy(ixf[l][:, :], ix[l][:, :, 0]))
                back.need(k)
                for t in range(T):
                    last = v.tensor_scalar(oh[l][:, t, :], iota8[:, :], ixf[l][:, t:t + 1], None, ALU.is_equal)
                last.then_inc(onehot_ready[u], 1)

            def queue(l, i):
                u, j = place(l, i)
                dve.wait_ge(ranks_psum[u], j + 1)
                rkp = V[u][:, 64:64 + T * NE].rearrange("p (t e) -> p t e", t=T)
                k = back.did(v.tensor_tensor(rk[l][:, :, :], rkp, carry[:, :].unsqueeze(1).broadcast_to([P, T, NE]),
                                             ALU.add))
                back.need(k)
                c = back.did(v.tensor_tensor(carry[:, :], carry[:, :], V[u][:, 128:128 + NE], ALU.add))
                back.need(c)
                k = back.did(v.tensor_tensor(rk[l][:, :, :], rk[l][:, :, :], oh[l][:, :, :], ALU.mult))
                back.need(k)
                k = back.did(v.tensor_reduce(pos[l][:, :], rk[l][:, :, :], AX.X, ALU.add))
                back.need(k)
                v.tensor_scalar(over[l][:, :], pos[l][:, :], float(CAP), float(8 * SLOTS), ALU.is_gt, ALU.mult)
                k = back.did(v.scalar_tensor_tensor(slot[l][:, :], ixf[l][:, :], float(CAP), pos[l][:, :],
                                                    ALU.mult, ALU.add))
                back.need(k)
                dve.wait_ge(filed[l], 32 * i)
                v.scalar_tensor_tensor(sloti[l][:, :], slot[l][:, :], -1.0, over[l][:, :],
                                       ALU.add, ALU.add).then_inc(slot_ready[u], 1)

            skewed(dve, ROUNDS, ((0, 1), (2, 3)), ORDER, {
                "f norm": norm, "f project": project, "f project v": project_v, "f project norm": project_norm,
                "f scores": score_max,
                "b probsT": invert, "b attend": attend, "b sums": sums, "b norm2": norm2, "b logits": route,
                "b ranks": queue,
            }, front, back)

        @block.tensor
        def _(pe):
            t_ = nc.tensor

            def transposes(bank, src, done):
                for c in range(C):
                    for t in range(T):
                        last = t_.transpose(halves(bank)[:, c, t * P:(t + 1) * P], src[:, t, c * P:(c + 1) * P],
                                            ident[:, :])
                if done is not None:
                    last.then_inc(done, 1)

            def normT(l, i):
                u, j = place(l, i)
                if first(i):
                    pe.wait_ge(consts, 2)
                pe.wait_ge(xn_ready[u], j + 1)
                pe.wait_ge(probs_ready[u], j)
                transposes(X[u], xn[l], xnT_psum[u])

            def project(l, i):
                u, j = place(l, i)
                if first(i):
                    pe.wait_ge(weights_in, 16 * 6)
                pe.wait_ge(xnT_ready[u], j + 1)
                for t, bank in enumerate((X[u], Y[u])):
                    for c in range(C):
                        last = t_.matmul(bank[:, :], xnT[l][:, c, t * P:(t + 1) * P], w[:, c, 0:2 * D], start=c == 0,
                                         stop=c == C - 1)
                last.then_inc(qk_psum[u], 1)

            def project_v(l, i):
                u, j = place(l, i)
                pe.wait_ge(qk_taken[u], j + 1)
                for t in range(T):
                    for c in range(C):
                        last = t_.matmul(halves(X[u])[:, t, :], xnT[l][:, c, t * P:(t + 1) * P],
                                         w[:, c, 2 * D:3 * D], start=c == 0, stop=c == C - 1)
                last.then_inc(v_psum[u], 1)

            def qkT(l, i):
                u, j = place(l, i)
                pe.wait_ge(qkvn_ready[u], j + 1)
                transposes(X[u], qkv[l][:, :, 0:D], None)
                transposes(Y[u], qkv[l][:, :, D:2 * D], qkT_psum[u])

            def scores(l, i):
                u, j = place(l, i)
                pe.wait_ge(qkT_ready[u], j + 1)
                for t in range(T):
                    for c in range(C):
                        last = t_.matmul(halves(X[u])[:, t, :], kT[l][:, c, t * P:(t + 1) * P], qT[l][:, c, :],
                                         start=c == 0, stop=c == C - 1)
                last.then_inc(scores_psum[u], 1)

            def probsT(l, i):
                u, j = place(l, i)
                pe.wait_ge(probs_ready[u], j + 1)
                pe.wait_ge(slot_ready[u], j)
                transposes(V[u], pr[l], prT_psum[u])

            def sums(l, i):
                u, j = place(l, i)
                pe.wait_ge(prT_ready[u], j + 1)
                if first(i):
                    pe.wait_ge(consts, 17 + LANES)
                pe.wait_ge(kv_ready[u], j + 1)
                t_.matmul(halves(V[u])[:, 0, :], decay[:, 0, 0:P], kv[l][:, 0, :], start=True, stop=True)
                t_.matmul(halves(V[u])[:, 1, :], decay[:, 0, P:2 * P], kv[l][:, 0, :], start=True, stop=False)
                t_.matmul(halves(V[u])[:, 1, :], decay[:, 1, P:2 * P], kv[l][:, 1, :], start=False, stop=True)\
                    .then_inc(sums_psum[u], 1)

            def attend(l, i):
                u, j = place(l, i)
                pe.wait_ge(prT_ready[u], j + 1)
                pe.wait_ge(v_ready[u], j + 1)
                for t in range(T):
                    for c in range(T):
                        last = t_.matmul(halves(Z[u])[:, t, :], prT[l][:, c, t * P:(t + 1) * P], vn[l][:, c, :],
                                         start=c == 0, stop=c == T - 1)
                last.then_inc(att_psum[u], 1)

            def norm2T(l, i):
                u, j = place(l, i)
                pe.wait_ge(x2n_ready[u], j + 1)
                transposes(Z[u], x2n[l], x2nT_psum[u])

            def logits(l, i):
                u, j = place(l, i)
                if first(i):
                    pe.wait_ge(rows_in, 16 * 4)
                pe.wait_ge(x2nT_ready[u], j + 1)
                for t in range(T):
                    for c in range(C):
                        last = t_.matmul(V[u][:, t * NE:(t + 1) * NE], x2nT[l][:, c, t * P:(t + 1) * P],
                                         wsw[:, c, :], start=c == 0, stop=c == C - 1)
                last.then_inc(logits_psum[u], 1)

            def ranks(l, i):
                u, j = place(l, i)
                pe.wait_ge(onehot_ready[u], j + 1)
                t_.matmul(V[u][:, 64:64 + NE], upto[:, :], oh[l][:, 0, :], start=True, stop=True)
                t_.matmul(V[u][:, 64 + NE:64 + 2 * NE], ones[:, :], oh[l][:, 0, :], start=True, stop=False)
                t_.matmul(V[u][:, 64 + NE:64 + 2 * NE], upto[:, :], oh[l][:, 1, :], start=False, stop=True)
                t_.matmul(V[u][:, 128:128 + NE], ones[:, :], oh[l][:, 0, :], start=True, stop=False)
                t_.matmul(V[u][:, 128:128 + NE], ones[:, :], oh[l][:, 1, :], start=False, stop=True)\
                    .then_inc(ranks_psum[u], 1)

            skewed(pe, ROUNDS, ((0, 1), (2, 3)), ORDER, {
                "f normT": normT, "f project": project, "f project v": project_v, "b sums": sums, "f qkT": qkT,
                "f scores": scores, "b probsT": probsT,
                "b attend": attend, "b normT": norm2T, "b logits": logits, "b ranks": ranks,
            })


def phase_b(nc, a, x2_d, x3_d, table_d, next_weights):
    NE, D, F = a["L0_ffn_W1"].shape
    SLOTS = table_d.shape[0]
    N_TOK = x2_d.shape[0]
    CAP = SLOTS // NE
    NT = 4
    N = NT * P
    C, FC = D // P, F // P
    Q = 4
    PASSES = SLOTS // N // Q
    RATIO = 2.0 ** 0.5 / 1.41421
    assert CAP == 2 * N
    with ExitStack() as ctx:
        sb = lambda name, shape, dt=F32: ctx.enter_context(nc.sbuf_tensor("b_" + name, shape, dt))
        sb2 = lambda name, shape, dt=F32: [sb(f"{name}{u}", shape, dt) for u in range(2)]
        sem = lambda name: nc.alloc_semaphore("b_" + name)
        sem2 = lambda name: [sem(f"{name}{u}") for u in range(2)]
        TB = [ctx.enter_context(nc.psum_tensor(f"b_T{n}", [P, 512], F32)) for n in range(2)]
        HB = [ctx.enter_context(nc.psum_tensor(f"b_H{n}", [P, 512], F32)) for n in range(4)]
        OB = [ctx.enter_context(nc.psum_tensor(f"b_O{n}", [P, 512], F32)) for n in range(2)]

        ident = sb("ident", [P, P])
        mhalf = sb("mhalf", [P, NT])
        idx_all = sb("idx_all", [P, SLOTS // N, NT], I32)
        idx = [sb(f"idx{q}", [P, NT], I32) for q in range(Q)]
        w1 = sb2("w1_", [P, C, F])
        w2 = sb2("w2_", [P, FC, D])
        b1 = sb2("b1_", [P, FC])
        b1r = sb2("b1r_", [P, FC])
        b2 = sb2("b2_", [P, D])
        xg = [sb(f"xg{q}", [P, NT, D]) for q in range(Q)]
        st = sb2("st", [P, NT, 6])
        mv = sb2("mv", [P, NT, 2])
        rs = sb2("rs", [P, NT])
        xn = sb2("xn", [P, NT, D])
        w1h, w1l = sb2("w1h", [P, C, F], F32R), sb2("w1l", [P, C, F], F32R)
        xTh, xTl = sb2("xTh", [P, C, N], F32R), sb2("xTl", [P, C, N], F32R)
        hT = sb2("hT", [P, FC, N])
        y = sb2("y", [P, NT, D])

        consts, table_in = sem("consts"), sem("table_in")
        w_loaded = sem2("w_loaded")
        gathered, scattered = sem2("gathered"), sem2("scattered")
        dve_step, pool_step, act_step = sem("dve_step"), sem("pool_step"), sem("act_step")
        dve_passed, pool_passed = sem("dve_passed"), sem("pool_passed")
        idx_ready = sem("idx_ready")
        var, rstd, xn_ready = sem2("var"), sem2("rstd"), sem2("xn_ready")
        xT_psum, xT_ready = sem2("xT_psum"), sem2("xT_ready")
        hidden_psum, hidden_ready = sem("hidden_psum"), sem("hidden_ready")
        out_psum, out_taken, y_ready = sem2("out_psum"), sem2("out_taken"), sem2("y_ready")
        b1_scaled, w1_high, w1_split = sem2("b1_scaled"), sem2("w1_high"), sem2("w1_split")
        xT_high = sem2("xT_high")

        block = ctx.enter_context(nc.Block())

        w1_v = a["L0_ffn_W1"].rearrange("(j q) (c p) f -> j q p c f", q=2, p=P)
        w2_v = a["L0_ffn_W2"].rearrange("(j q) (c p) f -> j q p c f", q=2, p=P)
        b1_v = a["L0_ffn_b1"].rearrange("(j q) (c p) -> j q p c", q=2, p=P)
        b2_v = a["L0_ffn_b2"].rearrange("(j q) d -> j q d", q=2)

        def turn(j, q):
            return q % 2, q // 2, 2 * j + q // 2

        def after(j, q):
            return (j, q + 1) if q + 1 < Q else (j + 1, 0)

        @block.sync
        def _(sync):
            def weights(j, p):
                sync.dma_start(w1[p][:, :, :], w1_v[j, p]).then_inc(w_loaded[p], 16)
                sync.dma_start(w2[p][:, :, :], w2_v[j, p]).then_inc(w_loaded[p], 16)
                sync.dma_start(b1[p][:, :], b1_v[j, p], allow_slow_non_contiguous=True).then_inc(w_loaded[p], 16)
                sync.dma_start(b2[p][:, :], b2_v[j, p].partition_broadcast(P)).then_inc(w_loaded[p], 16)

            sync.dma_start(idx_all[:, :, :], table_d.rearrange("(k p t) o -> p k (t o)", p=P, t=NT)).then_inc(table_in, 16)
            weights(0, 0)
            weights(0, 1)
            next_weights.load(sync)
            with sync.Fori(1, PASSES) as j:
                for p in range(2):
                    sync.wait_ge(y_ready[1], 2 * j + (p - 1))
                    weights(j, p)

        @block.gpsimd
        def _(pool):
            g = nc.gpsimd
            make_identity(nc, ident, consts, 0)
            g.memset(mhalf[:, :], -0.5).then_inc(consts, 1)
            for tile in xg:
                g.memset(tile[:, :, :], 0.0).then_inc(consts, 1)
            pool.wait_ge(consts, 3 + Q)
            pool.wait_ge(table_in, 16)
            steps = Steps(pool, pool_step, Q, 1)

            def gather(j, q):
                ch, p, n = turn(j, q)
                if not isinstance(j, int) or j > 0:
                    pool.wait_ge(scattered[ch], 16 * NT * (n - 1))
                    pool.wait_ge(out_taken[ch], n - 1)
                    stand_alone(pool, pool_passed)
                g.tensor_copy(idx[q][:, :], idx_all[:, bass.ds(Q * j + q, 1), :].rearrange("p k t -> p (k t)"))\
                    .then_inc(idx_ready, 1)
                pool.wait_ge(idx_ready, Q * j + q + 1)
                stand_alone(pool, pool_passed)
                for t in range(NT):
                    g.indirect_dma_start(xg[q][:, t, :], None, x2_d,
                                         bass.IndirectOffsetOnAxis(ap=idx[q][:, t:t + 1], axis=0),
                                         bounds_check=N_TOK - 1, oob_is_err=False).then_inc(gathered[ch], 16)

            def row_rstd(j, q):
                ch, p, n = turn(j, q)
                pool.wait_ge(var[ch], n + 1)
                stand_alone(pool, pool_passed)
                e = steps.did(g.tensor_scalar(rs[ch][:, :], mv[ch][:, :, 1], EPS, None, ALU.add))
                steps.need(e)
                g.tensor_tensor(rs[ch][:, :], rs[ch][:, :], mhalf[:, :], ALU.pow).then_inc(rstd[ch], 1)

            def scatter(j, q):
                ch, p, n = turn(j, q)
                pool.wait_ge(y_ready[ch], n + 1)
                stand_alone(pool, pool_passed)
                for t in range(NT):
                    g.indirect_dma_start(x3_d, bass.IndirectOffsetOnAxis(ap=idx[q][:, t:t + 1], axis=0),
                                         y[ch][:, t, :], None, bounds_check=N_TOK - 1,
                                         oob_is_err=False).then_inc(scattered[ch], 16)

            def one_pass(j, last):
                steps.begin(j)
                for q in range(Q):
                    if not (last and q >= Q - 2):
                        gather(*after(*after(j, q)))
                    if not (last and q == Q - 1):
                        row_rstd(*after(j, q))
                    scatter(j, q)

            gather(0, 0)
            gather(0, 1)
            row_rstd(0, 0)
            one_pass(0, False)
            with pool.Fori(1, PASSES - 1) as j:
                one_pass(j, False)
            one_pass(PASSES - 1, True)
            for ch in range(2):
                pool.wait_ge(scattered[ch], 16 * NT * 2 * PASSES)

        @block.scalar
        def _(act):
            s = nc.scalar

            def high_parts(j, q):
                ch, p, n = turn(j, q)
                if ch == 0:
                    act.wait_ge(w_loaded[p], 64 * (j + 1))
                    s.activation(w1h[p][:, :, :], w1[p][:, :, :], ACT.Copy).then_inc(w1_high[p], 1)
                act.wait_ge(xT_psum[ch], n + 1)
                s.activation(xTh[ch][:, 0, :], TB[0][:, :], ACT.Copy)
                s.activation(xTh[ch][:, 1, :], TB[1][:, :], ACT.Copy).then_inc(xT_high[ch], 1)

            def one_pass(j, last):
                for q in range(Q):
                    ch, p, n = turn(j, q)
                    if ch == 0:
                        act.wait_ge(w_loaded[p], 64 * (j + 1))
                        s.activation(b1r[p][:, :], b1[p][:, :], ACT.Copy, scale=RATIO).then_inc(b1_scaled[p], 1)
                        act.wait_ge(b1_scaled[p], j + 1)
                    for f in range(FC):
                        act.wait_ge(hidden_psum, (Q * j + q) * FC + f + 1)
                        s.activation(hT[ch][:, f, :], HB[f % 4][:, :], ACT.Gelu, bias=b1r[p][:, f:f + 1],
                                     scale=RATIO).then_inc(hidden_ready, 1)
                    if not (last and q == Q - 1):
                        high_parts(*after(j, q))

            high_parts(0, 0)
            one_pass(0, False)
            with act.Fori(1, PASSES - 1) as j:
                one_pass(j, False)
            one_pass(PASSES - 1, True)

        @block.vector
        def _(dve):
            v = nc.vector
            steps = Steps(dve, dve_step, NT * Q, NT)

            def norm(j, q):
                ch, p, n = turn(j, q)
                dve.wait_ge(gathered[ch], 16 * NT * (n + 1))
                done = [steps.did(v.bn_stats(st[ch][:, t, :], xg[q][:, t, :])) for t in range(NT)]
                for t in range(NT):
                    steps.need(done[t])
                    stand_alone(dve, dve_passed)
                    last = v.bn_aggr(mv[ch][:, t, :], st[ch][:, t, :])
                last.then_inc(var[ch], 1)
                dve.wait_ge(rstd[ch], n + 1)
                for t in range(NT):
                    last = v.tensor_scalar(xn[ch][:, t, :], xg[q][:, t, :], mv[ch][:, t, 0:1], rs[ch][:, t:t + 1],
                                           ALU.subtract, ALU.mult)
                last.then_inc(xn_ready[ch], 1)

            def low_parts(j, q):
                ch, p, n = turn(j, q)
                if ch == 0:
                    dve.wait_ge(w1_high[p], j + 1)
                    v.tensor_tensor(w1l[p][:, :, :], w1[p][:, :, :], w1h[p][:, :, :].bitcast(F32), ALU.subtract)\
                        .then_inc(w1_split[p], 1)
                dve.wait_ge(xT_high[ch], n + 1)
                v.tensor_tensor(xTl[ch][:, 0, :], TB[0][:, :], xTh[ch][:, 0, :].bitcast(F32), ALU.subtract)
                v.tensor_tensor(xTl[ch][:, 1, :], TB[1][:, :], xTh[ch][:, 1, :].bitcast(F32), ALU.subtract)\
                    .then_inc(xT_ready[ch], 1)

            def residual(j, q):
                ch, p, n = turn(j, q)
                dve.wait_ge(out_psum[ch], n + 1)
                dve.wait_ge(scattered[ch], 16 * NT * n)
                for b in range(2):
                    last = v.scalar_tensor_tensor(y[ch][:, 2 * b:2 * b + 2, :],
                                                  OB[b][:, :].rearrange("p (t d) -> p t d", t=2), 1.0 / RATIO,
                                                  xg[q][:, 2 * b:2 * b + 2, :], ALU.mult, ALU.add)
                last.then_inc(out_taken[ch], 1)
                dve.wait_ge(out_taken[ch], n + 1)
                v.tensor_tensor(y[ch][:, :, :], y[ch][:, :, :], b2[p][:, :].unsqueeze(1).broadcast_to([P, NT, D]),
                                ALU.add).then_inc(y_ready[ch], 1)

            def one_pass(j, last):
                steps.begin(j)
                for q in range(Q):
                    if not (last and q == Q - 1):
                        norm(*after(j, q))
                        low_parts(*after(j, q))
                    residual(j, q)

            norm(0, 0)
            low_parts(0, 0)
            one_pass(0, False)
            with dve.Fori(1, PASSES - 1) as j:
                one_pass(j, False)
            one_pass(PASSES - 1, True)

        @block.tensor
        def _(pe):
            t_ = nc.tensor

            def transposes(j, q):
                ch, p, n = turn(j, q)
                pe.wait_ge(xn_ready[ch], n + 1)
                for c in range(C):
                    for t in range(NT):
                        last = t_.transpose(TB[c][:, t * P:(t + 1) * P], xn[ch][:, t, c * P:(c + 1) * P], ident[:, :])
                last.then_inc(xT_psum[ch], 1)

            def up(j, q):
                ch, p, n = turn(j, q)
                pe.wait_ge(xT_ready[ch], n + 1)
                if ch == 0:
                    pe.wait_ge(w1_split[p], j + 1)
                for f in range(FC):
                    if f >= 4:
                        pe.wait_ge(hidden_ready, (Q * j + q) * FC + f - 3)
                    cols = slice(f * P, (f + 1) * P)
                    products = [(w, x, c) for c in range(C) for w, x in ((w1l, xTh), (w1h, xTl), (w1h, xTh))]
                    for k, (w, x, c) in enumerate(products):
                        last = t_.matmul(HB[f % 4][:, :], w[p][:, c, cols], x[ch][:, c, :], start=k == 0,
                                         stop=k == len(products) - 1)
                    last.then_inc(hidden_psum, 1)

            def down(j, q):
                ch, p, n = turn(j, q)
                if ch == 0:
                    pe.wait_ge(out_taken[1], n)
                else:
                    pe.wait_ge(out_taken[0], n + 1)
                for t in range(NT):
                    for f in range(FC):
                        if t == 0:
                            pe.wait_ge(hidden_ready, (Q * j + q) * FC + f + 1)
                        last = t_.matmul(OB[t // 2][:, t % 2 * D:(t % 2 + 1) * D], hT[ch][:, f, t * P:(t + 1) * P],
                                         w2[p][:, f, :], start=f == 0, stop=f == FC - 1)
                last.then_inc(out_psum[ch], 1)

            def one_pass(j, last):
                for q in range(Q):
                    up(j, q)
                    if not (last and q == Q - 1):
                        transposes(*after(j, q))
                    down(j, q)

            pe.wait_ge(consts, 3 + Q)
            transposes(0, 0)
            one_pass(0, False)
            with pe.Fori(1, PASSES - 1) as j:
                one_pass(j, False)
            one_pass(PASSES - 1, True)


class Layer1Weights:

    def __init__(self, nc, ctx, a):
        D, D3 = a["L1_attn_w_qkv"].shape
        NE = a["L1_ffn_gate_w"].shape[1]
        DH = a["L1_attn_q_gamma"].shape[0]
        C, H = D // P, D // DH
        sb = lambda name, shape: ctx.enter_context(nc.sbuf_tensor("c_" + name, shape, F32))
        self.a, self.D, self.H = a, D, H
        self.loaded = nc.alloc_semaphore("c_weights_loaded")
        self.wqkv, self.wo, self.wvx = sb("wqkv", [P, C, D3]), sb("wo", [P, C, D]), sb("wvx", [P, C, D])
        self.bqT, self.bkT, self.bvx = sb("bqT", [P, C]), sb("bkT", [P, C]), sb("bvx", [P, D])
        self.gam = sb("gam", [P, 2 * H, DH])
        self.bet = sb("bet", [P, 2 * H, DH])
        self.gw, self.gb = sb("gw", [P, C, NE]), sb("gb", [P, NE])
        self.w1, self.w2 = sb("w1", [P, NE, C, D]), sb("w2", [P, NE, C, D])
        self.b1, self.b2 = sb("b1", [P, NE, C]), sb("b2", [NE, D])
        self.count = 16

    def load(self, sync):
        a, by_chunk = self.a, lambda t: t.rearrange("(c p) n -> p c n", p=P)

        def weight(dst, src, **kw):
            sync.dma_start(dst, src, **kw).then_inc(self.loaded, 16)

        col = dict(allow_slow_non_contiguous=True)
        weight(self.bqT[:, :], a["L1_xattn_bq"].rearrange("(c p) -> p c", p=P), **col)
        weight(self.bkT[:, :], a["L1_xattn_bk"].rearrange("(c p) -> p c", p=P), **col)
        weight(self.wqkv[:, :, :], by_chunk(a["L1_attn_w_qkv"]))
        weight(self.wo[:, :, :], by_chunk(a["L1_attn_w_proj"]))
        weight(self.wvx[:, :, :], by_chunk(a["L1_xattn_Wv"]))
        weight(self.bvx[:, :], a["L1_xattn_bv"].partition_broadcast(P))
        for n, name in enumerate("qk"):
            weight(self.gam[:, n * self.H, :], a[f"L1_attn_{name}_gamma"].partition_broadcast(P))
            weight(self.bet[:, n * self.H, :], a[f"L1_attn_{name}_beta"].partition_broadcast(P))
        weight(self.gw[:, :, :], by_chunk(a["L1_ffn_gate_w"]))
        weight(self.gb[:, :], a["L1_ffn_gate_b"].partition_broadcast(P))
        weight(self.w1[:, :, :, :], a["L1_ffn_w1"].rearrange("e (c p) n -> p e c n", p=P))
        weight(self.w2[:, :, :, :], a["L1_ffn_w2"].rearrange("e (c p) n -> p e c n", p=P))
        weight(self.b1[:, :, :], a["L1_ffn_b1"].rearrange("e (c p) -> p e c", p=P), **col)
        weight(self.b2[:, :], a["L1_ffn_b2"])


def phase_c(nc, a, x3_d, out, w):
    ctx_in = a["ctx_1024"]
    B, S, D = ctx_in.shape
    C, T = D // P, S // P
    DH = a["L1_attn_q_gamma"].shape[0]
    H = D // DH
    NE = a["L1_ffn_gate_w"].shape[1]
    PAIRS = B // 2
    HG = 4
    NG = H // HG
    SL = 4 * DH
    NB = H * SL // P
    with ExitStack() as ctx:
        sb = lambda name, shape, dt=F32: ctx.enter_context(nc.sbuf_tensor("c_" + name, shape, dt))
        sb2 = lambda name, shape, dt=F32: [sb(f"{name}{u}", shape, dt) for u in range(2)]
        sem = lambda name: nc.alloc_semaphore("c_" + name)
        sem2 = lambda name: [sem(f"{name}{u}") for u in range(2)]
        X = [ctx.enter_context(nc.psum_tensor(f"c_X{u}", [P, 512], F32)) for u in range(2)]
        Y = [ctx.enter_context(nc.psum_tensor(f"c_Y{u}", [P, 512], F32)) for u in range(2)]
        SR = [ctx.enter_context(nc.psum_tensor(f"c_S{n}", [P, 1024], F32)) for n in range(2)]
        halves = lambda bank: bank[:, 0:512].rearrange("p (c n) -> p c n", c=2)
        heads = lambda ring: ring[:, :].rearrange("p (h n) -> p h n", h=HG)
        blocks = lambda bank: slice(bank * NB // 2, (bank + 1) * NB // 2)
        of_bank = lambda ring, bank: ring[:, bank * 512:(bank + 1) * 512].rearrange("p (b n) -> p b n", n=P)
        place = lambda h: h % 2 * 2 + h % HG // 2

        half = lambda n, e: SR[n][:, e % 2 * 512:e % 2 * 512 + 512].rearrange("p (c n) -> p c n", c=2)

        ident = sb("ident", [P, P])
        identr = sb("identr", [P, P], F32R)
        ones = sb("ones", [P, 1])
        eps = sb("eps", [P, 1])
        mhalf = sb("mhalf", [P, 2 * T * H])
        iota8 = sb("iota8", [P, NE])
        selh = sb("selh", [P, H, DH])
        wqkv, wo, wvx, bqT, bkT, bvx, gam, bet = w.wqkv, w.wo, w.wvx, w.bqT, w.bkT, w.bvx, w.gam, w.bet
        gw, gb, w1, w2, b1, b2 = w.gw, w.gb, w.w1, w.w2, w.b1, w.b2
        wqk = sb("wqk", [P, C, D])
        g0 = sb("g0", [P, C])
        wr = sb("wr", [P, C])
        r0 = sb("r0", [P, 1])

        q4 = sb("q4", [P, T, H, SL], F32R)
        k4 = sb("k4", [P, T, H, SL], F32R)
        PT = [sb(f"PT{n}", [P, T, HG, S]) for n in range(3)]
        sq = sb("sq", [P, T, 2 * H, DH])
        hid = [sb(f"hid{n}", [P, C, S]) for n in range(2)]

        x = sb2("x", [P, T, D])
        cx = sb2("cx", [P, T, D])
        cxT = sb2("cxT", [P, C, S])
        st = sb2("st", [P, T, 6])
        mv = sb2("mv", [P, T, 2])
        rs = sb2("rs", [P, T])
        xn = sb2("xn", [P, T, D])
        xnT = sb2("xnT", [P, C, S])
        qk = sb2("qk", [P, T, 2 * H, DH])
        hm = sb2("hm", [P, T * 2 * H])
        v32 = sb2("v32", [P, T, H, 2 * DH])
        q4T = sb2("q4T", [P, NB, S], F32R)
        k4T = sb2("k4T", [P, NB, S], F32R)
        nm = sb2("nm", [P, T, P])
        nmT = sb2("nmT", [P, S])
        rden = sb2("rden", [P, T, H])
        x4 = sb2("x4", [P, T, D])
        pe2 = sb2("pe2", [P, T, S + 1])
        m2 = sb2("m2", [P, T])
        nb2 = sb2("nb2", [P, T])
        r2 = sb2("r2", [P, T])
        den2 = sb2("den2", [P, T])
        rden2 = sb2("rden2", [P, T])
        peT = sb2("peT", [P, T, S])
        mix = sb2("mix", [P, T, D])
        xmT = sb2("xmT", [P, C, S])
        lg = sb2("lg", [P, T, NE])
        mx = sb2("mx", [P, T, 8])
        ix = sb2("ix", [P, T, 8], U32)
        ixf = sb2("ixf", [P, T, 2])
        top = sb2("top", [P, T, NE])
        comb = sb2("comb", [P, T, NE])
        combT = sb2("combT", [NE, S])
        y = sb2("y", [P, T, D])
        oT = [t[:, :, :, :].rearrange("p t h d -> p (t h d)").rearrange("p (g s) -> p g s", g=NG) for t in qk]
        gT = [t[:, 0, :, :].rearrange("p h d -> p (h d)").rearrange("p (c s) -> p c s", c=C) for t in qk]
        gx = [t[:, 1, :, :].rearrange("p h d -> p (h d)").rearrange("p (c s) -> p c s", c=C) for t in qk]

        consts, w_in, dve_consts = sem("consts"), sem("w_in"), sem("dve_consts")
        pro_psum, pro_sb = sem("pro_psum"), sem("pro_sb")
        dve_front, dve_back = sem("dve_front"), sem("dve_back")
        pool_front, pool_back, squared = sem("pool_front"), sem("pool_back"), sem("squared")
        dve_passed, pool_passed = sem("dve_passed"), sem("pool_passed")
        x_loaded, cx_loaded, out_stored = sem2("x_loaded"), sem2("cx_loaded"), sem2("out_stored")
        var, rstd, xn_ready = sem2("var"), sem2("rstd"), sem2("xn_ready")
        xnT_psum, xnT_ready = sem2("xnT_psum"), sem2("xnT_ready")
        cxT_psum, cxT_ready = sem2("cxT_psum"), sem2("cxT_ready")
        qk_psum, qk_taken = sem2("qk_psum"), sem2("qk_taken")
        v_psum, v_ready = sem2("v_psum"), sem2("v_ready")
        centred, hvar, hroot = sem2("centred"), sem2("hvar"), sem2("hroot")
        qk_ready, high_ready, low_ready = sem2("qk_ready"), sem2("high_ready"), sem2("low_ready")
        q4T_psum, k4T_psum = sem("q4T_psum"), sem("k4T_psum")
        q4T_taken, k4T_taken = sem("q4T_taken"), sem("k4T_taken")
        raw_psum, raw_taken = sem("raw_psum"), sem("raw_taken")
        nm_ready, nmT_psum = sem2("nm_ready"), sem2("nmT_psum")
        nmT_ready, shift_ready = sem2("nmT_ready"), sem2("shift_ready")
        scores_psum, probs_ready, probs_used = sem("scores_psum"), sem("probs_ready"), sem("probs_used")
        oT_ready, o_psum, o_ready = sem2("oT_ready"), sem2("o_psum"), sem2("o_ready")
        o2T_psum, o2T_ready = sem2("o2T_psum"), sem2("o2T_ready")
        proj_psum, x4_ready = sem2("proj_psum"), sem2("x4_ready")
        g_psum, g_ready, gx_ready = sem2("g_psum"), sem2("g_ready"), sem2("gx_ready")
        s2_psum, nb2_ready, p2_ready = sem2("s2_psum"), sem2("nb2_ready"), sem2("p2_ready")
        own_ready = sem2("own_ready")
        peT_psum, peT_ready = sem2("peT_psum"), sem2("peT_ready")
        mix_psum, mix_ready = sem2("mix_psum"), sem2("mix_ready")
        mixT_psum, mixT_ready = sem2("mixT_psum"), sem2("mixT_ready")
        cross_psum, x5_ready = sem2("cross_psum"), sem2("x5_ready")
        gates_psum, comb_ready = sem2("gates_psum"), sem2("comb_ready")
        combT_psum, combT_ready = sem2("combT_psum"), sem2("combT_ready")
        bias_psum, y_ready = sem2("bias_psum"), sem2("y_ready")
        hid_psum, hid_ready = sem2("hid_psum"), sem2("hid_ready")
        eo_psum, eo_taken = sem2("eo_psum"), sem2("eo_taken")

        rows = lambda t: t.rearrange("(i u t p) d -> i u p t d", u=2, t=T, p=P)
        x_rows, cx_rows, out_rows = rows(x3_d), rows(ctx_in.rearrange("b s d -> (b s) d")), rows(out.rearrange("b s d -> (b s) d"))
        by_chunk = lambda t: t.rearrange("(c p) n -> p c n", p=P)

        ORDER = (
            "f stats", "m expert0", "f norm", "b o", "m expert1", "f normT", "b o2T", "m expert2", "m expert3",
            "f qk", "b proj", "f head sum", "m expert4", "b norm2", "m expert5", "f head mean", "f head var",
            "f head root", "f head scale", "b norm2T", "m expert6", "b g", "f split", "m expert7", "b scores",
            "b exp", "m expert8", "b expT", "f splitT0", "f splitT1", "b mix", "f raw0", "f raw1", "f raw2",
            "f raw3", "f max0", "f raw4", "b mixT", "f raw5", "f shift0", "b cross", "f raw6", "f raw7",
            "f max1", "f v", "b norm3", "f shift1", "b norm3T", "f attend0", "b gates", "f attend1", "b bias",
            "f attend2", "f attend3", "f attend4")

        block = ctx.enter_context(nc.Block())

        @block.sync
        def _(sync):
            def load(u, i):
                sync.wait_ge(x4_ready[u], i)
                sync.dma_start(x[u][:, :, :], x_rows[i, u]).then_inc(x_loaded[u], 16)
                sync.wait_ge(mix_psum[u], i)
                sync.dma_start(cx[u][:, :, :], cx_rows[i, u]).then_inc(cx_loaded[u], 16)

            def store(u, i):
                sync.wait_ge(eo_taken[u], (i + 1) * NE)
                sync.dma_start(out_rows[i, u], y[u][:, :, :]).then_inc(out_stored[u], 16)

            for tile, name in zip(cxT, ("Wq", "Wk")):
                sync.dma_start(tile[:, :, :], by_chunk(a[f"L1_xattn_{name}"])).then_inc(w_in, 16)
            load(0, 0)
            load(1, 0)
            load(0, 1)
            load(1, 1)
            store(0, 0)
            with sync.Fori(1, PAIRS - 1) as i:
                for u in range(2):
                    load(u, i + 1)
                    store(1 - u, i - 1 + u)
            store(1, PAIRS - 2)
            store(0, PAIRS - 1)
            store(1, PAIRS - 1)
            for u in range(2):
                sync.wait_ge(out_stored[u], 16 * PAIRS)

        @block.gpsimd
        def _(pool):
            g = nc.gpsimd
            make_identity(nc, ident, consts, 0)
            g.memset(ones[:, :], 1.0).then_inc(consts, 1)
            g.memset(mhalf[:, :], -0.5).then_inc(consts, 1)
            g.iota(iota8[:, :], [[1, NE]], base=0, channel_multiplier=0,
                   allow_small_or_imprecise_dtypes=True).then_inc(consts, 1)
            g.memset(selh[:, :, :], 0.0).then_inc(consts, 1)
            pool.wait_ge(consts, 6)
            by_place = selh[:, :, :].rearrange("p (g a b) d -> p g a b d", a=2, b=2).rearrange("p g a b d -> p g a (b d)")
            for b in range(2):
                part = by_place[:, :, :, b * DH:(b + 1) * DH]
                g.affine_select(out=part, in_=part, compare_op=ALU.not_equal, fill=1.0, base=2 * b,
                                pattern=[[HG, NG], [1, 2], [-1, DH]], channel_multiplier=0).then_inc(consts, 1)
            for u in range(2):
                g.memset(v32[u][:, :, :, :], 0.0).then_inc(consts, 1)
                g.memset(nm[u][:, :, :], 0.0).then_inc(consts, 1)
            pool.wait_ge(consts, 12)
            for u in range(2):
                g.memset(v32[u][:, :, :, DH:DH + 1], 1.0).then_inc(consts, 1)
            pool.wait_ge(consts, 14)
            front, back = Steps(pool, pool_front, 1), Steps(pool, pool_back, 2)

            def row_rstd(steps, u, n):
                pool.wait_ge(var[u], n)
                stand_alone(pool, pool_passed)
                e = steps.did(g.tensor_scalar(rs[u][:, :], mv[u][:, :, 1], EPS, None, ALU.add))
                steps.need(e)
                g.tensor_tensor(rs[u][:, :], rs[u][:, :], mhalf[:, 0:T], ALU.pow).then_inc(rstd[u], 1)

            def own_scores(u, i):
                pool.wait_ge(g_ready[u], i + 1)
                g.tensor_tensor(gx[u], gT[u], xnT[u][:, :, :], ALU.mult).then_inc(gx_ready[u], 1)

            skewed(pool, PAIRS, ((0,), (1,)), ORDER, {
                "f stats": lambda u, i: row_rstd(front, u, 3 * i + 1),
                "b norm2": lambda u, i: row_rstd(back, u, 3 * i + 2),
                "b g": own_scores, "b norm3": lambda u, i: row_rstd(back, u, 3 * i + 3),
            }, front, back)

        @block.scalar
        def _(act):
            s = nc.scalar
            act.wait_ge(pro_psum, 1)
            s.activation(xnT[0][:, :, :], halves(X[0]), ACT.Copy).then_inc(pro_sb, 1)
            s.activation(xnT[1][:, :, :], halves(X[1]), ACT.Copy).then_inc(pro_sb, 1)
            act.wait_ge(pro_psum, 2)
            s.activation(wqk[:, :, :], halves(X[0]), ACT.Copy).then_inc(pro_sb, 1)
            s.activation(g0[:, :], X[1][:, 0:C], ACT.Copy).then_inc(pro_sb, 1)
            s.activation(wr[:, :], X[1][:, C:2 * C], ACT.Copy).then_inc(pro_sb, 1)
            s.activation(r0[:, :], X[1][:, 2 * C:2 * C + 1], ACT.Copy).then_inc(pro_sb, 1)
            act.wait_ge(pro_sb, 6)
            act.wait_ge(w.loaded, 16 * w.count)
            act.wait_ge(consts, 14)
            act.wait_ge(dve_consts, 7)

            def take_xnT(u, n):
                act.wait_ge(xnT_psum[u], n)
                s.activation(xnT[u][:, :, :], halves(X[u]), ACT.Copy).then_inc(xnT_ready[u], 1)

            def normT(u, i):
                take_xnT(u, 3 * i + 1)
                act.wait_ge(cxT_psum[u], i + 1)
                s.activation(cxT[u][:, :, :], halves(Y[u]), ACT.Copy).then_inc(cxT_ready[u], 1)

            def take_qk(u, i):
                act.wait_ge(qk_psum[u], i + 1)
                for t, bank in enumerate((X[u], Y[u])):
                    last = s.activation(qk[u][:, t, :, :], bank[:, :].rearrange("p (h d) -> p h d", d=DH), ACT.Copy)
                last.then_inc(qk_taken[u], 1)

            def take_v(u, i):
                act.wait_ge(v_psum[u], i + 1)
                s.activation(v32[u][:, :, :, 0:DH], Y[u][:, :].rearrange("p (t h d) -> p t h d", t=T, d=DH),
                             ACT.Copy).then_inc(v_ready[u], 1)

            def head_squares(u, i):
                act.wait_ge(centred[u], i + 1)
                act.wait_ge(hvar[1 - u], i + u)
                s.activation(sq[:, :, :, :], qk[u][:, :, :, :], ACT.Square).then_inc(squared, 1)

            def head_root(u, i):
                act.wait_ge(hvar[u], i + 1)
                s.activation(hm[u][:, :], hm[u][:, :], ACT.Sqrt, bias=eps[:, 0:1], scale=1.0 / DH)\
                    .then_inc(hroot[u], 1)

            def split(u, i):
                act.wait_ge(qk_ready[u], i + 1)
                act.wait_ge(k4T_psum, 8 * i + 4 * u)
                for t in range(T):
                    src = lambda n: qk[u][:, t, n * H:(n + 1) * H, :].unsqueeze(2).broadcast_to([P, H, 2, DH])
                    s.activation(q4[:, t, :, DH:3 * DH].rearrange("p h (r d) -> p h r d", r=2), src(0), ACT.Copy)
                    k = k4[:, t, :, :].rearrange("p h (r d) -> p h r d", d=DH)[:, :, 1:4:2, :]
                    last = s.activation(k, src(1), ACT.Copy)
                last.then_inc(high_ready[u], 1)

            def take_q4T(t, u, i):
                for bank in range(2):
                    act.wait_ge(q4T_psum, 8 * i + 4 * u + 2 * t + bank + 1)
                    s.activation(q4T[u][:, blocks(bank), t * P:(t + 1) * P], of_bank(SR[0], bank), ACT.Copy)\
                        .then_inc(q4T_taken, 1)

            def shift(t, u, i):
                act.wait_ge(nmT_ready[u], T * i + t + 1)
                at, cols = slice(SL, SL + H), slice(t * P, (t + 1) * P)
                s.activation(q4T[u][at, :, cols], nmT[u][at, cols].unsqueeze(1).broadcast_to([H, NB, P]), ACT.Copy)\
                    .then_inc(shift_ready[u], 1)

            def attend(g, u, i):
                if g < NG:
                    n = (2 * i + u) * NG + g
                    act.wait_ge(probs_used, n - 2 if u * NG + g >= 3 else 2 * i * NG)
                    for t in range(T):
                        act.wait_ge(scores_psum, n * T + t + 1)
                        s.activation(PT[(u * NG + g) % 3][:, t, :, :], heads(SR[t]), ACT.Exp,
                                     scale=float(DH) ** -0.5).then_inc(probs_ready, 1)
                else:
                    act.wait_ge(probs_used, (2 * i + u + 1) * NG)
                    for b, bank in enumerate((X[u], Y[u])):
                        last = s.activation(oT[u][:, 2 * b:2 * b + 2, :], halves(bank), ACT.Copy)
                    last.then_inc(oT_ready[u], 1)

            def take_o2T(u, i):
                act.wait_ge(o2T_psum[u], i + 1)
                s.activation(xnT[u][:, :, :], halves(X[u]), ACT.Copy).then_inc(o2T_ready[u], 1)

            def take_g(u, i):
                act.wait_ge(g_psum[u], i + 1)
                for c in range(C):
                    last = s.activation(gT[u][:, c, :], halves(Y[u])[:, c, :], ACT.Identity, bias=g0[:, c:c + 1])
                last.then_inc(g_ready[u], 1)

            def exps(u, i):
                act.wait_ge(nb2_ready[u], i + 1)
                for t, bank in enumerate((X[u], Y[u])):
                    last = s.activation(pe2[u][:, t, :], bank[:, 0:S + 1], ACT.Exp, bias=nb2[u][:, t:t + 1],
                                        accum_out=den2[u][:, t:t + 1])
                last.then_inc(p2_ready[u], 1)

            def take_expT(u, i):
                act.wait_ge(p2_ready[u], i + 1)
                act.wait_ge(mixT_psum[u], i)
                for t in range(T):
                    last = s.activation(mix[u][:, t, :], xn[u][:, t, :], ACT.Identity, scale=pe2[u][:, t, S:S + 1])
                last.then_inc(own_ready[u], 1)
                act.wait_ge(peT_psum[u], i + 1)
                s.activation(peT[u][:, :, :], halves(X[u]), ACT.Copy).then_inc(peT_ready[u], 1)

            def take_mixT(u, i):
                act.wait_ge(mixT_psum[u], i + 1)
                s.activation(peT[u][:, :, :], halves(X[u]), ACT.Copy).then_inc(mixT_ready[u], 1)

            def take_xmT(u, i):
                act.wait_ge(xnT_psum[u], 3 * i + 3)
                s.activation(xmT[u][:, :, :], halves(X[u]), ACT.Copy).then_inc(xnT_ready[u], 1)

            def take_combT(u, i):
                act.wait_ge(combT_psum[u], i + 1)
                s.activation(combT[u][:, :], Y[u][0:NE, P:P + S], ACT.Copy).then_inc(combT_ready[u], 1)

            def hidden(e, u, i):
                act.wait_ge(hid_psum[u], i * NE + e + 1)
                for c in range(C):
                    last = s.activation(hid[e % 2][:, c, :], half(0, e)[:, c, :], ACT.Relu, bias=b1[:, e, c:c + 1])
                last.then_inc(hid_ready[u], 1)

            skewed(act, PAIRS, ((0,), (1,)), ORDER, {
                "f normT": normT, "f qk": take_qk, "f v": take_v, "f head mean": head_squares,
                "f head root": head_root, "f split": split,
                "f splitT0": partial(take_q4T, 0), "f splitT1": partial(take_q4T, 1),
                "f shift0": partial(shift, 0), "f shift1": partial(shift, 1), "b o2T": take_o2T,
                "b norm2T": lambda u, i: take_xnT(u, 3 * i + 2), "b g": take_g, "b exp": exps,
                "b expT": take_expT, "b mixT": take_mixT,
                "b norm3T": take_xmT, "b bias": take_combT,
                **{f"f attend{g}": partial(attend, g) for g in range(NG + 1)},
                **{f"m expert{e}": partial(hidden, e) for e in range(NE)},
            })

        @block.vector
        def _(dve):
            v = nc.vector
            dve.wait_ge(w.loaded, 16 * w.count)
            dve.wait_ge(consts, 14)
            v.tensor_copy(identr[:, :], ident[:, :]).then_inc(dve_consts, 1)
            for n in range(2):
                for tile in (gam, bet):
                    v.tensor_copy(tile[:, n * H + 1:(n + 1) * H, :],
                                  tile[:, n * H:n * H + 1, :].broadcast_to([P, H - 1, DH])).then_inc(dve_consts, 1)
            for t in range(T):
                v.tensor_copy(k4[:, t, :, 0:DH], selh[:, :, :])
                last = v.tensor_scalar(q4[:, t, :, 0:DH], selh[:, :, :], 0.0, None, ALU.mult)
            last.then_inc(dve_consts, 1)
            v.memset(eps[:, :], EPS).then_inc(dve_consts, 1)
            front, back = Steps(dve, dve_front, 7), Steps(dve, dve_back, 23)

            def stats(steps, u, src):
                done = [steps.did(v.bn_stats(st[u][:, t, :], src[:, t, :])) for t in range(T)]
                for t in range(T):
                    steps.need(done[t])
                    stand_alone(dve, dve_passed)
                    last = v.bn_aggr(mv[u][:, t, :], st[u][:, t, :])
                last.then_inc(var[u], 1)

            def norm(u, src, n):
                dve.wait_ge(rstd[u], n)
                for t in range(T):
                    last = v.tensor_scalar(xn[u][:, t, :], src[:, t, :], mv[u][:, t, 0:1], rs[u][:, t:t + 1],
                                           ALU.subtract, ALU.mult)
                last.then_inc(xn_ready[u], 1)

            def first_stats(u, i):
                dve.wait_ge(x_loaded[u], 16 * i + 16)
                stats(front, u, x[u])

            q32 = [t[:, :, :, :].rearrange("p t h d -> p (t h) d") for t in qk]
            over_head = [t[:, :].unsqueeze(2).broadcast_to([P, T * 2 * H, DH]) for t in hm]

            def head_sum(u, i):
                dve.wait_ge(qk_taken[u], i + 1)
                k = front.did(v.tensor_reduce(hm[u][:, :], q32[u], AX.X, ALU.add))
                front.need(k)
                k = front.did(v.tensor_scalar(hm[u][:, :], hm[u][:, :], 1.0 / DH, None, ALU.mult))
                front.need(k)
                v.tensor_tensor(q32[u], q32[u], over_head[u], ALU.subtract).then_inc(centred[u], 1)

            def head_var(u, i):
                dve.wait_ge(squared, 2 * i + u + 1)
                v.tensor_reduce(hm[u][:, :], sq[:, :, :, :].rearrange("p t h d -> p (t h) d"), AX.X, ALU.add)\
                    .then_inc(hvar[u], 1)

            def head_scale(u, i):
                dve.wait_ge(hroot[u], i + 1)
                k = front.did(v.reciprocal(hm[u][:, :], hm[u][:, :]))
                front.need(k)
                k = front.did(v.tensor_tensor(q32[u], q32[u], over_head[u], ALU.mult))
                for tile, op in ((gam, ALU.mult), (bet, ALU.add)):
                    front.need(k)
                    k = [v.tensor_tensor(qk[u][:, t, :, :], qk[u][:, t, :, :], tile[:, :, :], op) for t in range(T)][-1]
                    if tile is gam:
                        k = front.did(k)
                k.then_inc(qk_ready[u], 1)

            def split(u, i):
                dve.wait_ge(high_ready[u], i + 1)
                for t in range(T):
                    for n, (dst, at) in enumerate(((q4, 3 * DH), (k4, 2 * DH))):
                        last = v.tensor_tensor(dst[:, t, :, at:at + DH], qk[u][:, t, n * H:(n + 1) * H, :],
                                               dst[:, t, :, DH:2 * DH].bitcast(F32), ALU.subtract)
                last.then_inc(low_ready[u], 1)

            def take_k4T(t, u, i):
                for bank in range(2):
                    dve.wait_ge(k4T_psum, 8 * i + 4 * u + 2 * t + bank + 1)
                    v.tensor_copy(k4T[u][:, blocks(bank), t * P:(t + 1) * P], of_bank(SR[1], bank))\
                        .then_inc(k4T_taken, 1)

            def raw_max(f, u, i):
                t, g = f // NG, f % NG
                dve.wait_ge(raw_psum, (2 * i + u) * T * NG + f + 1)
                v.tensor_reduce(nm[u][:, t, g * HG:(g + 1) * HG], heads(SR[f % 2]), AX.X, ALU.max, negate=True)\
                    .then_inc(raw_taken, 1)

            def copy_max(t, u, i):
                dve.wait_ge(raw_taken, (2 * i + u) * T * NG + (t + 1) * NG)
                v.tensor_copy(nm[u][:, t, SL:SL + H], nm[u][:, t, 0:H]).then_inc(nm_ready[u], 1)

            def shift(t, u, i):
                cols = slice(t * P, (t + 1) * P)
                dve.wait_ge(nmT_psum[u], T * i + t + 1)
                v.tensor_copy(nmT[u][:, cols], X[u][:, cols]).then_inc(nmT_ready[u], 1)
                dve.wait_ge(nmT_ready[u], T * i + t + 1)
                v.tensor_copy(q4T[u][0:H, :, cols], nmT[u][0:H, cols].unsqueeze(1).broadcast_to([H, NB, P]))\
                    .then_inc(shift_ready[u], 1)

            def take_o(u, i):
                dve.wait_ge(o_psum[u], i + 1)
                for t, bank in enumerate((X[u], Y[u])):
                    k = back.did(v.reciprocal(rden[u][:, t, :], bank[:, :].rearrange("p (h d) -> p h d", h=H)[:, :, DH]))
                back.need(k)
                for t, bank in enumerate((X[u], Y[u])):
                    o = bank[:, :].rearrange("p (h d) -> p h d", h=H)
                    last = v.tensor_tensor(xn[u][:, t, :].rearrange("p (h d) -> p h d", h=H), o[:, :, 0:DH],
                                           rden[u][:, t, :].unsqueeze(2).broadcast_to([P, H, DH]), ALU.mult)
                last.then_inc(o_ready[u], 1)

            def add_proj(u, i):
                dve.wait_ge(proj_psum[u], i + 1)
                v.tensor_tensor(x4[u][:, :, :], x[u][:, :, :], halves(Y[u]), ALU.add).then_inc(x4_ready[u], 1)
                dve.wait_ge(x4_ready[u], i + 1)
                stats(back, u, x4[u])

            def norm2(u, i):
                norm(u, x4[u], 3 * i + 2)
                dve.wait_ge(xn_ready[u], 3 * i + 2)
                back.did(v.tensor_tensor(x4[u][:, :, :], x4[u][:, :, :],
                                         bvx[:, :].unsqueeze(1).broadcast_to([P, T, D]), ALU.add))

            def score_max(u, i):
                dve.wait_ge(s2_psum[u], i + 1)
                for t, bank in enumerate((X[u], Y[u])):
                    back.did(v.tensor_reduce(m2[u][:, t:t + 1], bank[:, 0:S + 1], AX.X, ALU.max))
                    k = back.did(v.tensor_scalar(r2[u][:, t:t + 1], bank[:, S + 2:S + 3], r0[:, 0:1], None, ALU.add))
                back.need(k)
                k = back.did(v.tensor_tensor(m2[u][:, :], m2[u][:, :], r2[u][:, :], ALU.add))
                back.need(k)
                v.tensor_tensor(nb2[u][:, :], r2[u][:, :], m2[u][:, :], ALU.subtract).then_inc(nb2_ready[u], 1)

            def invert(u, i):
                dve.wait_ge(p2_ready[u], i + 1)
                back.did(v.reciprocal(rden2[u][:, :], den2[u][:, :]))

            def add_mix(u, i):
                dve.wait_ge(mix_psum[u], i + 1)
                dve.wait_ge(own_ready[u], i + 1)
                v.tensor_tensor(mix[u][:, :, :], mix[u][:, :, :], halves(Y[u]), ALU.add).then_inc(mix_ready[u], 1)

            def add_cross(u, i):
                dve.wait_ge(cross_psum[u], i + 1)
                dve.wait_ge(eo_taken[u], i * NE)
                dve.wait_ge(out_stored[u], 16 * i)
                for t in range(T):
                    last = v.scalar_tensor_tensor(y[u][:, t, :], halves(Y[u])[:, t, :], rden2[u][:, t:t + 1],
                                                  x4[u][:, t, :], ALU.mult, ALU.add)
                last.then_inc(x5_ready[u], 1)
                dve.wait_ge(x5_ready[u], i + 1)
                stats(back, u, y[u])

            def gates(u, i):
                dve.wait_ge(gates_psum[u], i + 1)
                k = back.did(v.tensor_tensor(lg[u][:, :, :], Y[u][:, 0:T * NE].rearrange("p (t e) -> p t e", t=T),
                                             gb[:, :].unsqueeze(1).broadcast_to([P, T, NE]), ALU.add))
                back.need(k)
                stand_alone(dve, dve_passed)
                for t in range(T):
                    k = back.did(v.max(mx[u][:, t, :], lg[u][:, t, :]))
                back.need(k)
                stand_alone(dve, dve_passed)
                for t in range(T):
                    k = back.did(v.max_index(ix[u][:, t, :], mx[u][:, t, :], lg[u][:, t, :]))
                back.need(k)
                k = back.did(v.tensor_copy(ixf[u][:, :, :], ix[u][:, :, 0:2]))
                back.need(k)
                for t in range(T):
                    back.did(v.scalar_tensor_tensor(comb[u][:, t, :], iota8[:, :], ixf[u][:, t, 0:1],
                                                    lg[u][:, t, :], ALU.is_equal, ALU.mult))
                    k = back.did(v.scalar_tensor_tensor(top[u][:, t, :], iota8[:, :], ixf[u][:, t, 1:2],
                                                        lg[u][:, t, :], ALU.is_equal, ALU.mult))
                back.need(k)
                v.tensor_tensor(comb[u][:, :, :], comb[u][:, :, :], top[u][:, :, :], ALU.add).then_inc(comb_ready[u], 1)

            def add_bias(u, i):
                dve.wait_ge(bias_psum[u], i + 1)
                v.tensor_tensor(y[u][:, :, :], y[u][:, :, :], halves(Y[u]), ALU.add).then_inc(y_ready[u], 1)

            def expert(e, u, i):
                if e == 0:
                    dve.wait_ge(y_ready[u], i + 1)
                else:
                    dve.wait_ge(eo_taken[u], i * NE + e)
                dve.wait_ge(eo_psum[u], i * NE + e + 1)
                for t in range(T):
                    last = v.scalar_tensor_tensor(y[u][:, t, :], half(1, e)[:, t, :], comb[u][:, t, e:e + 1],
                                                  y[u][:, t, :], ALU.mult, ALU.add)
                last.then_inc(eo_taken[u], 1)

            skewed(dve, PAIRS, ((0,), (1,)), ORDER, {
                "f stats": first_stats, "f norm": lambda u, i: norm(u, x[u], 3 * i + 1), "f head sum": head_sum,
                "f head var": head_var, "f head scale": head_scale, "f split": split,
                "f splitT0": partial(take_k4T, 0), "f splitT1": partial(take_k4T, 1),
                "f max0": partial(copy_max, 0), "f max1": partial(copy_max, 1), "f shift0": partial(shift, 0),
                "f shift1": partial(shift, 1), "b o": take_o, "b proj": add_proj, "b norm2": norm2,
                "b scores": score_max, "b expT": invert, "b mix": add_mix, "b cross": add_cross,
                "b norm3": lambda u, i: norm(u, y[u], 3 * i + 3), "b gates": gates, "b bias": add_bias,
                **{f"f raw{f}": partial(raw_max, f) for f in range(T * NG)},
                **{f"m expert{e + 1}": partial(expert, e) for e in range(NE)},
            }, front, back)

        @block.tensor
        def _(pe):
            t_ = nc.tensor

            def transposes(bank, src):
                for c in range(C):
                    for t in range(T):
                        last = t_.transpose(halves(bank)[:, c, t * P:(t + 1) * P], src[:, t, c * P:(c + 1) * P],
                                            ident[:, :])
                return last

            def project(bank, srcT, weight):
                for t in range(T):
                    for c in range(C):
                        last = t_.matmul(halves(bank)[:, t, :], srcT[:, c, t * P:(t + 1) * P], weight[:, c, :],
                                         start=c == 0, stop=c == C - 1)
                return last

            pe.wait_ge(consts, 14)
            pe.wait_ge(w.loaded, 16 * w.count)
            pe.wait_ge(w_in, 32)
            pe.wait_ge(dve_consts, 7)
            transposes(X[0], cxT[0])
            transposes(X[1], cxT[1]).then_inc(pro_psum, 1)
            pe.wait_ge(pro_sb, 2)
            wqT, wkT = xnT
            for m in range(C):
                cols = slice(m * P, (m + 1) * P)
                for c in range(C):
                    t_.matmul(halves(X[0])[:, m, :], wqT[:, c, cols], wkT[:, c, :], start=c == 0, stop=c == C - 1)
                for c in range(C):
                    t_.matmul(X[1][:, m:m + 1], wkT[:, c, cols], bqT[:, c:c + 1], start=c == 0, stop=c == C - 1)
                for c in range(C):
                    t_.matmul(X[1][:, C + m:C + m + 1], wqT[:, c, cols], bkT[:, c:c + 1], start=c == 0, stop=c == C - 1)
            for c in range(C):
                last = t_.matmul(X[1][:, 2 * C:2 * C + 1], bqT[:, c:c + 1].broadcast_to([P, P]), bkT[:, c:c + 1],
                                 start=c == 0, stop=c == C - 1)
            last.then_inc(pro_psum, 1)
            pe.wait_ge(pro_sb, 6)

            def rowT(n, u, i):
                pe.wait_ge(xn_ready[u], 3 * i + n)
                transposes(X[u], xn[u]).then_inc(xnT_psum[u], 1)

            def normT(u, i):
                pe.wait_ge(y_ready[u], i)
                rowT(1, u, i)
                pe.wait_ge(cx_loaded[u], 16 * i + 16)
                transposes(Y[u], cx[u]).then_inc(cxT_psum[u], 1)

            def project_qk(u, i):
                pe.wait_ge(xnT_ready[u], 3 * i + 1)
                pe.wait_ge(cxT_ready[u], i + 1)
                for t, bank in enumerate((X[u], Y[u])):
                    for c in range(C):
                        last = t_.matmul(bank[:, :], xnT[u][:, c, t * P:(t + 1) * P], wqkv[:, c, 0:2 * D],
                                         start=c == 0, stop=c == C - 1)
                last.then_inc(qk_psum[u], 1)

            def project_v(u, i):
                pe.wait_ge(qk_taken[u], i + 1)
                project(Y[u], xnT[u], wqkv[:, :, 2 * D:3 * D]).then_inc(v_psum[u], 1)

            def splitT(t, u, i):
                if t == 0:
                    pe.wait_ge(low_ready[u], i + 1)
                    pe.wait_ge(eo_taken[u], i * NE)
                for src, ring, full, taken in ((q4, SR[0], q4T_psum, q4T_taken), (k4, SR[1], k4T_psum, k4T_taken)):
                    for bank in range(2):
                        pe.wait_ge(taken, 8 * i + 4 * u + (2 * t - 1 + bank if t else 0))
                        for b in range(NB)[blocks(bank)]:
                            last = t_.transpose(ring[:, b * P:(b + 1) * P].bitcast(F32R),
                                                src[:, t, 2 * b:2 * b + 2, :].rearrange("p h n -> p (h n)"),
                                                identr[:, :])
                        last.then_inc(full, 1)

            def raw(f, u, i):
                if f < 2:
                    pe.wait_ge(q4T_taken, 8 * i + 4 * u + 4)
                    pe.wait_ge(k4T_taken, 8 * i + 4 * u + 4)
                else:
                    pe.wait_ge(raw_taken, (2 * i + u) * T * NG + f - 1)
                t, g = f // NG, f % NG
                for h in range(g * HG, (g + 1) * HG):
                    at = slice(h % 2 * SL, h % 2 * SL + SL)
                    last = t_.matmul(heads(SR[f % 2])[:, place(h), :], q4T[u][at, h // 2, t * P:(t + 1) * P],
                                     k4T[u][at, h // 2, :], start=True, stop=True)
                last.then_inc(raw_psum, 1)

            def shiftT(t, u, i):
                pe.wait_ge(nm_ready[u], T * i + t + 1)
                if t == 0:
                    pe.wait_ge(qk_taken[u], i + 1)
                t_.transpose(X[u][:, t * P:(t + 1) * P], nm[u][:, t, :], ident[:, :]).then_inc(nmT_psum[u], 1)

            def attend(g, u, i):
                n = (2 * i + u) * NG + g
                if g == 0:
                    pe.wait_ge(shift_ready[u], 2 * T * i + 2 * T)
                    pe.wait_ge(raw_taken, (2 * i + u + 1) * T * NG)
                if g < NG:
                    for t in range(T):
                        if g:
                            pe.wait_ge(probs_ready, (n - 1) * T + t + 1)
                        for h in range(g * HG, (g + 1) * HG):
                            at = slice(h % 2 * SL, h % 2 * SL + SL)
                            last = t_.matmul(heads(SR[t])[:, place(h), :], k4T[u][at, h // 2, t * P:(t + 1) * P],
                                             q4T[u][at, h // 2, :], start=True, stop=True)
                        last.then_inc(scores_psum, 1)
                if g:
                    b = g - 1
                    pe.wait_ge(probs_ready, n * T)
                    if b == 0:
                        pe.wait_ge(v_ready[u], i + 1)
                    bank = halves((X[u], Y[u])[b // 2])[:, b % 2, :]
                    for t in range(T):
                        for h in range(HG):
                            last = t_.matmul(bank[h * 2 * DH:(h + 1) * 2 * DH, :], v32[u][:, t, b * HG + h, :],
                                             PT[(u * NG + b) % 3][:, t, place(h), :], start=t == 0, stop=t == T - 1)
                    last.then_inc(probs_used, 1)

            def o(u, i):
                pe.wait_ge(oT_ready[u], i + 1)
                for t, bank in enumerate((X[u], Y[u])):
                    for g in range(NG):
                        last = t_.transpose(bank[:, g * P:(g + 1) * P], oT[u][:, g, t * P:(t + 1) * P], ident[:, :])
                last.then_inc(o_psum[u], 1)

            def o2T(u, i):
                pe.wait_ge(o_ready[u], i + 1)
                transposes(X[u], xn[u]).then_inc(o2T_psum[u], 1)

            def project_o(u, i):
                pe.wait_ge(o2T_ready[u], i + 1)
                project(Y[u], xnT[u], wo).then_inc(proj_psum[u], 1)

            def project_g(u, i):
                pe.wait_ge(xnT_ready[u], 3 * i + 2)
                for m in range(C):
                    for c in range(C):
                        last = t_.matmul(halves(Y[u])[:, m, :], wqk[:, c, m * P:(m + 1) * P], xnT[u][:, c, :],
                                         start=c == 0, stop=c == C - 1)
                last.then_inc(g_psum[u], 1)

            def cross_scores(u, i):
                pe.wait_ge(g_ready[u], i + 1)
                for part in range(3):
                    if part == 2:
                        pe.wait_ge(gx_ready[u], i + 1)
                    for t, bank in enumerate((X[u], Y[u])):
                        cols = slice(t * P, (t + 1) * P)
                        lhs, rhs, at = ((gT[u], lambda c: cxT[u][:, c, :], slice(0, S)),
                                        (xnT[u], lambda c: wr[:, c:c + 1], slice(S + 2, S + 3)),
                                        (gx[u], lambda c: ones[:, :], slice(S, S + 1)))[part]
                        for c in range(C):
                            last = t_.matmul(bank[:, at], lhs[:, c, cols], rhs(c), start=c == 0, stop=c == C - 1)
                last.then_inc(s2_psum[u], 1)

            def expT(u, i):
                pe.wait_ge(p2_ready[u], i + 1)
                transposes(X[u], pe2[u]).then_inc(peT_psum[u], 1)

            def mixed(u, i):
                pe.wait_ge(peT_ready[u], i + 1)
                project(Y[u], peT[u], cx[u]).then_inc(mix_psum[u], 1)

            def mixT(u, i):
                pe.wait_ge(mix_ready[u], i + 1)
                transposes(X[u], mix[u]).then_inc(mixT_psum[u], 1)

            def cross(u, i):
                pe.wait_ge(mixT_ready[u], i + 1)
                project(Y[u], peT[u], wvx).then_inc(cross_psum[u], 1)

            def gates(u, i):
                pe.wait_ge(xnT_ready[u], 3 * i + 3)
                for t in range(T):
                    for c in range(C):
                        last = t_.matmul(Y[u][:, t * NE:(t + 1) * NE], xmT[u][:, c, t * P:(t + 1) * P], gw[:, c, :],
                                         start=c == 0, stop=c == C - 1)
                last.then_inc(gates_psum[u], 1)

            def bias(u, i):
                pe.wait_ge(comb_ready[u], i + 1)
                for t in range(T):
                    last = t_.transpose(Y[u][0:NE, P + t * P:P + (t + 1) * P], comb[u][:, t, :], ident[:, :])
                last.then_inc(combT_psum[u], 1)
                pe.wait_ge(combT_ready[u], i + 1)
                for t in range(T):
                    last = t_.matmul(halves(Y[u])[:, t, :], combT[u][:, t * P:(t + 1) * P], b2[:, :], start=True, stop=True)
                last.then_inc(bias_psum[u], 1)

            def expert(e, u, i):
                if e < NE:
                    if e >= 2:
                        pe.wait_ge(hid_ready[u], i * NE + e - 1)
                    for m in range(C):
                        for c in range(C):
                            last = t_.matmul(half(0, e)[:, m, :], w1[:, e, c, m * P:(m + 1) * P], xmT[u][:, c, :],
                                             start=c == 0, stop=c == C - 1)
                    last.then_inc(hid_psum[u], 1)
                if e:
                    b = e - 1
                    pe.wait_ge(hid_ready[u], i * NE + b + 1)
                    if b >= 2:
                        pe.wait_ge(eo_taken[u], i * NE + b - 1)
                    for t in range(T):
                        for m in range(C):
                            last = t_.matmul(half(1, b)[:, t, :], hid[b % 2][:, m, t * P:(t + 1) * P], w2[:, b, m, :],
                                             start=m == 0, stop=m == C - 1)
                    last.then_inc(eo_psum[u], 1)

            skewed(pe, PAIRS, ((0,), (1,)), ORDER, {
                "f normT": normT, "f qk": project_qk, "f v": project_v, "f splitT0": partial(splitT, 0),
                "f splitT1": partial(splitT, 1),
                "f shift0": partial(shiftT, 0), "f shift1": partial(shiftT, 1),
                "b o": o, "b o2T": o2T, "b proj": project_o, "b norm2T": partial(rowT, 2), "b g": project_g,
                "b scores": cross_scores, "b expT": expT, "b mix": mixed, "b mixT": mixT, "b cross": cross,
                "b norm3T": partial(rowT, 3), "b gates": gates, "b bias": bias,
                **{f"f raw{f}": partial(raw, f) for f in range(T * NG)},
                **{f"f attend{g}": partial(attend, g) for g in range(NG + 1)},
                **{f"m expert{e}": partial(expert, e) for e in range(NE + 1)},
            })


_INS = [
    "x", "ctx_1024",
    *[f"L0_attn_{n}" for n in ("Wk", "bk", "gk", "betak", "Wq", "bq", "gq", "betaq", "Wv", "bv", "gv", "betav")],
    *[f"L0_ffn_{n}" for n in ("W_sw", "b_sw", "W1", "b1", "W2", "b2")],
    *[f"L1_attn_{n}" for n in ("w_qkv", "w_proj", "q_gamma", "q_beta", "k_gamma", "k_beta")],
    *[f"L1_xattn_{n}" for n in ("Wq", "bq", "Wk", "bk", "Wv", "bv")],
    *[f"L1_ffn_{n}" for n in ("gate_w", "gate_b", "w1", "b1", "w2", "b2")],
]


def decoder(nc, a, out):
    B, S, D = a["x"].shape
    x2_d = nc.dram_tensor("x2_scratch", (B * S, D), F32).ap()
    x3_d = nc.dram_tensor("x3_scratch", (B * S, D), F32).ap()
    table_d = nc.dram_tensor("slot_table", (B * S, 1), I32).ap()
    with nc.cleanup_on_exit():
        phase_a(nc, a, x2_d, x3_d, table_d)
    nc.all_engine_barrier()
    with ExitStack() as ctx:
        layer1_weights = Layer1Weights(nc, ctx, a)
        with nc.cleanup_on_exit():
            phase_b(nc, a, x2_d, x3_d, table_d, layer1_weights)
        nc.all_engine_barrier()
        phase_c(nc, a, x3_d, out, layer1_weights)


def kernel(**inputs):
    import numpy as _np
    import concourse.bacc as _bacc
    from concourse import mybir as _mybir
    from concourse.bass_utils import run_bass_kernel_spmd as _run

    nc = _bacc.Bacc("TRN2", target_bir_lowering=False, num_devices=1)
    arrays, args = {}, {}
    for name in _INS:
        arrays[f"in_{name}_dram"] = _np.ascontiguousarray(inputs[name])
        args[name] = nc.dram_tensor(f"in_{name}_dram", arrays[f"in_{name}_dram"].shape, _mybir.dt.float32,
                                    kind="ExternalInput").ap()
    out = nc.dram_tensor("out_0_dram", inputs["x"].shape, _mybir.dt.float32, kind="ExternalOutput").ap()
    decoder(nc, args, out)
    r = _run(nc, [arrays], core_ids=[0])
    return r.results[0]["out_0_dram"]
```
